# Optimizing a Trainium2 kernel written in Bass

```python
import numpy as np
import jax
import jax.numpy as jnp

def _softmax(x, axis=-1):
    return jax.nn.softmax(x, axis=axis)

def _gelu(x):
    return jax.nn.gelu(x, approximate=True)

def _silu(x):
    return jax.nn.silu(x)

def _sigmoid(x):
    return jax.nn.sigmoid(x)

def _layernorm(x, axis=-1, eps=1e-05):
    m = jnp.mean(x, axis=axis, keepdims=True)
    v = jnp.var(x, axis=axis, keepdims=True)
    return (x - m) / jnp.sqrt(v + eps)

def _scatter_add(tgt, idx, src, axis=0):
    return tgt.at[idx].add(src)

def _segment_sum(src, seg, n):
    return jax.ops.segment_sum(src, seg, n)
kernel_name = 'mk_gnn_resnorm_d2_gnn_r64_c8edac'

def setup_inputs(seed: int=0):
    np.random.seed(seed)
    _w = jnp.asarray

    def _rec_inputs():
        import jax
        import jax.numpy as jnp
        _gk = jax.random.key(seed)
        x = -0.0003713 + 1 * jax.random.normal(jax.random.fold_in(_gk, 1), (100000, 128), jnp.float32)
        src = jax.random.randint(jax.random.fold_in(_gk, 2), (25000,), 0, 100000, jnp.int32)
        dst = jax.random.randint(jax.random.fold_in(_gk, 3), (25000,), 0, 100000, jnp.int32)
        _o = jnp.argsort(dst, stable=True)
        src = src[_o]
        dst = dst[_o]
        edge_attr_3 = 0.00011001 + 1.00018 * jax.random.normal(jax.random.fold_in(_gk, 11), (25000, 3), jnp.float32)
        return (x, src, dst, edge_attr_3)
    x, src, dst, edge_attr_3 = _rec_inputs()

    def _L0_gnn_setup():
        import jax, jax.numpy as jnp
        import numpy as np
        N = 100000
        H = 128
        E = 12500
        NEG_SLOPE = 0.2

        def prelu(x, a):
            return jnp.where(x >= 0, x, a * x)

        def segment_softmax(logits, seg, num_segments):
            m = jax.ops.segment_max(logits, seg, num_segments=num_segments)
            m = jnp.where(jnp.isfinite(m), m, 0.0)
            e = jnp.exp(logits - m[seg])
            s = jax.ops.segment_sum(e, seg, num_segments=num_segments)
            return e / (s[seg] + 1e-16)

        def hconv(x, W, att, b, row, col):
            xw = x @ W
            a_i, a_j = (att[:H], att[H:])
            logits = jax.nn.leaky_relu((xw @ a_i)[row] + (xw @ a_j)[col], NEG_SLOPE)
            alpha = segment_softmax(logits, col, N)
            ones = jnp.ones_like(alpha)
            D = jax.ops.segment_sum(ones, row, num_segments=N)
            D_inv = jnp.where(D > 0, 1.0 / D, 0.0)
            B = jax.ops.segment_sum(ones, col, num_segments=N)
            B_inv = jnp.where(B > 0, 1.0 / B, 0.0)
            edge_feat = B_inv[:, None] * jax.ops.segment_sum(alpha[:, None] * xw[row], col, num_segments=N)
            out = D_inv[:, None] * jax.ops.segment_sum(alpha[:, None] * edge_feat[col], row, num_segments=N)
            return out + b
        key = jax.random.key(seed)
        ks = jax.random.split(key, 8)
        x = jax.random.normal(ks[0], (N, H), dtype=jnp.float32)
        hyperedge_index = jax.random.randint(ks[1], (2, E), 0, N, dtype=jnp.int64)
        kaiming = np.sqrt(2.0 / H)
        glorot = np.sqrt(6.0 / (2 * H + 1))
        W1 = jax.random.normal(ks[2], (H, H), dtype=jnp.float32) * kaiming
        W2 = jax.random.normal(ks[3], (H, H), dtype=jnp.float32) * kaiming
        att1 = jax.random.uniform(ks[4], (2 * H,), dtype=jnp.float32, minval=-glorot, maxval=glorot)
        att2 = jax.random.uniform(ks[5], (2 * H,), dtype=jnp.float32, minval=-glorot, maxval=glorot)
        b1 = jnp.zeros((H,), dtype=jnp.float32)
        b2 = jnp.zeros((H,), dtype=jnp.float32)
        prelu_a = jnp.array(0.25, dtype=jnp.float32)
        return {'x': x, 'hyperedge_index': hyperedge_index, 'W1': W1, 'att1': att1, 'b1': b1, 'W2': W2, 'att2': att2, 'b2': b2, 'prelu_a': prelu_a}
    _L0_gnn_all = _L0_gnn_setup()
    _L0_gnn_in = {k: v for k, v in _L0_gnn_all.items() if k in ('W1', 'att1', 'b1', 'W2', 'att2', 'b2', 'prelu_a')}
    del _L0_gnn_all

    def _L1_gnn_setup():
        import jax, jax.numpy as jnp
        import numpy as np
        T, D, E, DE = (50000, 128, 25000, 3)
        EPS = 1e-05
        key = jax.random.key(seed)
        ks = jax.random.split(key, 8)
        H = jax.random.normal(ks[0], (T, D), dtype=jnp.float32)
        edge_index = jax.random.randint(ks[1], (2, E), 0, T, dtype=jnp.int64)
        edge_attr = jax.random.normal(ks[2], (E, DE), dtype=jnp.float32)
        s1 = 1.0 / np.sqrt(D + DE)
        s2 = 1.0 / np.sqrt(D)
        W1 = jax.random.uniform(ks[3], (D + DE, D), minval=-s1, maxval=s1, dtype=jnp.float32)
        b1 = jax.random.uniform(ks[4], (D,), minval=-s1, maxval=s1, dtype=jnp.float32)
        W2 = jax.random.uniform(ks[5], (D, D), minval=-s2, maxval=s2, dtype=jnp.float32)
        b2 = jax.random.uniform(ks[6], (D,), minval=-s2, maxval=s2, dtype=jnp.float32)
        gamma = jnp.ones((D,), dtype=jnp.float32)
        beta = jnp.zeros((D,), dtype=jnp.float32)
        return {'H': H, 'edge_index': edge_index, 'edge_attr': edge_attr, 'W1': W1, 'b1': b1, 'W2': W2, 'b2': b2, 'gamma': gamma, 'beta': beta}
    _L1_gnn_all = _L1_gnn_setup()
    _L1_gnn_in = {k: v for k, v in _L1_gnn_all.items() if k in ('W1', 'b1', 'W2', 'b2', 'gamma', 'beta')}
    del _L1_gnn_all
    return {'x': x, 'src': src, 'dst': dst, 'edge_attr_3': edge_attr_3, 'L0_gnn_W1': _L0_gnn_in['W1'], 'L0_gnn_att1': _L0_gnn_in['att1'], 'L0_gnn_b1': _L0_gnn_in['b1'], 'L0_gnn_W2': _L0_gnn_in['W2'], 'L0_gnn_att2': _L0_gnn_in['att2'], 'L0_gnn_b2': _L0_gnn_in['b2'], 'L0_gnn_prelu_a': _L0_gnn_in['prelu_a'], 'L1_gnn_W1': _L1_gnn_in['W1'], 'L1_gnn_b1': _L1_gnn_in['b1'], 'L1_gnn_W2': _L1_gnn_in['W2'], 'L1_gnn_b2': _L1_gnn_in['b2'], 'L1_gnn_gamma': _L1_gnn_in['gamma'], 'L1_gnn_beta': _L1_gnn_in['beta']}

def reference(x, src, dst, edge_attr_3, L0_gnn_W1, L0_gnn_att1, L0_gnn_b1, L0_gnn_W2, L0_gnn_att2, L0_gnn_b2, L0_gnn_prelu_a, L1_gnn_W1, L1_gnn_b1, L1_gnn_W2, L1_gnn_b2, L1_gnn_gamma, L1_gnn_beta):
    import jax
    import jax.numpy as jnp

    def _L0_gnn_ref(x, hyperedge_index, W1, att1, b1, W2, att2, b2, prelu_a):
        import jax, jax.numpy as jnp
        import numpy as np
        N = 100000
        H = 128
        E = 12500
        NEG_SLOPE = 0.2

        def prelu(x, a):
            return jnp.where(x >= 0, x, a * x)

        def segment_softmax(logits, seg, num_segments):
            m = jax.ops.segment_max(logits, seg, num_segments=num_segments)
            m = jnp.where(jnp.isfinite(m), m, 0.0)
            e = jnp.exp(logits - m[seg])
            s = jax.ops.segment_sum(e, seg, num_segments=num_segments)
            return e / (s[seg] + 1e-16)

        def hconv(x, W, att, b, row, col):
            xw = x @ W
            a_i, a_j = (att[:H], att[H:])
            logits = jax.nn.leaky_relu((xw @ a_i)[row] + (xw @ a_j)[col], NEG_SLOPE)
            alpha = segment_softmax(logits, col, N)
            ones = jnp.ones_like(alpha)
            D = jax.ops.segment_sum(ones, row, num_segments=N)
            D_inv = jnp.where(D > 0, 1.0 / D, 0.0)
            B = jax.ops.segment_sum(ones, col, num_segments=N)
            B_inv = jnp.where(B > 0, 1.0 / B, 0.0)
            edge_feat = B_inv[:, None] * jax.ops.segment_sum(alpha[:, None] * xw[row], col, num_segments=N)
            out = D_inv[:, None] * jax.ops.segment_sum(alpha[:, None] * edge_feat[col], row, num_segments=N)
            return out + b
        row, col = (hyperedge_index[0], hyperedge_index[1])
        out1 = prelu(hconv(x, W1, att1, b1, row, col), prelu_a)
        out1 = hconv(out1, W2, att2, b2, row, col) + x
        return prelu(out1, prelu_a)

    def _L1_gnn_ref(H, edge_index, edge_attr, W1, b1, W2, b2, gamma, beta):
        import jax, jax.numpy as jnp
        import numpy as np
        T, D, E, DE = (50000, 128, 25000, 3)
        EPS = 1e-05
        src, dst = (edge_index[0], edge_index[1])
        Hj = H[src]
        feat = jnp.concatenate([Hj, edge_attr], axis=-1)
        h = jax.nn.gelu(feat @ W1 + b1, approximate=False)
        m = h @ W2 + b2
        agg = jax.ops.segment_sum(m, dst, num_segments=H.shape[0])
        x = H + agg
        mu = jnp.mean(x, axis=-1, keepdims=True)
        var = jnp.mean((x - mu) ** 2, axis=-1, keepdims=True)
        return (x - mu) * jax.lax.rsqrt(var + EPS) * gamma + beta
    edge_index = jnp.stack([src, dst])
    x = _layernorm(x + _L0_gnn_ref(x, edge_index, L0_gnn_W1, L0_gnn_att1, L0_gnn_b1, L0_gnn_W2, L0_gnn_att2, L0_gnn_b2, L0_gnn_prelu_a), axis=-1)
    x = _layernorm(x + _L1_gnn_ref(x, edge_index, edge_attr_3, L1_gnn_W1, L1_gnn_b1, L1_gnn_W2, L1_gnn_b2, L1_gnn_gamma, L1_gnn_beta), axis=-1)
    return x

_drawn_inputs = setup_inputs


def setup_inputs(seed=0):
    import zlib

    import numpy as np

    out = dict(_drawn_inputs(seed))
    spreads = {'L0_gnn_b1': (0.0, 0.466),
     'L0_gnn_b2': (0.0, 0.1),
     'L1_gnn_gamma': (1.0, 0.2),
     'L1_gnn_beta': (0.0, 0.1)}
    factors = {'edge_attr_3': 7.478,
     'L0_gnn_att1': 8.0,
     'L0_gnn_att2': 8.0,
     'L1_gnn_b1': 8.0,
     'L1_gnn_b2': 3.751}
    for name, (base, spread) in spreads.items():
        noise = np.random.default_rng([zlib.crc32(name.encode()), seed]).standard_normal(out[name].shape)
        drawn = base * np.exp(spread * noise) if base else spread * noise
        out[name] = jnp.asarray(drawn.astype(out[name].dtype))
    for name, factor in factors.items():
        out[name] = (out[name] * factor).astype(out[name].dtype)
    return out
```

```python
import concourse.bass as bass
import concourse.mybir as mybir
from contextlib import ExitStack

F32 = mybir.dt.float32
F16 = mybir.dt.float16
I32 = mybir.dt.int32
ALU = mybir.AluOpType
ACT = mybir.ActivationFunctionType
AX = mybir.AxisListType

P = 128
N = 100000
D = 128
E = 25000
T = 196
EP = P * T
LO = 128
HI = 782
HH = HI // 2
PAD_KEY = HI * LO - 1
ABSENT = EP
ROWS = EP + P
W = 132
EPS = 1e-5
LAST = P - 1
LEFT = E - LAST * T
HUGE = 1.0e38
G = 7
C = T // G
DP = 125
DG = 10
DC = N // (DP * DG)
BARE_CHUNKS = {"b": 18, "n0": 16, "c1": 34, "n1": 12}


class Tally:

    def __init__(self, n=0):
        self.n, self.base, self.start = n, 0, 0

    def next(self, by=1):
        self.n += by
        return self.base + self.n

    def loop(self, turn, each):
        self.start = self.base + self.n
        self.base, self.n = turn * each + self.start, 0

    def end(self, turns, each):
        assert self.n == each, (self.n, each)
        self.base, self.n = self.start + turns * each, 0


class Finished(Tally):

    def __init__(self, eng, sem, n=0):
        Tally.__init__(self, n)
        self.eng, self.sem = eng, sem

    def after(self, ins):
        ins.then_inc(self.sem, 1)
        self.eng.wait_ge(self.sem, self.next())


def over_chunks(eng, body, tallies=()):
    turns = C // 2 - 1
    with eng.Fori(0, turns, 1) as i:
        for tally, each in tallies:
            tally.loop(i, 2 * each)
        body(i * 2, 0, False)
        body(i * 2 + 1, 1, False)
    for tally, each in tallies:
        tally.end(turns, 2 * each)
    body(C - 2, 0, False)
    body(C - 1, 1, True)


def semaphore(nc, ctx, name):
    handle = nc.alloc_semaphore(name)
    ctx.callback(nc.clear_and_free_semaphores, [handle])
    return handle


def phase(nc):
    ctx = ExitStack()
    ctx.callback(nc.all_engine_barrier, sem_only=True)
    return ctx


def row(ap):
    return ap.rearrange("p a n -> p (a n)")


def program(nc, x, src, dst, edge_attr, w1, att1, b1, w2, att2, b2, prelu_a,
            m1, mb1, m2, mb2, gamma, beta, out):
    ctx = ExitStack()
    with ctx:
        def sb(name, shape, dt=F32):
            return ctx.enter_context(nc.sbuf_tensor(name, shape, dt))

        def dram(name, shape, dt=F32):
            return nc.dram_tensor(name, shape, dt, kind="Internal").ap()

        big = sb("big", [P, T + 1, W])
        psum = ctx.enter_context(nc.psum_tensor("psum", [P, 8, 512], F32))
        ps = [psum[:, n, :] for n in range(8)]
        pairs = [psum[:, n:n + 2, 0:HH] for n in range(7)]
        ident = sb("ident", [P, P])
        ident16 = sb("ident16", [P, P], F16)
        ones16 = sb("ones16", [P, P], F16)
        ones = sb("ones", [P, P])
        before = sb("before", [P, P])
        later = sb("later", [P, P])
        iota_p = sb("iota_p", [P, 1])
        place = sb("place", [P, T])
        eps = sb("eps", [P, 1])
        eps_sq = sb("eps_sq", [P, 1])
        alpha = sb("alpha", [P, 1])
        drop = sb("drop", [P, 1])
        w1s, w2s, m1s, m2s = (sb(n, [P, D]) for n in ("w1s", "w2s", "m1s", "m2s"))
        edge_w = sb("edge_w", [4 * G, G * D])
        rows_ = {n: sb("row_" + n, [P, D]) for n in ("b1", "b2", "mb2", "gamma", "beta", "wi1", "wj1", "wi2", "wj2")}
        aj_absent = sb("aj_absent", [P, 1])
        src_key, dst_key = sb("src_key", [P, T]), sb("dst_key", [P, T])
        src_gather, dst_gather = sb("src_gather", [P, T], I32), sb("dst_gather", [P, T], I32)
        src_start, dst_start = sb("src_start", [P, T]), sb("dst_start", [P, T])
        src_start_i, dst_start_i = sb("src_start_i", [P, T], I32), sb("dst_start_i", [P, T], I32)
        src_place, src_place_i = sb("src_place", [P, T]), sb("src_place_i", [P, T], I32)
        orders = {}
        for o in ("d", "s"):
            orders[o] = {n: sb(f"{o}_{n}", [P, T]) for n in
                         ("prev", "new", "same", "next", "runs", "tail", "fix", "start")}
            orders[o].update({n: sb(f"{o}_{n}", [P, P]) for n in ("from_before", "from_later", "sel_before", "sel_later")})
            orders[o].update({n: sb(f"{o}_{n}", [P, 1]) for n in ("has_new",)})
            orders[o]["extra"] = sb(f"{o}_extra", [P, W])
        s_key = sb("s_key", [P, T])
        s_gather = sb("s_gather", [P, T], I32)
        s_scatter = sb("s_scatter", [P, T], I32)
        s_dstart_i = sb("s_dstart_i", [P, T], I32)
        d_scatter = sb("d_scatter", [P, T], I32)
        ai, aj, top, ex, coef = (sb(n, [P, T]) for n in ("ai", "aj", "top", "ex", "coef"))
        tmp = [sb(f"tmp{n}", [P, T]) for n in range(4)]
        ai2_s = sb("ai2_s", [P, T])
        absent = sb("absent", [P, T])

        x_dst = dram("x_dst", [EP, D])
        record = dram("record", [EP + 1, 4])
        sums = [dram(f"sums{n}", [EP, W]) for n in range(2)]
        hidden = dram("hidden", [ROWS, W])
        hidden_aj = dram("hidden_aj", [ROWS, 1])
        mixed = dram("mixed", [ROWS, D])
        mixed_m = dram("mixed_m", [ROWS, D])

        B = dict(locals())
        setup(nc, B)
        counting(nc, B)
        order_flags(nc, B, "d")
        conv_edges(nc, B, 0)
        by_source(nc, B)
        order_flags(nc, B, "s")
        conv_nodes(nc, B, 0)
        conv_edges(nc, B, 1)
        conv_nodes(nc, B, 1)
        edge_network(nc, B)


def shifted_loads(eng, dest, source, sem, offset=0):
    flat = source
    eng.dma_start(dest[0:1, 1:T], flat[0:T - 1].rearrange("(p t) -> p t", p=1)).then_inc(sem, 16)
    eng.dma_start(dest[1:LAST, :], flat[T - 1:LAST * T - 1].rearrange("(p t) -> p t", t=T)).then_inc(sem, 16)
    eng.dma_start(dest[LAST:P, 0:LEFT + 1], flat[LAST * T - 1:E].rearrange("(p t) -> p t", p=1)).then_inc(sem, 16)


def setup(nc, B):
    with phase(nc) as ctx:
        def sem(name):
            return semaphore(nc, ctx, name)
        key_i = [ctx.enter_context(nc.sbuf_tensor(f"key_i{n}", [P, T], I32)) for n in range(2)]
        prev_i = ctx.enter_context(nc.sbuf_tensor("prev_i", [P, T], I32))
        wt = [ctx.enter_context(nc.sbuf_tensor(f"wt{n}", [P, P], F32)) for n in range(2)]
        att_bc = [ctx.enter_context(nc.sbuf_tensor(f"att_bc{n}", [P, P], F32)) for n in range(4)]
        att_col = ctx.enter_context(nc.sbuf_tensor("att_col", [P, 4], F32))
        hid_row = ctx.enter_context(nc.sbuf_tensor("hid_row", [P, W], F32))
        junk = ctx.enter_context(nc.sbuf_tensor("junk", [P, D], F32))
        more_junk = ctx.enter_context(nc.sbuf_tensor("junk2", [P, D], F32))
        zero_row = ctx.enter_context(nc.sbuf_tensor("zero_row", [P, D], F32))
        place_i = ctx.enter_context(nc.sbuf_tensor("place_i", [P, T], I32))
        filled, loaded, made, own = sem("filled"), sem("loaded"), sem("made"), sem("own")
        weights_up, turned, copied, rows_up, absent_row, stored = (
            sem(n) for n in ("weights_up", "turned", "copied", "rows_up", "absent_row", "stored"))
        pool_own = sem("pool_own")
        block = ctx.enter_context(nc.Block())
        rows_, ps = B["rows_"], B["ps"]

        @block.sync
        def _(sp):
            n = 0
            for dest, source in ((B["w1s"], B["w1"]), (B["w2s"], B["w2"]), (B["m1s"], B["m1"][0:D, :]), (B["m2s"], B["m2"])):
                sp.dma_start(dest[:, :], source).then_inc(weights_up, 16)
            for n, att in enumerate((B["att1"], B["att2"])):
                sp.dma_start(att_col[:, 2 * n:2 * n + 2], att.rearrange("(a p) -> p a", p=P),
                             allow_slow_non_contiguous=True).then_inc(weights_up, 16)
            for name in ("b1", "b2", "mb2", "gamma", "beta"):
                sp.dma_start(rows_[name][:, :], B[name].rearrange("(a n) -> a n", a=1).to_broadcast([P, D]))\
                  .then_inc(weights_up, 16)
            sp.dma_start(B["alpha"][:, :], B["prelu_a"].rearrange("(a n) -> a n", a=1).to_broadcast([P, 1]))\
              .then_inc(weights_up, 16)
            sp.wait_ge(filled, 3)
            for k, source in ((key_i[0], B["src"]), (key_i[1], B["dst"])):
                sp.dma_start(k[0:LAST, :], source[0:LAST * T].rearrange("(p t) -> p t", t=T)).then_inc(loaded, 16)
                sp.dma_start(k[LAST:P, 0:LEFT], source[LAST * T:E].rearrange("(p t) -> p t", p=1)).then_inc(loaded, 16)
            shifted_loads(sp, prev_i, B["dst"], loaded)
            sp.wait_ge(absent_row, 2)
            sp.dma_start(B["hidden"][EP:ROWS, :], hid_row[:, :]).then_inc(stored, 16)
            sp.dma_start(B["hidden_aj"][EP:ROWS, :], B["aj_absent"][:, :]).then_inc(stored, 16)
            sp.dma_start(B["mixed"][EP:ROWS, :], zero_row[:, :]).then_inc(stored, 16)
            sp.dma_start(B["mixed_m"][EP:ROWS, :], zero_row[:, :]).then_inc(stored, 16)
            sp.wait_ge(stored, 64)

        @block.gpsimd
        def _(gp):
            gp.memset(B["ident"][:, :], 0.0).then_inc(pool_own, 1)
            gp.memset(B["before"][:, :], 1.0).then_inc(pool_own, 1)
            gp.memset(B["later"][:, :], 1.0).then_inc(pool_own, 1)
            gp.wait_ge(pool_own, 3)
            gp.affine_select(out=B["ident"][:, :], in_=B["ident"][:, :], compare_op=ALU.not_equal, fill=1.0,
                             base=0, pattern=[[-1, P]], channel_multiplier=1).then_inc(made, 1)
            gp.affine_select(out=B["before"][:, :], in_=B["before"][:, :], compare_op=ALU.is_gt, fill=0.0,
                             base=0, pattern=[[1, P]], channel_multiplier=-1).then_inc(made, 1)
            gp.affine_select(out=B["later"][:, :], in_=B["later"][:, :], compare_op=ALU.is_gt, fill=0.0,
                             base=0, pattern=[[-1, P]], channel_multiplier=1).then_inc(made, 1)
            gp.iota(place_i[:, :], pattern=[[1, T]], base=0, channel_multiplier=T).then_inc(made, 1)

        @block.vector
        def _(dve):
            fin = Finished(dve, own)
            nc.vector.memset(key_i[0][:, :], PAD_KEY).then_inc(filled, 1)
            nc.vector.memset(key_i[1][:, :], PAD_KEY).then_inc(filled, 1)
            nc.vector.memset(prev_i[:, :], PAD_KEY).then_inc(filled, 1)
            nc.vector.memset(B["ones16"][:, :], 1.0)
            nc.vector.memset(B["ones"][:, :], 1.0)
            nc.vector.memset(B["eps"][:, :], EPS)
            nc.vector.memset(B["eps_sq"][:, :], EPS * EPS)
            nc.vector.memset(hid_row[:, :], 0.0)
            nc.vector.memset(zero_row[:, :], 0.0)
            fin.after(nc.vector.memset(B["big"][:, :, :], 0.0))
            dve.wait_ge(made, 4)
            nc.vector.tensor_copy(B["ident16"][:, :], B["ident"][:, :])
            nc.vector.tensor_copy(B["place"][:, :], place_i[:, :])
            dve.wait_ge(loaded, 7 * 16)
            nc.vector.tensor_copy(B["src_key"][:, :], key_i[0][:, :])
            nc.vector.tensor_copy(B["dst_key"][:, :], key_i[1][:, :])
            fin.after(nc.vector.tensor_copy(B["orders"]["d"]["prev"][:, :], prev_i[:, :]))
            fin.after(nc.vector.memset(B["orders"]["d"]["prev"][0:1, 0:1], -1.0))
            nc.vector.tensor_scalar(B["src_gather"][:, :], B["src_key"][:, :], float(N - 1), None, ALU.min)
            nc.vector.tensor_scalar(B["dst_gather"][:, :], B["dst_key"][:, :], float(N - 1), None, ALU.min)
            dve.wait_ge(weights_up, 12 * 16)
            for n in range(4):
                fin.after(nc.vector.tensor_scalar(att_bc[n][:, :], B["ones"][:, :], att_col[:, n:n + 1], None, ALU.mult))
            dve.wait_ge(turned, 2)
            nc.vector.tensor_copy(wt[0][:, :], ps[0][:, 0:P]).then_inc(copied, 1)
            nc.vector.tensor_copy(wt[1][:, :], ps[1][:, 0:P]).then_inc(copied, 1)
            dve.wait_ge(rows_up, 1)
            for n, name in enumerate(("wi1", "wj1", "wi2", "wj2")):
                nc.vector.tensor_copy(rows_[name][:, :], ps[2][:, n * P:n * P + P])
            fin.after(nc.vector.tensor_scalar(B["drop"][:, :], B["alpha"][:, :], -1.0, 1.0, ALU.mult, ALU.add))
            fin.after(nc.vector.tensor_scalar(junk[:, :], rows_["b1"][:, :], -1.0, 0.0, ALU.mult, ALU.max))
            fin.after(nc.vector.scalar_tensor_tensor(out=hid_row[:, 0:D], in0=junk[:, :], scalar=B["drop"][:, 0:1],
                                                     in1=rows_["b1"][:, :], op0=ALU.mult, op1=ALU.add))
            fin.after(nc.vector.scalar_tensor_tensor(
                out=junk[:, :], in0=hid_row[:, 0:D], scalar=1.0, in1=rows_["wj2"][:, :],
                op0=ALU.mult, op1=ALU.mult, accum_out=B["aj_absent"][:, :]))
            nc.vector.scalar_tensor_tensor(
                out=more_junk[:, :], in0=hid_row[:, 0:D], scalar=1.0, in1=rows_["wi2"][:, :],
                op0=ALU.mult, op1=ALU.mult, accum_out=hid_row[:, D:D + 1]).then_inc(absent_row, 2)

        @block.tensor
        def _(pe):
            pe.wait_ge(weights_up, 12 * 16)
            pe.wait_ge(made, 1)
            for n, w in enumerate((B["w1s"], B["w2s"])):
                nc.tensor.transpose(ps[n][:, 0:P], w[:, :], B["ident"][:, :]).then_inc(turned, 1)
            pe.wait_ge(copied, 2)
            pe.wait_ge(own, 7)
            for n in range(4):
                last = nc.tensor.matmul(ps[2][:, n * P:n * P + P], att_bc[n][:, :], wt[n // 2][:, :],
                                        start=True, stop=True)
            last.then_inc(rows_up, 1)


def halves(bank0, bank1):
    return (bank0[:, 0:HH], bank1[:, 0:HH])


def counting(nc, B):
    with phase(nc) as ctx:
        def sb(name, shape, dt=F32):
            return ctx.enter_context(nc.sbuf_tensor(name, shape, dt))

        def sem(name):
            return semaphore(nc, ctx, name)
        ps = B["ps"]
        digits_i = sb("digits_i", [P, T], I32)
        lo = {k: sb(f"lo_{k}", [P, T + 4]) for k in "sd"}
        hi = {k: sb(f"hi_{k}", [P, T + 4]) for k in "sd"}
        iota_i = sb("iota_i", [P, HI], I32)
        iota16 = sb("iota16", [P, HI], F16)
        oh_lo = [sb(f"oh_lo{n}", [P, LO], F16) for n in range(2)]
        oh_hi = [sb(f"oh_hi{n}", [P, HI], F16) for n in range(2)]
        count = sb("count", [P, HI])
        upto = sb("upto", [P, HI])
        start = sb("start", [P, HI])
        ones_hi = sb("ones_hi", [P, HI])
        start_i = sb("start_i", [P, HI], I32)
        start_lo_i = sb("start_lo_i", [P, HI], I32)
        start_hi16, start_lo16 = sb("start_hi16", [P, HI], F16), sb("start_lo16", [P, HI], F16)
        offset = sb("offset", [P, 1])
        iota_pi = sb("iota_pi", [P, 1], I32)
        diag = [sb(f"diag{n}", [P, P], F16) for n in range(2)]
        lo_hot16 = [sb(f"lo_hot16_{n}", [P, P], F16) for n in range(2)]
        lo_hot = [sb(f"lo_hot{n}", [P, P]) for n in range(2)]
        twins = [sb(f"twins{n}", [P, P], F16) for n in range(2)]
        so_far = [sb(f"so_far{n}", [P, HI]) for n in range(2)]
        earlier = sb("earlier", [P, T])
        junk = [sb(f"junk_c{n}", [P, HI], F16) for n in range(2)]
        zero16 = sb("zero16", [P, HH], F16)
        ring = [sb(f"x_ring{n}", [P, D]) for n in range(4)]
        place_i = sb("place_si", [P, T], I32)

        with phase(nc) as c2:
            made, own, ready, used, summed, ranked = (semaphore(nc, c2, n) for n in
                                                      ("c_made", "c_own", "c_ready", "c_used", "c_summed", "c_ranked"))
            block = c2.enter_context(nc.Block())

            @block.gpsimd
            def _(gp):
                gp.iota(iota_i[:, :], pattern=[[1, HI]], base=0, channel_multiplier=0).then_inc(made, 1)
                gp.iota(iota_pi[:, :], pattern=[[1, 1]], base=0, channel_multiplier=1).then_inc(made, 1)

            @block.vector
            def _(dve):
                fin = Finished(dve, own)
                dve.wait_ge(made, 2)
                nc.vector.tensor_copy(iota16[:, :], iota_i[:, :])
                nc.vector.tensor_copy(B["iota_p"][:, :], iota_pi[:, :])
                nc.vector.memset(ones_hi[:, :], 1.0)
                nc.vector.memset(zero16[:, :], 0.0)
                for k, key in (("s", B["src_key"]), ("d", B["dst_key"])):
                    nc.vector.memset(lo[k][:, T:T + 4], 0.0)
                    nc.vector.memset(hi[k][:, T:T + 4], 0.0)
                    fin.after(nc.vector.tensor_copy(digits_i[:, :], key[:, :]))
                    fin.after(nc.vector.tensor_single_scalar(place_i[:, :], digits_i[:, :], LO - 1, op=ALU.bitwise_and))
                    fin.after(nc.vector.tensor_copy(lo[k][:, 0:T], place_i[:, :]))
                    fin.after(nc.vector.tensor_single_scalar(place_i[:, :], digits_i[:, :], 7, op=ALU.logical_shift_right))
                    fin.after(nc.vector.tensor_copy(hi[k][:, 0:T], place_i[:, :]))

                def hot(t, slot):
                    dve.wait_ge(used, t + 1)
                    nc.vector.tensor_scalar(oh_lo[slot][:, :], iota16[:, 0:LO], lo["s"][:, bass.ds(t, 1)], None, ALU.is_equal)
                    nc.vector.tensor_scalar(oh_hi[slot][:, :], iota16[:, :], hi["s"][:, bass.ds(t, 1)], None, ALU.is_equal)\
                      .then_inc(ready, 1)
                with dve.Fori(0, T // 4, 1) as i:
                    for j in range(4):
                        hot(i * 4 + j, j % 2)
                dve.wait_ge(summed, 1)
                for h, half in enumerate(halves(ps[0], ps[1])):
                    fin.after(nc.vector.tensor_copy(count[:, h * HH:h * HH + HH], half))
                fin.after(nc.vector.tensor_tensor_scan(upto[:, :], ones_hi[:, :], count[:, :], 0.0, ALU.mult, ALU.add))
                dve.wait_ge(ranked, 1)
                fin.after(nc.vector.tensor_copy(offset[:, :], ps[2][:, 0:1]))
                fin.after(nc.vector.scalar_tensor_tensor(out=start[:, :], in0=upto[:, :], scalar=offset[:, 0:1],
                                                         in1=count[:, :], op0=ALU.add, op1=ALU.subtract))
                fin.after(nc.vector.tensor_scalar(upto[:, :], count[:, :], 0.0, None, ALU.is_gt))
                fin.after(nc.vector.scalar_tensor_tensor(out=start[:, :], in0=start[:, :], scalar=-float(ABSENT),
                                                         in1=upto[:, :], op0=ALU.add, op1=ALU.mult))
                fin.after(nc.vector.tensor_scalar(start[:, :], start[:, :], float(ABSENT), None, ALU.add))
                fin.after(nc.vector.tensor_copy(start_i[:, :], start[:, :]))
                fin.after(nc.vector.tensor_single_scalar(start_lo_i[:, :], start_i[:, :], 255, op=ALU.bitwise_and))
                fin.after(nc.vector.tensor_copy(upto[:, :], start_lo_i[:, :]))
                fin.after(nc.vector.tensor_copy(start_lo16[:, :], upto[:, :]))
                fin.after(nc.vector.tensor_tensor(start_hi16[:, :], start[:, :], upto[:, :], ALU.subtract))

            @block.tensor
            def _(pe):
                pe.sem_inc(used, 2)
                acc = halves(ps[0], ps[1])
                pe.wait_ge(own, 1)
                for h in range(2):
                    nc.tensor.matmul(acc[h], zero16[:, 0:P], zero16[:, :], start=True, stop=False)
                with pe.Fori(0, T // 4, 1) as i:
                    for j in range(4):
                        pe.wait_ge(ready, i * 4 + j + 1)
                        for h in range(2):
                            last = nc.tensor.matmul(acc[h], oh_lo[j % 2][:, :], oh_hi[j % 2][:, h * HH:h * HH + HH],
                                                    start=False, stop=False)
                        last.then_inc(used, 1)
                for h in range(2):
                    last = nc.tensor.matmul(acc[h], zero16[:, 0:P], zero16[:, :], start=False, stop=True)
                last.then_inc(summed, 1)
                pe.wait_ge(own, 13)
                nc.tensor.matmul(ps[2][:, 0:1], B["before"][:, :], upto[:, HI - 1:HI], start=True, stop=True)\
                  .then_inc(ranked, 1)

        with phase(nc) as c2:
            def sem2(name):
                return semaphore(nc, c2, name)
            own, diag_up, lo_up, hot_up, earlier_up, looked, taken, done = (
                sem2(n) for n in ("r_own", "r_diag", "r_lo", "r_hot", "r_snap", "r_looked", "r_taken", "r_done"))
            big_in = [sem2(f"r_big{n}") for n in range(4)]
            ring_in = [sem2(f"r_in{n}") for n in range(4)]
            ring_out = [sem2(f"r_out{n}") for n in range(4)]
            block = c2.enter_context(nc.Block())

            @block.gpsimd
            def _(gp):
                for t in range(T):
                    if t >= 4:
                        gp.wait_ge(big_in[t % 4], 16 * (t // 4))
                    gp.indirect_dma_start(out=B["big"][:, t, 0:D], out_offset=None, in_=B["x"],
                                          in_offset=bass.IndirectOffsetOnAxis(ap=B["src_gather"][:, t:t + 1], axis=0))\
                      .then_inc(big_in[t % 4], 16)
                for t in range(T):
                    if t >= 4:
                        gp.wait_ge(ring_out[t % 4], 16 * (t // 4))
                    gp.indirect_dma_start(out=ring[t % 4][:, :], out_offset=None, in_=B["x"],
                                          in_offset=bass.IndirectOffsetOnAxis(ap=B["dst_gather"][:, t:t + 1], axis=0))\
                      .then_inc(ring_in[t % 4], 16)
                for n in range(4):
                    gp.wait_ge(big_in[n], 16 * (T // 4))

            @block.sync
            def _(sp):
                table = B["x_dst"].rearrange("(p t) d -> p t d", t=T)
                with sp.Fori(0, T // 4, 1) as i:
                    for j in range(4):
                        sp.wait_ge(ring_in[j], i * 16 + 16)
                        sp.dma_start(table[:, bass.ds(i * 4 + j, 1), :], ring[j][:, :].rearrange("p (a d) -> p a d", a=1))\
                          .then_inc(ring_out[j], 16)
                for j in range(4):
                    sp.wait_ge(ring_out[j], 16 * (T // 4))

            @block.scalar
            def _(act):
                def digit(t, slot):
                    act.wait_ge(lo_up, t)
                    act.wait_ge(own, 1)
                    nc.scalar.activation(diag[slot][:, :], B["ident16"][:, :], ACT.Copy,
                                         scale=lo["s"][:, bass.ds(t, 1)]).then_inc(diag_up, 1)

                digit(0, 0)
                with act.Fori(0, T // 4, 1) as i:
                    for j in range(4):
                        t = i * 4 + j
                        digit(t + 1, (j + 1) % 2)
                        act.wait_ge(done, t + 1)
                        for h, half in enumerate(halves(ps[0], ps[1])):
                            last = nc.scalar.activation(so_far[j % 2][:, h * HH:h * HH + HH], half, ACT.Copy)
                        last.then_inc(earlier_up, 1)

            @block.tensor
            def _(pe):
                acc = halves(ps[0], ps[1])
                at_start = halves(ps[2], ps[3])
                at_count = halves(ps[4], ps[5])
                pe.wait_ge(own, 1)
                for h in range(2):
                    last = nc.tensor.matmul(acc[h], zero16[:, 0:P], zero16[:, :], start=True, stop=True)
                last.then_inc(done, 1)

                def low_row(t, slot):
                    pe.wait_ge(diag_up, t + 1)
                    pe.wait_ge(hot_up, t)
                    nc.tensor.matmul(ps[6 + slot][:, 0:P], B["ones16"][:, :], diag[slot][:, :], start=True, stop=True)\
                      .then_inc(lo_up, 1)

                low_row(0, 0)
                with pe.Fori(0, T // 4, 1) as i:
                    for j in range(4):
                        t, s = i * 4 + j, j % 2
                        low_row(t + 1, 1 - s)
                        pe.wait_ge(hot_up, t + 2)
                        pe.wait_ge(taken, t + 1)
                        for h in range(2):
                            nc.tensor.matmul(at_start[h], lo_hot16[s][:, :], start_hi16[:, h * HH:h * HH + HH], start=True, stop=False)
                            nc.tensor.matmul(at_start[h], lo_hot16[s][:, :], start_lo16[:, h * HH:h * HH + HH], start=False, stop=True)
                        pe.wait_ge(earlier_up, t + 1)
                        for h in range(2):
                            nc.tensor.matmul(at_count[h], lo_hot[s][:, :], so_far[s][:, h * HH:h * HH + HH], start=True, stop=False)
                            last = nc.tensor.matmul(at_count[h], twins[s][:, :], oh_hi[s][:, h * HH:h * HH + HH], start=False, stop=True)
                        last.then_inc(looked, 1)
                        for h in range(2):
                            last = nc.tensor.matmul(acc[h], oh_lo[s][:, :], oh_hi[s][:, h * HH:h * HH + HH],
                                                    start=False, stop=True, skip_group_check=True)
                        last.then_inc(done, 1)

            @block.vector
            def _(dve):
                dve.sem_inc(lo_up, 1)
                dve.sem_inc(taken, 1)
                dve.sem_inc(hot_up, 1)
                dve.sem_inc(own, 1)

                def hot(t, slot):
                    dve.wait_ge(lo_up, t + 2)
                    dve.wait_ge(done, t)
                    col = bass.ds(t, 1)
                    nc.vector.tensor_scalar(lo_hot16[slot][:, :], ps[6 + slot][:, 0:P], B["iota_p"][:, 0:1], None, ALU.is_equal)
                    nc.vector.tensor_scalar(lo_hot[slot][:, :], ps[6 + slot][:, 0:P], B["iota_p"][:, 0:1], None, ALU.is_equal)
                    nc.vector.scalar_tensor_tensor(out=twins[slot][:, :], in0=ps[6 + slot][:, 0:P], scalar=lo["s"][:, col],
                                                   in1=B["before"][:, :], op0=ALU.is_equal, op1=ALU.mult)
                    nc.vector.tensor_scalar(oh_lo[slot][:, :], iota16[:, 0:LO], lo["s"][:, col], None, ALU.is_equal)
                    nc.vector.tensor_scalar(oh_hi[slot][:, :], iota16[:, :], hi["s"][:, col], None, ALU.is_equal)\
                      .then_inc(hot_up, 1)

                hot(0, 0)
                with dve.Fori(0, T // 4, 1) as i:
                    for j in range(4):
                        t, s = i * 4 + j, j % 2
                        dve.wait_ge(taken, t + 1)
                        hot(t + 1, 1 - s)
                        dve.wait_ge(looked, t + 1)
                        hot3 = oh_hi[s][:, :].rearrange("p (h k) -> p h k", h=2)
                        dve.wait_ge(hot_up, t + 2)
                        for n, (target, bank) in enumerate(((B["src_start"], 2), (earlier, 4))):
                            pair = B["pairs"][bank]
                            last = nc.vector.scalar_tensor_tensor(
                                out=junk[n][:, :].rearrange("p (h k) -> p h k", h=2), in0=pair, scalar=1.0, in1=hot3,
                                op0=ALU.mult, op1=ALU.mult, accum_out=target[:, bass.ds(t, 1)])
                        last.then_inc(taken, 1)

        with phase(nc) as c2:
            def sem3(name):
                return semaphore(nc, c2, name)
            own, diag_up, lo_up, hot_up, looked, taken = (
                sem3(n) for n in ("q_own", "q_diag", "q_lo", "q_hot", "q_looked", "q_taken"))
            block = c2.enter_context(nc.Block())

            @block.scalar
            def _(act):
                def digit(t, slot):
                    act.wait_ge(lo_up, t)
                    act.wait_ge(own, 1)
                    nc.scalar.activation(diag[slot][:, :], B["ident16"][:, :], ACT.Copy,
                                         scale=lo["d"][:, bass.ds(t, 1)]).then_inc(diag_up, 1)
                digit(0, 0)
                with act.Fori(0, T // 4, 1) as i:
                    for j in range(4):
                        digit(i * 4 + j + 1, (j + 1) % 2)

            @block.tensor
            def _(pe):
                def low_row(t, slot):
                    pe.wait_ge(diag_up, t + 1)
                    pe.wait_ge(hot_up, t)
                    nc.tensor.matmul(ps[6 + slot][:, 0:P], B["ones16"][:, :], diag[slot][:, :], start=True, stop=True)\
                      .then_inc(lo_up, 1)
                low_row(0, 0)
                with pe.Fori(0, T // 4, 1) as i:
                    for j in range(4):
                        t, s = i * 4 + j, j % 2
                        low_row(t + 1, 1 - s)
                        pe.wait_ge(hot_up, t + 2)
                        pe.wait_ge(taken, t)
                        at_start = halves(ps[2 * s], ps[2 * s + 1])
                        for h in range(2):
                            nc.tensor.matmul(at_start[h], lo_hot16[s][:, :], start_hi16[:, h * HH:h * HH + HH], start=True, stop=False)
                            last = nc.tensor.matmul(at_start[h], lo_hot16[s][:, :], start_lo16[:, h * HH:h * HH + HH], start=False, stop=True)
                        last.then_inc(looked, 1)

            @block.vector
            def _(dve):
                dve.sem_inc(lo_up, 1)
                dve.sem_inc(looked, 1)
                dve.sem_inc(hot_up, 1)
                dve.sem_inc(taken, 1)
                dve.sem_inc(own, 1)

                def hot(t, slot, free):
                    dve.wait_ge(lo_up, t + 2)
                    dve.wait_ge(looked, free)
                    nc.vector.tensor_scalar(lo_hot16[slot][:, :], ps[6 + slot][:, 0:P], B["iota_p"][:, 0:1], None, ALU.is_equal)
                    nc.vector.tensor_scalar(oh_hi[slot][:, :], iota16[:, :], hi["d"][:, bass.ds(t, 1)], None, ALU.is_equal)\
                      .then_inc(hot_up, 1)

                hot(0, 0, 1)
                with dve.Fori(0, T // 4, 1) as i:
                    for j in range(4):
                        t, s = i * 4 + j, j % 2
                        dve.wait_ge(taken, t + 1)
                        hot(t + 1, 1 - s, t + 1)
                        dve.wait_ge(looked, t + 2)
                        dve.wait_ge(hot_up, t + 2)
                        nc.vector.scalar_tensor_tensor(
                            out=junk[s][:, :].rearrange("p (h k) -> p h k", h=2), in0=B["pairs"][2 * s], scalar=1.0,
                            in1=oh_hi[s][:, :].rearrange("p (h k) -> p h k", h=2),
                            op0=ALU.mult, op1=ALU.mult, accum_out=B["dst_start"][:, bass.ds(t, 1)]).then_inc(taken, 1)
                fin = Finished(dve, own, 1)
                dve.wait_ge(taken, T + 1)
                fin.after(nc.vector.tensor_tensor(B["src_place"][:, :], B["src_start"][:, :], earlier[:, :], ALU.add))
                nc.vector.tensor_scalar(B["src_place_i"][:, :], B["src_place"][:, :], 1.0, None, ALU.add)
                nc.vector.tensor_copy(B["src_start_i"][:, :], B["src_start"][:, :])
                nc.vector.tensor_copy(B["dst_start_i"][:, :], B["dst_start"][:, :])


def propagate(dve, nc, B, o, fin, values, out, spare, sent, came, turn):
    q = B["orders"][o]
    fin.after(nc.vector.tensor_tensor(spare[:, :], values, q["new"][:, :], ALU.mult))
    fin.after(nc.vector.tensor_tensor_scan(out[:, :], q["same"][:, :], spare[:, :], 0.0, ALU.mult, ALU.add))
    nc.vector.tensor_tensor(spare[:, 0:1], out[:, T - 1:T], q["has_new"][:, :], ALU.mult).then_inc(sent, 1)
    dve.wait_ge(came, turn)
    fin.after(nc.vector.scalar_tensor_tensor(out=out[:, :], in0=q["runs"][:, :], scalar=B["ps"][turn][:, 0:1],
                                             in1=out[:, :], op0=ALU.mult, op1=ALU.add))


def propagate_pe(pe, nc, B, o, spare, sent, came, turn):
    pe.wait_ge(sent, turn)
    nc.tensor.matmul(B["ps"][turn][:, 0:1], B["orders"][o]["from_before"][:, :], spare[:, 0:1],
                     start=True, stop=True).then_inc(came, 1)


def order_flags(nc, B, o):
    q, ps = B["orders"][o], B["ps"]
    key = B["dst_key"] if o == "d" else B["s_key"]
    with phase(nc) as ctx:
        def sem(name):
            return semaphore(nc, ctx, name)
        own, cols_up, rows_up, sent, came = (sem(o + "_f_" + n) for n in ("own", "cols", "rows", "sent", "came"))
        diag_f = ctx.enter_context(nc.sbuf_tensor(o + "_diag_f", [P, P], F32))
        diag_l = ctx.enter_context(nc.sbuf_tensor(o + "_diag_l", [P, P], F32))
        ones_t = ctx.enter_context(nc.sbuf_tensor(o + "_ones_t", [P, T], F32))
        block = ctx.enter_context(nc.Block())
        first, last = key[:, 0:1], key[:, T - 1:T]

        @block.vector
        def _(dve):
            fin = Finished(dve, own)
            nc.vector.tensor_scalar(diag_f[:, :], B["ident"][:, :], first, None, ALU.mult)
            nc.vector.tensor_scalar(diag_l[:, :], B["ident"][:, :], last, None, ALU.mult).then_inc(cols_up, 1)
            nc.vector.memset(ones_t[:, :], 1.0)
            nc.vector.memset(q["next"][:, :], 0.0)
            nc.vector.tensor_tensor(q["same"][:, :], key[:, :], q["prev"][:, :], ALU.is_equal)
            fin.after(nc.vector.tensor_tensor(q["new"][:, :], key[:, :], q["prev"][:, :], ALU.not_equal))
            nc.vector.tensor_scalar(q["tail"][:, :], key[:, :], last, None, ALU.is_equal)
            nc.vector.tensor_copy(q["next"][:, 0:T - 1], q["same"][:, 1:T])
            fin.after(nc.vector.tensor_tensor_scan(q["runs"][:, :], q["same"][:, :], ones_t[:, :], 1.0, ALU.mult, ALU.mult))
            nc.vector.tensor_tensor(q["fix"][:, :], q["new"][:, :], q["tail"][:, :], ALU.mult)
            fin.after(nc.vector.tensor_scalar(q["has_new"][:, :], q["runs"][:, T - 1:T], -1.0, 1.0, ALU.mult, ALU.add))
            dve.wait_ge(rows_up, 1)
            for name, bank, col, side in (("from_before", 0, last, "before"), ("from_later", 1, first, "later"),
                                          ("sel_before", 1, first, "later"), ("sel_later", 0, last, "before")):
                step = nc.vector.scalar_tensor_tensor(out=q[name][:, :], in0=ps[bank][:, 0:P], scalar=col,
                                                      in1=B[side][:, :], op0=ALU.is_equal, op1=ALU.mult)
            fin.after(step)
            propagate(dve, nc, B, o, fin, B["place"][:, :], q["start"], B["tmp"][0], sent, came, 1)
            target = B["d_scatter"] if o == "d" else B["s_scatter"]
            fin.after(nc.vector.scalar_tensor_tensor(out=B["tmp"][1][:, :], in0=key[:, :], scalar=-float(PAD_KEY),
                                                     in1=q["new"][:, :], op0=ALU.add, op1=ALU.mult))
            fin.after(nc.vector.tensor_scalar(target[:, :], B["tmp"][1][:, :], float(PAD_KEY), None, ALU.add))

        @block.tensor
        def _(pe):
            pe.wait_ge(cols_up, 1)
            nc.tensor.matmul(ps[0][:, 0:P], B["ones"][:, :], diag_f[:, :], start=True, stop=True)
            nc.tensor.matmul(ps[1][:, 0:P], B["ones"][:, :], diag_l[:, :], start=True, stop=True).then_inc(rows_up, 1)
            pe.wait_ge(own, 4)
            propagate_pe(pe, nc, B, o, B["tmp"][0], sent, came, 1)


def edge_logits(dve, nc, B, fin, ai, aj, out, spare):
    fin.after(nc.vector.tensor_tensor(spare, ai, aj, ALU.add))
    fin.after(nc.vector.scalar_tensor_tensor(out=out, in0=spare, scalar=0.2, in1=spare, op0=ALU.mult, op1=ALU.max))


def running_sums(nc, B, o, scale, name):
    q, big = B["orders"][o], B["big"]
    with phase(nc) as ctx:
        def sem(n):
            return semaphore(nc, ctx, name + n)
        scaled, own, extra_up = sem("scaled"), sem("own"), sem("extra")
        block = ctx.enter_context(nc.Block())

        @block.scalar
        def _(act):
            if scale is not None:
                with act.Fori(0, T // 4, 1) as i:
                    first = i * -4 + (T - 4)
                    for j in range(4):
                        at = bass.ds(first + (3 - j), 1)
                        nc.scalar.activation(row(big[:, at, 0:D]), row(big[:, at, 0:D]), ACT.Copy,
                                             scale=scale[:, at]).then_inc(scaled, 1)

        @block.vector
        def _(dve):
            dve.sem_inc(own, 1)
            with dve.Fori(0, T // 4, 1) as i:
                first = i * -4 + (T - 4)
                for j in range(4):
                    t = first + (3 - j)
                    dve.wait_ge(own, i * 4 + j + 1)
                    if scale is not None:
                        dve.wait_ge(scaled, i * 4 + j + 1)
                    nc.vector.scalar_tensor_tensor(
                        out=row(big[:, bass.ds(t, 1), 0:130]), in0=row(big[:, bass.ds(t + 1, 1), 0:130]),
                        scalar=q["next"][:, bass.ds(t, 1)], in1=row(big[:, bass.ds(t, 1), 0:130]),
                        op0=ALU.mult, op1=ALU.add).then_inc(own, 1)
            dve.wait_ge(extra_up, 1)
            nc.vector.tensor_copy(q["extra"][:, :], B["ps"][0][:, 0:W])

        @block.tensor
        def _(pe):
            pe.wait_ge(own, T + 1)
            nc.tensor.matmul(B["ps"][0][:, 0:W], q["from_later"][:, :], big[:, 0, :], start=True, stop=True)\
              .then_inc(extra_up, 1)


def conv_edges(nc, B, layer):
    q, big, ps = B["orders"]["d"], B["big"], B["ps"]
    ai, aj, top, ex, tmp = B["ai"], B["aj"], B["top"], B["ex"], B["tmp"]
    with phase(nc) as ctx:
        def sem(n):
            return semaphore(nc, ctx, f"e{layer}_" + n)
        if layer == 0:
            inn, free = [sem(f"in{n}") for n in range(2)], sem("free")
            ring = [ctx.enter_context(nc.sbuf_tensor(f"xd{n}", [P, G, D], F32)) for n in range(2)]
            junk = [ctx.enter_context(nc.sbuf_tensor(f"e_junk{n}", [P, G, D], F32)) for n in range(2)]
            ai_up = sem("ai_up")
            block = ctx.enter_context(nc.Block())

            @block.sync
            def _(sp):
                table = B["x_dst"].rearrange("(p t) d -> p t d", t=T)

                def load(c, slot, last):
                    sp.wait_ge(free, c + 1)
                    sp.dma_start(ring[slot][:, :, :], table[:, bass.ds(c * G, G), :]).then_inc(inn[slot], 16)
                over_chunks(sp, load)

            @block.vector
            def _(dve):
                dve.sem_inc(free, 2)
                dve.sem_inc(ai_up, 1)

                def dots(c, slot, last):
                    dve.wait_ge(ai_up, c + 1)
                    for g in range(G):
                        at = bass.ds(c * G + g, 1)
                        ins = nc.vector.scalar_tensor_tensor(out=junk[0][:, g, :], in0=row(big[:, at, 0:D]), scalar=1.0,
                                                       in1=B["rows_"]["wi1"][:, :], op0=ALU.mult, op1=ALU.mult,
                                                       accum_out=ai[:, at])
                    ins.then_inc(ai_up, 1)
                    dve.wait_ge(free, c + 2)
                    dve.wait_ge(inn[slot], c * 8 + (16 if slot == 0 else 8))
                    for g in range(G):
                        at = bass.ds(c * G + g, 1)
                        ins = nc.vector.scalar_tensor_tensor(out=junk[1][:, g, :], in0=ring[slot][:, g, :], scalar=1.0,
                                                             in1=B["rows_"]["wj1"][:, :], op0=ALU.mult, op1=ALU.mult,
                                                             accum_out=aj[:, at])
                    ins.then_inc(free, 1)
                over_chunks(dve, dots)
        else:
            rows_in = [sem(f"rows{n}") for n in range(4)]
            aj_in = [sem(f"aj{n}") for n in range(4)]
            bare = BareRows(nc, ctx, B, "c1")
            block = ctx.enter_context(nc.Block())

            @block.vector
            def _(dve):
                bare.vector(dve)

            @block.scalar
            def _(act):
                bare.scalar(act)

            @block.sync
            def _(sp):
                bare.sync(sp)

            @block.gpsimd
            def _(gp):
                for t in range(T):
                    if t >= 4:
                        gp.wait_ge(rows_in[t % 4], 16 * (t // 4))
                        gp.wait_ge(aj_in[t % 4], 16 * (t // 4))
                    gp.indirect_dma_start(out=big[:, t, :], out_offset=None, in_=B["hidden"],
                                          in_offset=bass.IndirectOffsetOnAxis(ap=B["src_start_i"][:, t:t + 1], axis=0))\
                      .then_inc(rows_in[t % 4], 16)
                    gp.indirect_dma_start(out=aj[:, t:t + 1], out_offset=None, in_=B["hidden_aj"],
                                          in_offset=bass.IndirectOffsetOnAxis(ap=B["dst_start_i"][:, t:t + 1], axis=0))\
                      .then_inc(aj_in[t % 4], 16)
                for n in range(4):
                    gp.wait_ge(rows_in[n], 16 * (T // 4))
                    gp.wait_ge(aj_in[n], 16 * (T // 4))

    with phase(nc) as ctx:
        def sem(n):
            return semaphore(nc, ctx, f"m{layer}_" + n)
        own, cols_up, rows_up, shifted, exp_up = (sem(n) for n in ("own", "cols", "rows", "shifted", "exp"))
        diag = [ctx.enter_context(nc.sbuf_tensor(f"m{layer}_diag{n}", [P, P], F32)) for n in range(2)]
        masked = [ctx.enter_context(nc.sbuf_tensor(f"m{layer}_masked{n}", [P, P], F32)) for n in range(2)]
        most = ctx.enter_context(nc.sbuf_tensor(f"m{layer}_most", [P, 2], F32))
        block = ctx.enter_context(nc.Block())

        @block.vector
        def _(dve):
            fin = Finished(dve, own)
            if layer == 1:
                fin.after(nc.vector.tensor_copy(ai[:, :], big[:, 0:T, D]))
            edge_logits(dve, nc, B, fin, ai[:, :], aj[:, :], ex[:, :], tmp[0][:, :])
            nc.vector.tensor_scalar(tmp[0][:, :], q["same"][:, :], 1.0, HUGE, ALU.subtract, ALU.mult)
            fin.after(nc.vector.tensor_scalar(tmp[1][:, :], q["next"][:, :], 1.0, HUGE, ALU.subtract, ALU.mult))
            fin.after(nc.vector.tensor_tensor_scan(tmp[2][:, :], tmp[0][:, :], ex[:, :], -HUGE, ALU.add, ALU.max))
            fin.after(nc.vector.tensor_tensor_scan(top[:, ::-1], tmp[1][:, ::-1], tmp[2][:, ::-1], -HUGE, ALU.add, ALU.max))
            nc.vector.tensor_scalar(diag[0][:, :], B["ident"][:, :], tmp[2][:, T - 1:T], None, ALU.mult)
            nc.vector.tensor_scalar(diag[1][:, :], B["ident"][:, :], top[:, 0:1], None, ALU.mult).then_inc(cols_up, 1)
            nc.vector.tensor_scalar(masked[0][:, :], q["sel_before"][:, :], 1.0, HUGE, ALU.subtract, ALU.mult)
            fin.after(nc.vector.tensor_scalar(masked[1][:, :], q["sel_later"][:, :], 1.0, HUGE, ALU.subtract, ALU.mult))
            dve.wait_ge(rows_up, 1)
            nc.vector.tensor_tensor(masked[0][:, :], ps[0][:, 0:P], masked[0][:, :], ALU.add)
            fin.after(nc.vector.tensor_tensor(masked[1][:, :], ps[1][:, 0:P], masked[1][:, :], ALU.add))
            nc.vector.reduce_max(most[:, 0:1], masked[0][:, :], AX.X)
            nc.vector.reduce_max(most[:, 1:2], masked[1][:, :], AX.X)
            nc.vector.tensor_scalar(tmp[0][:, :], B["dst_key"][:, :], B["dst_key"][:, 0:1], None, ALU.is_equal)
            fin.after(nc.vector.tensor_scalar(tmp[1][:, :], q["tail"][:, :], 1.0, HUGE, ALU.subtract, ALU.mult))
            fin.after(nc.vector.tensor_scalar(tmp[0][:, :], tmp[0][:, :], 1.0, HUGE, ALU.subtract, ALU.mult))
            for n in range(2):
                fin.after(nc.vector.scalar_tensor_tensor(out=top[:, :], in0=tmp[n][:, :], scalar=most[:, n:n + 1],
                                                         in1=top[:, :], op0=ALU.add, op1=ALU.max))
            nc.vector.tensor_tensor(tmp[3][:, :], ex[:, :], top[:, :], ALU.subtract).then_inc(shifted, 1)
            nc.vector.tensor_copy(big[:, 0:T, 130], top[:, :])
            nc.vector.tensor_copy(big[:, 0:T, 131], aj[:, :])
            nc.vector.memset(big[:, 0:T, 129], 1.0)
            dve.wait_ge(exp_up, 1)
            fin.after(nc.vector.tensor_copy(big[:, 0:T, D], ex[:, :]))

        @block.tensor
        def _(pe):
            pe.wait_ge(cols_up, 1)
            for n in range(2):
                last = nc.tensor.matmul(ps[n][:, 0:P], B["ones"][:, :], diag[n][:, :], start=True, stop=True)
            last.then_inc(rows_up, 1)

        @block.scalar
        def _(act):
            act.wait_ge(shifted, 1)
            nc.scalar.activation(ex[:, :], tmp[3][:, :], ACT.Exp).then_inc(exp_up, 1)

    running_sums(nc, B, "d", ex, f"se{layer}_")

    with phase(nc) as ctx:
        fixed, stored = (semaphore(nc, ctx, n) for n in (f"w{layer}_fixed", f"w{layer}_stored"))
        block = ctx.enter_context(nc.Block())

        @block.vector
        def _(dve):
            with dve.Fori(0, T // 4, 1) as i:
                for j in range(4):
                    t = i * 4 + j
                    nc.vector.scalar_tensor_tensor(
                        out=row(big[:, bass.ds(t, 1), 0:130]), in0=q["extra"][:, 0:130], scalar=q["fix"][:, bass.ds(t, 1)],
                        in1=row(big[:, bass.ds(t, 1), 0:130]), op0=ALU.mult, op1=ALU.add).then_inc(fixed, 1)

        @block.sync
        def _(sp):
            table = B["sums"][layer].rearrange("(p t) d -> p t d", t=T)
            for c in range(7):
                sp.wait_ge(fixed, 28 * (c + 1))
                sp.dma_start(table[:, 28 * c:28 * c + 28, :], big[:, 28 * c:28 * c + 28, :]).then_inc(stored, 16)
            sp.wait_ge(stored, 16 * 7)


def by_source(nc, B):
    with phase(nc) as ctx:
        def sem(n):
            return semaphore(nc, ctx, "b_" + n)
        own, packed, edged, loaded = (sem(n) for n in ("own", "packed", "edged", "loaded"))
        sent = [sem(f"sent{n}") for n in range(4)]
        rec = ctx.enter_context(nc.sbuf_tensor("rec", [P, T, 4], F32))
        back = ctx.enter_context(nc.sbuf_tensor("back", [P, T, 4], F32))
        prev = ctx.enter_context(nc.sbuf_tensor("prev_rec", [P, T, 4], F32))
        front = ctx.enter_context(nc.sbuf_tensor("front", [1, 4], F32))
        bare = BareRows(nc, ctx, B, "b")
        block = ctx.enter_context(nc.Block())
        table = B["record"]

        @block.vector
        def _(dve):
            fin = Finished(dve, own)
            nc.vector.memset(front[:, :], -1.0)
            fin.after(nc.vector.memset(rec[:, :, :], 0.0))
            nc.vector.tensor_copy(rec[:, :, 0], B["orders"]["d"]["start"][:, :])
            nc.vector.tensor_copy(rec[:, :, 2], B["ai"][:, :])
            nc.vector.tensor_copy(rec[:, :, 1], B["src_key"][:, :]).then_inc(packed, 1)
            bare.vector(dve)
            dve.wait_ge(loaded, 32)
            nc.vector.tensor_copy(B["ai"][:, :], back[:, :, 2])
            nc.vector.tensor_copy(B["s_key"][:, :], back[:, :, 1])
            nc.vector.tensor_copy(B["s_dstart_i"][:, :], back[:, :, 0])
            nc.vector.tensor_copy(B["orders"]["s"]["prev"][:, :], prev[:, :, 1])
            nc.vector.tensor_scalar(B["s_gather"][:, :], back[:, :, 1], float(N - 1), None, ALU.min)

        @block.gpsimd
        def _(gp):
            gp.wait_ge(packed, 1)
            for t in range(T):
                if t >= 4:
                    gp.wait_ge(sent[t % 4], 16 * (t // 4))
                gp.indirect_dma_start(out=table, out_offset=bass.IndirectOffsetOnAxis(ap=B["src_place_i"][:, t:t + 1], axis=0),
                                      in_=rec[:, t, :], in_offset=None).then_inc(sent[t % 4], 16)

        @block.scalar
        def _(act):
            bare.scalar(act)

        @block.sync
        def _(sp):
            sp.wait_ge(own, 1)
            sp.dma_start(table[0:1, :], front[:, :]).then_inc(edged, 16)
            bare.sync(sp)
            sp.wait_ge(edged, 16)
            for n in range(4):
                sp.wait_ge(sent[n], 16 * (T // 4))
            sp.dma_start(back[:, :, :], table[1:EP + 1, :].rearrange("(p t) c -> p t c", t=T)).then_inc(loaded, 16)
            sp.dma_start(prev[:, :, :], table[0:EP, :].rearrange("(p t) c -> p t c", t=T)).then_inc(loaded, 16)


def conv_nodes(nc, B, layer):
    q, big, ps, tmp = B["orders"]["s"], B["big"], B["ps"], B["tmp"]
    ai, coef, top, ex = B["ai"], B["coef"], B["top"], B["ex"]
    with phase(nc) as ctx:
        def sem(n):
            return semaphore(nc, ctx, f"n{layer}_" + n)
        big_in = [sem(f"big{n}") for n in range(4)]
        bare = BareRows(nc, ctx, B, f"n{layer}")
        block = ctx.enter_context(nc.Block())

        @block.gpsimd
        def _(gp):
            for t in range(T):
                if t >= 4:
                    gp.wait_ge(big_in[t % 4], 16 * (t // 4))
                gp.indirect_dma_start(out=big[:, t, :], out_offset=None, in_=B["sums"][layer],
                                      in_offset=bass.IndirectOffsetOnAxis(ap=B["s_dstart_i"][:, t:t + 1], axis=0))\
                  .then_inc(big_in[t % 4], 16)
            for n in range(4):
                gp.wait_ge(big_in[n], 16 * (T // 4))

        @block.vector
        def _(dve):
            bare.vector(dve)

        @block.scalar
        def _(act):
            bare.scalar(act)

        @block.sync
        def _(sp):
            bare.sync(sp)

    with phase(nc) as ctx:
        def sem(n):
            return semaphore(nc, ctx, f"a{layer}_" + n)
        own, shifted, exp_up, sent, came = (sem(n) for n in ("own", "shifted", "exp", "sent", "came"))
        block = ctx.enter_context(nc.Block())

        @block.vector
        def _(dve):
            fin = Finished(dve, own)
            if layer == 1:
                propagate(dve, nc, B, "s", fin, B["ai2_s"][:, :], ai, tmp[2], sent, came, 1)
            edge_logits(dve, nc, B, fin, ai[:, :], big[:, 0:T, 131], ex[:, :], tmp[0][:, :])
            nc.vector.tensor_tensor(tmp[1][:, :], ex[:, :], big[:, 0:T, 130], ALU.subtract).then_inc(shifted, 1)
            fin.after(nc.vector.tensor_scalar(tmp[0][:, :], big[:, 0:T, D], 1e-16, None, ALU.add))
            fin.after(nc.vector.tensor_tensor(tmp[0][:, :], tmp[0][:, :], tmp[0][:, :], ALU.mult))
            fin.after(nc.vector.tensor_tensor(tmp[0][:, :], tmp[0][:, :], big[:, 0:T, 129], ALU.mult))
            fin.after(nc.vector.reciprocal(tmp[3][:, :], tmp[0][:, :]))
            nc.vector.memset(big[:, 0:T, 129], 1.0)
            dve.wait_ge(exp_up, 1)
            fin.after(nc.vector.tensor_tensor(coef[:, :], ex[:, :], tmp[3][:, :], ALU.mult))

        @block.scalar
        def _(act):
            act.wait_ge(shifted, 1)
            nc.scalar.activation(ex[:, :], tmp[1][:, :], ACT.Exp).then_inc(exp_up, 1)

        if layer == 1:
            @block.tensor
            def _(pe):
                propagate_pe(pe, nc, B, "s", tmp[2], sent, came, 1)

    running_sums(nc, B, "s", coef, f"sn{layer}_")
    if layer == 0:
        first_rows(nc, B)
    else:
        second_rows(nc, B)


def bank_rows(ps, first):
    return [ps[first + g // 4][:, (g % 4) * D:(g % 4) * D + D] for g in range(G)]


def fix_step(nc, B, o, dest, t):
    q = B["orders"][o]
    return nc.vector.scalar_tensor_tensor(
        out=dest, in0=q["extra"][:, 0:130], scalar=q["fix"][:, bass.ds(t, 1)],
        in1=row(B["big"][:, bass.ds(t, 1), 0:130]), op0=ALU.mult, op1=ALU.add)


def first_rows(nc, B):
    ps, rows_ = B["ps"], B["rows_"]
    with phase(nc) as ctx:
        def sem(n):
            return semaphore(nc, ctx, "h_" + n)

        def sb(n, shape):
            return ctx.enter_context(nc.sbuf_tensor("h_" + n, shape, F32))
        own, fixed, turned, copied, product, biased, active, dotted = (
            sem(n) for n in ("own", "fixed", "turned", "copied", "product", "biased", "active", "dotted"))
        stored = [sem(f"stored{n}") for n in range(2)]
        aj_stored, kept = sem("aj_stored"), sem("kept")
        full = [sb(f"full{n}", [P, G, W]) for n in range(2)]
        flipped = [sb(f"flipped{n}", [P, G * D]) for n in range(2)]
        inverse = [sb(f"inverse{n}", [P, G]) for n in range(2)]
        pre = [sb(f"pre{n}", [P, G, D]) for n in range(2)]
        below = [sb(f"below{n}", [P, G, D]) for n in range(2)]
        hid = [sb(f"hid{n}", [P, G, W]) for n in range(2)]
        junk = sb("junk", [P, 2 * G, D])
        aj_s = sb("aj_s", [P, T])
        block = ctx.enter_context(nc.Block())

        @block.vector
        def _(dve):
            fin = Finished(dve, own)
            dve.sem_inc(fixed, 1)
            dve.sem_inc(turned, 1)
            dve.sem_inc(kept, 1)
            nc.vector.memset(hid[0][:, :, :], 0.0)
            fin.after(nc.vector.memset(hid[1][:, :, :], 0.0))
            for n in range(2):
                dve.sem_inc(stored[n], 16)

            def fix(c, slot):
                for g in range(G):
                    ins = fix_step(nc, B, "s", full[slot][:, g, 0:130], c * G + g)
                ins.then_inc(fixed, 1)

            fix(0, 0)

            def body(c, slot, last):
                if not last:
                    dve.wait_ge(turned, c + 1)
                    fix(c + 1, 1 - slot)
                dve.wait_ge(fixed, c + 2)
                fin.after(nc.vector.reciprocal(inverse[slot][:, :], full[slot][:, :, 129]))
                dve.wait_ge(product, c + 1)
                for g, o in enumerate(bank_rows(ps, 4 + 2 * slot)):
                    ins = nc.vector.scalar_tensor_tensor(out=pre[slot][:, g, :], in0=o, scalar=inverse[slot][:, g:g + 1],
                                                         in1=rows_["b1"][:, :], op0=ALU.mult, op1=ALU.add)
                ins.then_inc(biased, 1)
                dve.wait_ge(active, c + 1)
                dve.wait_ge(stored[slot], c * 8 + (16 if slot == 0 else 8))
                dve.wait_ge(kept, c + 1)
                fin.after(nc.vector.scalar_tensor_tensor(out=hid[slot][:, :, 0:D], in0=below[slot][:, :, :],
                                                         scalar=B["drop"][:, 0:1], in1=pre[slot][:, :, :],
                                                         op0=ALU.mult, op1=ALU.add))
                for g in range(G):
                    at = bass.ds(c * G + g, 1)
                    nc.vector.scalar_tensor_tensor(out=junk[:, 2 * g, :], in0=hid[slot][:, g, 0:D], scalar=1.0, in1=rows_["wj2"][:, :],
                                                   op0=ALU.mult, op1=ALU.mult, accum_out=aj_s[:, at])
                    ins = nc.vector.scalar_tensor_tensor(out=junk[:, 2 * g + 1, :], in0=hid[slot][:, g, 0:D], scalar=1.0, in1=rows_["wi2"][:, :],
                                                         op0=ALU.mult, op1=ALU.mult, accum_out=hid[slot][:, g, D:D + 1])
                ins.then_inc(dotted, 1)
                dve.wait_ge(dotted, c + 1)
                nc.vector.tensor_copy(B["ai2_s"][:, bass.ds(c * G, G)], hid[slot][:, :, D]).then_inc(kept, 1)
            over_chunks(dve, body, [(fin, 2)])

        @block.tensor
        def _(pe):
            def body(c, slot, last):
                pe.wait_ge(fixed, c + 2)
                for g, o in enumerate(bank_rows(ps, 2 * slot)):
                    ins = nc.tensor.transpose(o, full[slot][:, g, 0:D], B["ident"][:, :])
                ins.then_inc(turned, 1)
                pe.wait_ge(copied, c + 1)
                for g, o in enumerate(bank_rows(ps, 4 + 2 * slot)):
                    ins = nc.tensor.matmul(o, flipped[slot][:, g * D:g * D + D], B["w1s"][:, :], start=True, stop=True)
                ins.then_inc(product, 1)
            over_chunks(pe, body)

        @block.scalar
        def _(act):
            def body(c, slot, last):
                act.wait_ge(turned, c + 2)
                nc.scalar.activation(flipped[slot][:, 0:4 * D], ps[2 * slot][:, 0:4 * D], ACT.Copy)
                nc.scalar.activation(flipped[slot][:, 4 * D:G * D], ps[2 * slot + 1][:, 0:3 * D], ACT.Copy).then_inc(copied, 1)
                act.wait_ge(biased, c + 1)
                nc.scalar.activation(below[slot][:, :, :], pre[slot][:, :, :], ACT.Relu, scale=-1.0).then_inc(active, 1)
            over_chunks(act, body)

        @block.sync
        def _(sp):
            table = B["hidden"][0:EP, :].rearrange("(p t) c -> p t c", t=T)

            def body(c, slot, last):
                sp.wait_ge(dotted, c + 1)
                sp.dma_start(table[:, bass.ds(c * G, G), :], hid[slot][:, :, :]).then_inc(stored[slot], 16)
            over_chunks(sp, body)
            sp.dma_start(B["hidden_aj"][0:EP, :].rearrange("(p t) c -> p (t c)", t=T), aj_s[:, :]).then_inc(aj_stored, 16)
            sp.wait_ge(aj_stored, 16)
            for n in range(2):
                sp.wait_ge(stored[n], 16 * (C // 2 + 1))


class Norm:

    def __init__(self, nc, ctx, name, parts, g, slots=2):
        self.nc, self.parts, self.g = nc, parts, g

        def sb(n, shape):
            return ctx.enter_context(nc.sbuf_tensor(name + n, shape, F32))
        self.stats = sb("stats", [P, g, 6])
        self.mean, self.gap, self.var, self.dev, self.inv = (sb(n, [P, g]) for n in ("mean", "gap", "var", "dev", "inv"))
        self.asked = semaphore(nc, ctx, name + "asked")
        self.answered = semaphore(nc, ctx, name + "answered")

    def dve(self, dve, fin, tally, rows, out):
        v, n, g = self.nc.vector, self.parts, self.g
        for k in range(g):
            ins = v.bn_stats(self.stats[0:n, k, :], rows[0:n, k, :])
        fin.after(ins)
        v.tensor_tensor(self.mean[0:n, :], self.stats[0:n, :, 1], self.stats[0:n, :, 4], ALU.add)
        v.tensor_tensor(self.var[0:n, :], self.stats[0:n, :, 2], self.stats[0:n, :, 5], ALU.add)
        fin.after(v.tensor_tensor(self.gap[0:n, :], self.stats[0:n, :, 1], self.stats[0:n, :, 4], ALU.subtract))
        v.tensor_scalar(self.mean[0:n, :], self.mean[0:n, :], 0.5, None, ALU.mult)
        fin.after(v.tensor_tensor(self.gap[0:n, :], self.gap[0:n, :], self.gap[0:n, :], ALU.mult))
        v.scalar_tensor_tensor(out=self.var[0:n, :], in0=self.gap[0:n, :], scalar=D / 4.0, in1=self.var[0:n, :],
                               op0=ALU.mult, op1=ALU.add).then_inc(self.asked, 1)
        dve.wait_ge(self.answered, tally.next())
        fin.after(v.reciprocal(self.inv[0:n, :], self.dev[0:n, :]))
        for k in range(g):
            ins = v.tensor_scalar(out[0:n, k, :], rows[0:n, k, :], self.mean[0:n, k:k + 1], self.inv[0:n, k:k + 1],
                                  ALU.subtract, ALU.mult)
        return ins

    def act(self, act, tally, eps):
        act.wait_ge(self.asked, tally.next())
        n = self.parts
        self.nc.scalar.activation(self.dev[0:n, :], self.var[0:n, :], ACT.Sqrt, bias=eps[0:n, 0:1], scale=1.0 / D)\
            .then_inc(self.answered, 1)


def wide(ap, g):
    return ap.rearrange("p (a d) -> p a d", a=1).to_broadcast([ap.shape[0], g, D])


FINISH_STEPS = 12


def finish(nc, B, norm, dve, fin, tally, y, z_in, z, out):
    n, g = norm.parts, norm.g
    v, rows_ = nc.vector, B["rows_"]
    fin.after(norm.dve(dve, fin, tally, z_in, z))
    fin.after(v.tensor_tensor(z[0:n, :, :], z[0:n, :, :], wide(rows_["gamma"][0:n, :], g), ALU.mult))
    fin.after(v.tensor_tensor(z[0:n, :, :], z[0:n, :, :], wide(rows_["beta"][0:n, :], g), ALU.add))
    fin.after(v.tensor_tensor(z[0:n, :, :], z[0:n, :, :], y[0:n, :, :], ALU.add))
    return norm.dve(dve, fin, tally, z, out)


def skip_and_prelu(nc, B, dve, fin, x_rows, below, v, n, g, asked, active, turn):
    fin.after(nc.vector.tensor_tensor(below[0:n, :, :], x_rows[0:n, :, :], wide(B["rows_"]["b2"][0:n, :], g), ALU.add))
    nc.vector.tensor_tensor(v[0:n, :, :], x_rows[0:n, :, :], below[0:n, :, :], ALU.add).then_inc(asked, 1)
    dve.wait_ge(asked, turn)
    dve.wait_ge(active, turn)
    fin.after(nc.vector.scalar_tensor_tensor(out=v[0:n, :, :], in0=below[0:n, :, :], scalar=B["drop"][0:n, 0:1],
                                             in1=v[0:n, :, :], op0=ALU.mult, op1=ALU.add))


class BareRows:

    def __init__(self, nc, ctx, B, name):
        self.nc, self.B, self.n = nc, B, BARE_CHUNKS[name]
        order = list(BARE_CHUNKS)
        assert sum(BARE_CHUNKS.values()) == DC and self.n % 2 == 0
        self.first = sum(BARE_CHUNKS[k] for k in order[:order.index(name)])

        def sem(n):
            return semaphore(nc, ctx, f"z{name}_" + n)

        def sb(n, shape):
            return ctx.enter_context(nc.sbuf_tensor(f"z{name}_" + n, shape, F32))
        self.own, self.act_own, self.x_free, self.below_up, self.clipped, self.mean_up, self.var_up = (
            sem(n) for n in ("own", "act_own", "x_free", "below_up", "clipped", "mean_up", "var_up"))
        self.roots_up, self.factor_up, self.u_up, self.u_var_up, self.done = (
            sem(n) for n in ("roots_up", "factor_up", "u_up", "u_var_up", "done"))
        self.x_in, self.stored = ([sem(f"{n}{k}") for k in range(2)] for n in ("x_in", "stored"))
        self.x, self.v, self.result = ([sb(f"{n}{k}", [DP, DG, D]) for k in range(2)] for n in ("x", "v", "result"))
        self.below, self.factor = sb("below", [DP, DG, D]), sb("factor", [DP, DG, D])
        self.sum, self.mean, self.squares, self.u_sum, self.u_mean, self.u_squares, self.u_dev, self.u_inv = (
            sb(n, [DP, DG]) for n in ("sum", "mean", "squares", "u_sum", "u_mean", "u_squares", "u_dev", "u_inv"))
        self.dev, self.inv = sb("dev", [DP, 2, DG]), sb("inv", [DP, 2, DG])

    def turns(self, eng, body, tallies=()):
        for slot in range(2):
            body(0, slot, True, slot == 1, False)
        pairs = self.n // 2 - 1
        with eng.Fori(0, pairs, 1) as i:
            for tally, each in tallies:
                tally.loop(i, 2 * each)
            for slot in range(2):
                body(i + 1, slot, True, True, True)
        for tally, each in tallies:
            tally.end(pairs, 2 * each)
        for slot in range(2):
            body(self.n // 2, slot, False, slot == 0, True)

    def vector(self, dve):
        v, B = self.nc.vector, self.B
        fin = Finished(dve, self.own)
        for n in range(2):
            dve.sem_inc(self.stored[n], 16)
        b2, beta = B["rows_"]["b2"][0:DP, :], B["rows_"]["beta"][0:DP, :]

        def body(pair, slot, new, middle, old):
            c = pair * 2 + slot
            this, last = self.v[slot], self.v[1 - slot]
            if middle:
                dve.wait_ge(self.var_up, c)
                v.reciprocal(self.inv[:, :, :], self.dev[:, :, :]).then_inc(self.roots_up, 1)
            if old:
                dve.wait_ge(self.u_var_up, c - 1)
                fin.after(v.reciprocal(self.u_inv[:, :], self.u_dev[:, :]))
                dve.wait_ge(self.stored[slot], pair * 16)
                for g in range(DG):
                    ins = v.tensor_scalar(self.result[slot][:, g, :], this[:, g, :], self.u_mean[:, g:g + 1],
                                          self.u_inv[:, g:g + 1], ALU.add, ALU.mult)
                ins.then_inc(self.done, 1)
                dve.wait_ge(self.done, c - 1)
            if new:
                dve.wait_ge(self.x_in[slot], pair * 16 + 16)
                v.tensor_tensor(self.below[:, :, :], self.x[slot][:, :, :], wide(b2, DG), ALU.add).then_inc(self.below_up, 1)
                v.scalar_tensor_tensor(out=this[:, :, :], in0=self.x[slot][:, :, :], scalar=2.0, in1=wide(b2, DG),
                                       op0=ALU.mult, op1=ALU.add).then_inc(self.x_free, 1)
            if middle:
                dve.wait_ge(self.factor_up, c)
                for g in range(DG):
                    ins = v.scalar_tensor_tensor(out=last[:, g, :], in0=last[:, g, :], scalar=self.mean[:, g:g + 1],
                                                 in1=self.factor[:, g, :], op0=ALU.add, op1=ALU.mult)
                fin.after(ins)
                for g in range(DG):
                    ins = v.scalar_tensor_tensor(out=last[:, g, :], in0=last[:, g, :], scalar=1.0, in1=beta,
                                                 op0=ALU.mult, op1=ALU.add, accum_out=self.u_sum[:, g:g + 1])
                fin.after(ins)
                v.tensor_scalar(self.u_mean[:, :], self.u_sum[:, :], -1.0 / D, None, ALU.mult).then_inc(self.u_up, 1)
            if new:
                dve.wait_ge(self.clipped, c + 1)
                dve.wait_ge(self.x_free, c + 1)
                for g in range(DG):
                    ins = v.scalar_tensor_tensor(out=this[:, g, :], in0=self.below[:, g, :], scalar=B["drop"][0:DP, 0:1],
                                                 in1=this[:, g, :], op0=ALU.mult, op1=ALU.add,
                                                 accum_out=self.sum[:, g:g + 1])
                fin.after(ins)
                v.tensor_scalar(self.mean[:, :], self.sum[:, :], -1.0 / D, None, ALU.mult).then_inc(self.mean_up, 1)
                dve.wait_ge(self.mean_up, c + 1)
        self.turns(dve, body, [(fin, 4)])

    def scalar(self, act):
        a, B = self.nc.scalar, self.B
        fin = Finished(act, self.act_own)
        gamma, eps, eps_sq = B["rows_"]["gamma"][0:DP, :], B["eps"][0:DP, 0:1], B["eps_sq"][0:DP, 0:1]

        def squares(rows, mean, unused, total):
            for g in range(DG):
                ins = a.activation(unused[:, g, :], rows[:, g, :], ACT.Square, bias=mean[:, g:g + 1],
                                   accum_out=total[:, g:g + 1])
            fin.after(ins)

        def body(pair, slot, new, middle, old):
            c = pair * 2 + slot
            if middle:
                act.wait_ge(self.roots_up, c)
                for g in range(DG):
                    ins = a.activation(self.factor[:, g, :], gamma, ACT.Identity, bias=self.inv[:, 0, g:g + 1],
                                       scale=self.inv[:, 1, g:g + 1])
                ins.then_inc(self.factor_up, 1)
            if new:
                act.wait_ge(self.below_up, c + 1)
                a.activation(self.below[:, :, :], self.below[:, :, :], ACT.Relu, scale=-1.0).then_inc(self.clipped, 1)
            if middle:
                act.wait_ge(self.u_up, c)
                squares(self.v[1 - slot], self.u_mean, self.factor, self.u_squares)
                a.activation(self.u_dev[:, :], self.u_squares[:, :], ACT.Sqrt, bias=eps, scale=1.0 / D)\
                    .then_inc(self.u_var_up, 1)
            if new:
                act.wait_ge(self.mean_up, c + 1)
                squares(self.v[slot], self.mean, self.below, self.squares)
                a.activation(self.dev[:, 0, :], self.squares[:, :], ACT.Sqrt, bias=eps, scale=1.0 / D)
                a.activation(self.dev[:, 1, :], self.squares[:, :], ACT.Sqrt, bias=eps_sq, scale=(1.0 + EPS) / D)\
                    .then_inc(self.var_up, 1)
                act.wait_ge(self.var_up, c + 1)
        self.turns(act, body, [(fin, 2)])

    def sync(self, sp):
        rows = DP * DG

        def at(table, c):
            flat = table[self.first * rows:(self.first + self.n) * rows, :].rearrange("(c p g) d -> c p g d", p=DP, g=DG)
            return flat[bass.ds(c, 1), :, :, :].rearrange("c p g d -> (c p) g d")

        def load(c, slot):
            sp.dma_start(self.x[slot][:, :, :], at(self.B["x"], c)).then_inc(self.x_in[slot], 16)

        def store(c, slot):
            sp.wait_ge(self.done, c + 1)
            sp.dma_start(at(self.B["out"], c), self.result[slot][:, :, :]).then_inc(self.stored[slot], 16)
        load(0, 0)
        load(1, 1)
        with sp.Fori(0, self.n // 2 - 1, 1) as i:
            for slot in range(2):
                sp.wait_ge(self.x_free, i * 2 + slot + 1)
                load(i * 2 + slot + 2, slot)
                store(i * 2 + slot, slot)
        for slot in range(2):
            store(self.n - 2 + slot, slot)
        for slot in range(2):
            sp.wait_ge(self.stored[slot], 16 * (self.n // 2 + 1))


def second_rows(nc, B):
    ps, rows_ = B["ps"], B["rows_"]
    with phase(nc) as ctx:
        def sem(n):
            return semaphore(nc, ctx, "g_" + n)

        def sb(n, shape):
            return ctx.enter_context(nc.sbuf_tensor("g_" + n, shape, F32))
        own, fixed, turned, copied, product, biased, summed, active, y_up, y_turned, y_copied, y_product, m_up, done = (
            sem(n) for n in ("own", "fixed", "turned", "copied", "product", "biased", "summed", "active", "y_up",
                             "y_turned", "y_copied", "y_product", "m_up", "done"))
        y_stored, m_stored = ([sem(f"{n}{k}") for k in range(2)] for n in ("y_stored", "m_stored"))
        x_in = [sem(f"x_in{n}") for n in range(G)]
        scattered = [sem(f"sc{n}") for n in range(G)]
        x_free, z_free = sem("x_free"), sem("z_free")
        full = [sb(f"full{n}", [P, G, 130]) for n in range(2)]
        flipped, y_flipped = sb("flipped", [P, G * D]), sb("y_flipped", [P, G * D])
        inverse = sb("inverse", [P, G])
        xs = [sb(f"x{n}", [P, G, D]) for n in range(2)]
        pre, v = sb("pre", [P, G, D]), sb("v", [P, G, D])
        ys = [sb(f"y{n}", [P, G, D]) for n in range(2)]
        ms = [sb(f"m{n}", [P, G, D]) for n in range(2)]
        result = [sb(f"result{n}", [P, G, D]) for n in range(2)]
        norm = Norm(nc, ctx, "gn_", P, G)
        block = ctx.enter_context(nc.Block())
        each = 1 + 2 + 4 + FINISH_STEPS + 1

        @block.vector
        def _(dve):
            fin, roots = Finished(dve, own), Tally()
            dve.sem_inc(x_free, 2)
            dve.sem_inc(fixed, 1)
            for credited in (turned, y_turned, m_up, y_product):
                dve.sem_inc(credited, 1)
            for n in range(2):
                dve.sem_inc(y_stored[n], 16)
                dve.sem_inc(m_stored[n], 16)
            dve.sem_inc(z_free, 2)

            def fix(c, slot):
                for g in range(G):
                    ins = fix_step(nc, B, "s", full[slot][:, g, :], c * G + g)
                ins.then_inc(fixed, 1)

            fix(0, 0)

            def body(c, slot, last):
                if not last:
                    dve.wait_ge(turned, c + 1)
                    fix(c + 1, 1 - slot)
                dve.wait_ge(fixed, c + 2)
                fin.after(nc.vector.reciprocal(inverse[:, :], full[slot][:, :, 129]))
                dve.wait_ge(product, c + 1)
                for g, o in enumerate(bank_rows(ps, 2)):
                    ins = nc.vector.scalar_tensor_tensor(out=pre[:, g, :], in0=o, scalar=inverse[:, g:g + 1],
                                                         in1=rows_["b2"][:, :], op0=ALU.mult, op1=ALU.add)
                ins.then_inc(biased, 1)
                dve.wait_ge(biased, c + 1)
                for n in range(G):
                    dve.wait_ge(x_in[n], c * 16 + 16)
                fin.after(nc.vector.tensor_tensor(pre[:, :, :], pre[:, :, :], xs[slot][:, :, :], ALU.add))
                nc.vector.tensor_tensor(v[:, :, :], pre[:, :, :], xs[slot][:, :, :], ALU.add).then_inc(summed, 1)
                dve.wait_ge(summed, c + 1)
                dve.wait_ge(active, c + 1)
                fin.after(nc.vector.scalar_tensor_tensor(out=v[:, :, :], in0=pre[:, :, :], scalar=B["drop"][:, 0:1],
                                                         in1=v[:, :, :], op0=ALU.mult, op1=ALU.add))
                dve.sem_inc(x_free, 1)
                dve.wait_ge(y_stored[slot], c * 8 + (16 if slot == 0 else 8))
                dve.wait_ge(y_turned, c + 1)
                norm.dve(dve, fin, roots, v, ys[slot]).then_inc(y_up, 1)
                dve.wait_ge(y_up, c + 1)
                dve.wait_ge(z_free, c + 1)
                fin.after(finish(nc, B, norm, dve, fin, roots, ys[slot], ys[slot], pre, result[slot]))
                dve.sem_inc(done, 1)
            over_chunks(dve, body, [(fin, each), (roots, 3)])

        @block.tensor
        def _(pe):
            def rows_of(c, slot, free):
                pe.wait_ge(fixed, c + 2)
                for g, o in enumerate(bank_rows(ps, 0)):
                    ins = nc.tensor.transpose(o, full[slot][:, g, 0:D], B["ident"][:, :])
                ins.then_inc(turned, 1)
                pe.wait_ge(copied, c + 1)
                pe.wait_ge(biased, free)
                for g, o in enumerate(bank_rows(ps, 2)):
                    ins = nc.tensor.matmul(o, flipped[:, g * D:g * D + D], B["w2s"][:, :], start=True, stop=True)
                ins.then_inc(product, 1)
            rows_of(0, 0, 0)

            def body(c, slot, last):
                if not last:
                    rows_of(c + 1, 1 - slot, c + 1)
                pe.wait_ge(y_up, c + 1)
                for g, o in enumerate(bank_rows(ps, 4)):
                    ins = nc.tensor.transpose(o, ys[slot][:, g, :], B["ident"][:, :])
                ins.then_inc(y_turned, 1)
                pe.wait_ge(y_copied, c + 1)
                pe.wait_ge(m_up, c + 1)
                for g, o in enumerate(bank_rows(ps, 6)):
                    ins = nc.tensor.matmul(o, y_flipped[:, g * D:g * D + D], B["m1s"][:, :], start=True, stop=True)
                ins.then_inc(y_product, 1)
            over_chunks(pe, body)

        def copy_flipped(dest, first, sem_up):
            nc.scalar.activation(dest[:, 0:4 * D], ps[first][:, 0:4 * D], ACT.Copy)
            nc.scalar.activation(dest[:, 4 * D:G * D], ps[first + 1][:, 0:3 * D], ACT.Copy).then_inc(sem_up, 1)

        @block.scalar
        def _(act):
            roots = Tally()

            def rows_of(c, done_before):
                act.wait_ge(turned, c + 2)
                act.wait_ge(product, done_before)
                copy_flipped(flipped, 0, copied)
            rows_of(0, 0)

            def body(c, slot, last):
                if not last:
                    rows_of(c + 1, c + 1)
                act.wait_ge(summed, c + 1)
                nc.scalar.activation(pre[:, :, :], pre[:, :, :], ACT.Relu, scale=-1.0).then_inc(active, 1)
                norm.act(act, roots, B["eps"])
                act.wait_ge(y_turned, c + 2)
                act.wait_ge(y_product, c + 1)
                copy_flipped(y_flipped, 4, y_copied)
                norm.act(act, roots, B["eps"])
                act.wait_ge(y_product, c + 2)
                act.wait_ge(m_stored[slot], c * 8 + (16 if slot == 0 else 8))
                flat = ms[slot][:, :, :].rearrange("p g d -> p (g d)")
                copy_flipped(flat, 6, m_up)
                norm.act(act, roots, B["eps"])
            over_chunks(act, body, [(roots, 3)])

        @block.sync
        def _(sp):
            def at(table, c):
                return table.rearrange("(p t) d -> p t d", t=T)[:, bass.ds(c * G, G), :]

            def body(c, slot, last):
                sp.wait_ge(y_up, c + 1)
                sp.dma_start(at(B["mixed"][0:EP, :], c), ys[slot][:, :, :]).then_inc(y_stored[slot], 16)
                sp.wait_ge(m_up, c + 2)
                sp.dma_start(at(B["mixed_m"][0:EP, :], c), ms[slot][:, :, :]).then_inc(m_stored[slot], 16)
            over_chunks(sp, body)
            for n in range(2):
                sp.wait_ge(y_stored[n], 16 * (C // 2 + 1))
                sp.wait_ge(m_stored[n], 16 * (C // 2 + 1))

        @block.gpsimd
        def _(gp):
            def gather(c):
                for g in range(G):
                    if c >= 1:
                        gp.wait_ge(x_in[g], 16 * c)
                    t = c * G + g
                    gp.indirect_dma_start(out=xs[c % 2][:, g, :], out_offset=None, in_=B["x"],
                                          in_offset=bass.IndirectOffsetOnAxis(ap=B["s_gather"][:, t:t + 1], axis=0))\
                      .then_inc(x_in[g], 16)
            gather(0)
            for c in range(C):
                if c + 1 < C:
                    gp.wait_ge(x_free, c + 2)
                    gather(c + 1)
                if c:
                    scattered_chunk(gp, scattered, z_free, c - 1)
                scatter_chunk(gp, B, "s_scatter", result, done, scattered, z_free, c)
            scattered_chunk(gp, scattered, z_free, C - 1)


def scatter_chunk(gp, B, name, result, done, scattered, free, c):
    gp.wait_ge(done, c + 1)
    for g in range(G):
        t = c * G + g
        gp.indirect_dma_start(out=B["out"], out_offset=bass.IndirectOffsetOnAxis(ap=B[name][:, t:t + 1], axis=0),
                              in_=result[c % 2][:, g, :], in_offset=None, bounds_check=N - 1, oob_is_err=False)\
          .then_inc(scattered[g], 16)


def scattered_chunk(gp, scattered, free, c):
    for g in range(G):
        gp.wait_ge(scattered[g], 16 * (c + 1))
    gp.sem_inc(free, 1)


def edge_network(nc, B):
    ps, rows_, big = B["ps"], B["rows_"], B["big"]
    with phase(nc) as ctx:
        def sem(n):
            return semaphore(nc, ctx, "u_" + n)

        def sb(n, shape):
            return ctx.enter_context(nc.sbuf_tensor("u_" + n, shape, F32))
        own, attr_in, cleared, sliced, turned, copied, product, summed = (
            sem(n) for n in ("own", "attr_in", "cleared", "sliced", "turned", "copied", "product", "summed"))
        big_in = [sem(f"big{n}") for n in range(G)]
        attr = sb("attr", [P, T, 4])
        piece = [sb(f"piece{n}", [P, 4 * G]) for n in range(2)]
        flipped = [sb(f"flipped{n}", [4 * G, P]) for n in range(2)]
        block = ctx.enter_context(nc.Block())

        @block.gpsimd
        def _(gp):
            gp.wait_ge(cleared, 1)
            for t in range(T):
                if t >= G:
                    gp.wait_ge(big_in[t % G], 16 * (t // G))
                gp.indirect_dma_start(out=big[:, t, 0:D], out_offset=None, in_=B["mixed_m"],
                                      in_offset=bass.IndirectOffsetOnAxis(ap=B["src_start_i"][:, t:t + 1], axis=0))\
                  .then_inc(big_in[t % G], 16)

        @block.sync
        def _(sp):
            sp.wait_ge(cleared, 1)
            sp.dma_start(attr[0:LAST, :, 0:3], B["edge_attr"][0:LAST * T, :].rearrange("(p t) k -> p t k", t=T))\
              .then_inc(attr_in, 16)
            sp.dma_start(attr[LAST:P, 0:LEFT, 0:3], B["edge_attr"][LAST * T:E, :].rearrange("(p t) k -> p t k", p=1))\
              .then_inc(attr_in, 16)
            for g in range(G):
                sp.dma_start(B["edge_w"][4 * g:4 * g + 3, g * D:g * D + D], B["m1"][D:D + 3, :]).then_inc(attr_in, 16)
                sp.dma_start(B["edge_w"][4 * g + 3:4 * g + 4, g * D:g * D + D], B["mb1"].rearrange("(a n) -> a n", a=1))\
                  .then_inc(attr_in, 16)

        @block.vector
        def _(dve):
            fin = Finished(dve, own)
            dve.sem_inc(turned, 1)
            fin.after(nc.vector.memset(attr[:, :, :], 0.0))
            nc.vector.memset(attr[:, :, 3], 1.0)
            nc.vector.memset(big[:, 0:T, 129], 1.0)
            nc.vector.memset(B["edge_w"][:, :], 0.0).then_inc(cleared, 1)
            dve.wait_ge(attr_in, 16 * (2 + 2 * G))
            nc.vector.tensor_copy(piece[0][:, :], attr[:, 0:G, :].rearrange("p g k -> p (g k)")).then_inc(sliced, 1)
            dve.wait_ge(sliced, 1)

            def body(c, slot, last):
                if not last:
                    dve.wait_ge(turned, c + 1)
                    nc.vector.tensor_copy(piece[1 - slot][:, :].rearrange("p (g k) -> p g k", k=4),
                                          attr[:, bass.ds(c * G + G, G), :]).then_inc(sliced, 1)
                dve.wait_ge(product, c + 1)
                for n in range(G):
                    dve.wait_ge(big_in[n], c * 16 + 16)
                for first, n in ((0, 4), (4, 3)):
                    rows = big[:, bass.ds(c * G + first, n), 0:D]
                    ins = nc.vector.tensor_tensor(
                        rows, ps[2 + 2 * slot + first // 4][:, 0:n * D].rearrange("p (g d) -> p g d", d=D), rows, ALU.add)
                ins.then_inc(summed, 1)
            over_chunks(dve, body)

        @block.tensor
        def _(pe):
            def body(c, slot, last):
                pe.wait_ge(sliced, c + 1)
                nc.tensor.transpose(ps[slot][0:4 * G, 0:P], piece[slot][:, :], B["ident"][:, :]).then_inc(turned, 1)
                pe.wait_ge(copied, c + 1)
                for n, wd in ((0, 4 * D), (1, 3 * D)):
                    ins = nc.tensor.matmul(ps[2 + 2 * slot + n][:, 0:wd], flipped[slot][:, :],
                                           B["edge_w"][:, n * 4 * D:n * 4 * D + wd], start=True, stop=True)
                ins.then_inc(product, 1)
            over_chunks(pe, body)

        @block.scalar
        def _(act):
            def body(c, slot, last):
                act.wait_ge(turned, c + 2)
                nc.scalar.activation(flipped[slot][:, :], ps[slot][0:4 * G, 0:P], ACT.Copy).then_inc(copied, 1)
                act.wait_ge(summed, c + 1)
                act.wait_ge(cleared, 1)
                rows = big[:, bass.ds(c * G, G), 0:D]
                nc.scalar.activation(rows, rows, ACT.Gelu)
            over_chunks(act, body)

    running_sums(nc, B, "d", None, "su_")
    with phase(nc) as ctx:
        def sem(n):
            return semaphore(nc, ctx, "v_" + n)

        def sb(n, shape):
            return ctx.enter_context(nc.sbuf_tensor("v_" + n, shape, F32))
        own, fixed, turned, copied, product, used, asked, active, done, freed = (
            sem(n) for n in ("own", "fixed", "turned", "copied", "product", "used", "asked", "active", "done", "freed"))
        x_in = [sem(f"x_in{n}") for n in range(2)]
        x_free, y_free = sem("x_free"), sem("y_free")
        y_in = [sem(f"y_in{n}") for n in range(G)]
        scattered = [sem(f"sc{n}") for n in range(G)]
        full = [sb(f"full{n}", [P, G, 130]) for n in range(2)]
        flipped = sb("flipped", [P, G * D])
        xs, ys, result = ([sb(f"{k}{n}", [P, G, D]) for n in range(2)] for k in ("x", "y", "result"))
        spare, z = sb("spare", [P, G, D]), sb("z", [P, G, D])
        norm = Norm(nc, ctx, "vn_", P, G)
        block = ctx.enter_context(nc.Block())
        each = 2 + 4 + 1 + 1 + 1 + FINISH_STEPS + 1

        @block.vector
        def _(dve):
            fin, roots = Finished(dve, own), Tally()
            dve.sem_inc(fixed, 1)
            dve.sem_inc(turned, 1)
            dve.sem_inc(used, 1)
            dve.sem_inc(x_free, 2)
            dve.sem_inc(freed, 2)
            nc.vector.tensor_scalar(B["absent"][:, :], B["dst_start"][:, :], float(ABSENT), None, ALU.is_equal)

            def fix(c, slot):
                for g in range(G):
                    ins = fix_step(nc, B, "d", full[slot][:, g, :], c * G + g)
                ins.then_inc(fixed, 1)

            fix(0, 0)

            def body(c, slot, last):
                if not last:
                    dve.wait_ge(turned, c + 1)
                    fix(c + 1, 1 - slot)
                dve.wait_ge(fixed, c + 2)
                dve.wait_ge(x_in[slot], c * 8 + (16 if slot == 0 else 8))
                skip_and_prelu(nc, B, dve, fin, xs[slot], z, spare, P, G, asked, active, c + 1)
                dve.sem_inc(x_free, 1)
                fin.after(norm.dve(dve, fin, roots, spare, spare))
                for n in range(G):
                    dve.wait_ge(y_in[n], c * 16 + 16)
                for g in range(G):
                    ins = nc.vector.scalar_tensor_tensor(
                        out=ys[slot][:, g, :], in0=spare[:, g, :], scalar=B["absent"][:, bass.ds(c * G + g, 1)],
                        in1=ys[slot][:, g, :], op0=ALU.mult, op1=ALU.add)
                fin.after(ins)
                dve.wait_ge(product, c + 1)
                for g, o in enumerate(bank_rows(ps, 2)):
                    ins = nc.vector.scalar_tensor_tensor(out=z[:, g, :], in0=rows_["mb2"][:, :], scalar=full[slot][:, g, 129:130],
                                                         in1=o, op0=ALU.mult, op1=ALU.add)
                ins.then_inc(used, 1)
                dve.wait_ge(used, c + 2)
                fin.after(nc.vector.tensor_tensor(z[:, :, :], z[:, :, :], ys[slot][:, :, :], ALU.add))
                dve.wait_ge(freed, c + 1)
                fin.after(finish(nc, B, norm, dve, fin, roots, ys[slot], z, z, result[slot]))
                dve.sem_inc(done, 1)
            over_chunks(dve, body, [(fin, each), (roots, 3)])

        @block.tensor
        def _(pe):
            def body(c, slot, last):
                pe.wait_ge(fixed, c + 2)
                for g, o in enumerate(bank_rows(ps, 0)):
                    ins = nc.tensor.transpose(o, full[slot][:, g, 0:D], B["ident"][:, :])
                ins.then_inc(turned, 1)
                pe.wait_ge(copied, c + 1)
                pe.wait_ge(used, c + 1)
                for g, o in enumerate(bank_rows(ps, 2)):
                    ins = nc.tensor.matmul(o, flipped[:, g * D:g * D + D], B["m2s"][:, :], start=True, stop=True)
                ins.then_inc(product, 1)
            over_chunks(pe, body)

        @block.scalar
        def _(act):
            roots = Tally()

            def rows_of(c, before):
                act.wait_ge(turned, c + 2)
                act.wait_ge(product, before)
                nc.scalar.activation(flipped[:, 0:4 * D], ps[0][:, 0:4 * D], ACT.Copy)
                nc.scalar.activation(flipped[:, 4 * D:G * D], ps[1][:, 0:3 * D], ACT.Copy).then_inc(copied, 1)
            rows_of(0, 0)

            def body(c, slot, last):
                act.wait_ge(asked, c + 1)
                nc.scalar.activation(z[:, :, :], z[:, :, :], ACT.Relu, scale=-1.0).then_inc(active, 1)
                norm.act(act, roots, B["eps"])
                norm.act(act, roots, B["eps"])
                norm.act(act, roots, B["eps"])
                if not last:
                    rows_of(c + 1, c + 1)
            over_chunks(act, body, [(roots, 3)])

        @block.sync
        def _(sp):
            table = B["x_dst"].rearrange("(p t) d -> p t d", t=T)

            def body(c, slot, last):
                sp.wait_ge(x_free, c + 1)
                sp.dma_start(xs[slot][:, :, :], table[:, bass.ds(c * G, G), :]).then_inc(x_in[slot], 16)
            over_chunks(sp, body)

        @block.gpsimd
        def _(gp):
            def gather(c):
                for g in range(G):
                    if c >= 1:
                        gp.wait_ge(y_in[g], 16 * c)
                    t = c * G + g
                    gp.indirect_dma_start(out=ys[c % 2][:, g, :], out_offset=None, in_=B["mixed"],
                                          in_offset=bass.IndirectOffsetOnAxis(ap=B["dst_start_i"][:, t:t + 1], axis=0))\
                      .then_inc(y_in[g], 16)
            gather(0)
            for c in range(C):
                if c + 1 < C:
                    if c >= 1:
                        gp.wait_ge(done, c)
                    gather(c + 1)
                if c:
                    scattered_chunk(gp, scattered, freed, c - 1)
                scatter_chunk(gp, B, "d_scatter", result, done, scattered, freed, c)
            scattered_chunk(gp, scattered, freed, C - 1)


_INS = ['x', 'src', 'dst', 'edge_attr_3', 'L0_gnn_W1', 'L0_gnn_att1', 'L0_gnn_b1', 'L0_gnn_W2', 'L0_gnn_att2',
        'L0_gnn_b2', 'L0_gnn_prelu_a', 'L1_gnn_W1', 'L1_gnn_b1', 'L1_gnn_W2', 'L1_gnn_b2', 'L1_gnn_gamma', 'L1_gnn_beta']


def kernel(**inputs):
    import numpy as _np
    import concourse.bacc as _bacc
    from concourse import mybir as _mybir
    from concourse.bass_utils import run_bass_kernel_spmd as _run

    nc = _bacc.Bacc("TRN2", target_bir_lowering=False, num_devices=1)
    arrays, args = {}, []
    for name in _INS:
        a = _np.ascontiguousarray(inputs[name])
        if a.ndim == 0:
            a = a.reshape(1)
        arrays[f"in_{name}"] = a
        args.append(nc.dram_tensor(f"in_{name}", a.shape, _mybir.dt.from_np(a.dtype), kind="ExternalInput").ap())
    out = nc.dram_tensor("out_rows", (N, D), _mybir.dt.float32, kind="ExternalOutput").ap()
    program(nc, *args, out)
    r = _run(nc, [arrays], core_ids=[0])
    return r.results[0]["out_rows"]
```

```python
import concourse.bass as bass
import concourse.mybir as mybir
from contextlib import ExitStack

F32 = mybir.dt.float32
F16 = mybir.dt.float16
I32 = mybir.dt.int32
ALU = mybir.AluOpType
ACT = mybir.ActivationFunctionType
AX = mybir.AxisListType

P = 128
N = 100000
D = 128
E = 25000
T = 196
EP = P * T
LO = 128
HI = 782
HH = HI // 2
PAD_KEY = HI * LO - 1
ABSENT = EP
ROWS = EP + P
W = 132
EPS = 1e-5
LAST = P - 1
LEFT = E - LAST * T
HUGE = 1.0e38
PARTS = 2
PT = T // PARTS
DVE_END, POOL_END = 20, 50
G = 7
C = T // G
DP = 125
DG = 10
DC = N // (DP * DG)
BARE_CHUNKS = {"b": 16, "n0": 16, "c1": 32, "n1": 16}


class Tally:

    def __init__(self, n=0):
        self.n, self.base, self.start = n, 0, 0

    def next(self, by=1):
        self.n += by
        return self.base + self.n

    def loop(self, turn, each):
        self.start = self.base + self.n
        self.base, self.n = turn * each + self.start, 0

    def end(self, turns, each):
        assert self.n == each, (self.n, each)
        self.base, self.n = self.start + turns * each, 0


class Finished(Tally):

    def __init__(self, eng, sem, n=0):
        Tally.__init__(self, n)
        self.eng, self.sem = eng, sem

    def after(self, ins):
        ins.then_inc(self.sem, 1)
        self.eng.wait_ge(self.sem, self.next())


def over_chunks(eng, body, tallies=()):
    turns = C // 2 - 1
    with eng.Fori(0, turns, 1) as i:
        for tally, each in tallies:
            tally.loop(i, 2 * each)
        body(i * 2, 0, False)
        body(i * 2 + 1, 1, False)
    for tally, each in tallies:
        tally.end(turns, 2 * each)
    body(C - 2, 0, False)
    body(C - 1, 1, True)


def turns(eng, n, depth, body, tallies=()):
    warm = depth + depth % 2

    def live(c):
        return [0 <= c - k < n for k in range(depth + 1)]
    for c in range(warm):
        body(c, c // 2, c % 2, live(c))
    pairs = (n - warm) // 2
    with eng.Fori(0, pairs, 1) as i:
        for tally, each in tallies:
            tally.loop(i, 2 * each)
        for slot in range(2):
            body(i * 2 + (warm + slot), i + warm // 2, slot, [True] * (depth + 1))
    for tally, each in tallies:
        tally.end(pairs, 2 * each)
    for c in range(n, n + depth):
        body(c, c // 2, c % 2, live(c))


def wait(eng, sem, value):
    if not isinstance(value, int) or value > 0:
        eng.wait_ge(sem, value)


def squares(nc, fin, rows, less_mean, unused, total):
    for g, place in enumerate(unused):
        ins = nc.scalar.activation(place, rows[:, g, :], ACT.Square, bias=less_mean[:, g:g + 1],
                                   accum_out=total[:, g:g + 1])
    fin.after(ins)


def semaphore(nc, ctx, name):
    handle = nc.alloc_semaphore(name)
    ctx.callback(nc.clear_and_free_semaphores, [handle])
    return handle


def phase(nc):
    ctx = ExitStack()
    ctx.callback(nc.all_engine_barrier, sem_only=True)
    return ctx


def row(ap):
    return ap.rearrange("p a n -> p (a n)")


def program(nc, x, src, dst, edge_attr, w1, att1, b1, w2, att2, b2, prelu_a,
            m1, mb1, m2, mb2, gamma, beta, out):
    ctx = ExitStack()
    with ctx:
        def sb(name, shape, dt=F32):
            return ctx.enter_context(nc.sbuf_tensor(name, shape, dt))

        def dram(name, shape, dt=F32):
            return nc.dram_tensor(name, shape, dt, kind="Internal").ap()

        big = sb("big", [P, T + 1, W])
        psum = ctx.enter_context(nc.psum_tensor("psum", [P, 8, 512], F32))
        ps = [psum[:, n, :] for n in range(8)]
        pairs = [psum[:, n:n + 2, 0:HH] for n in range(7)]
        ident = sb("ident", [P, P])
        ident16 = sb("ident16", [P, P], F16)
        ones16 = sb("ones16", [P, P], F16)
        ones = sb("ones", [P, P])
        before = sb("before", [P, P])
        later = sb("later", [P, P])
        iota_p = sb("iota_p", [P, 1])
        place = sb("place", [P, T])
        eps = sb("eps", [P, 1])
        eps_sq = sb("eps_sq", [P, 1])
        beta_mean = sb("beta_mean", [P, 1])
        alpha = sb("alpha", [P, 1])
        drop = sb("drop", [P, 1])
        w1s, w2s, m1s, m2s = (sb(n, [P, D]) for n in ("w1s", "w2s", "m1s", "m2s"))
        edge_w = sb("edge_w", [4 * G, G * D])
        rows_ = {n: sb("row_" + n, [P, D]) for n in ("b1", "b2", "mb2", "gamma", "beta", "wi1", "wj1", "wi2", "wj2")}
        aj_absent = sb("aj_absent", [P, 1])
        src_key, dst_key = sb("src_key", [P, T]), sb("dst_key", [P, T])
        src_gather, dst_gather = sb("src_gather", [P, T], I32), sb("dst_gather", [P, T], I32)
        src_start, dst_start = sb("src_start", [P, T]), sb("dst_start", [P, T])
        src_start_i, dst_start_i = sb("src_start_i", [P, T], I32), sb("dst_start_i", [P, T], I32)
        src_place, src_place_i = sb("src_place", [P, T]), sb("src_place_i", [P, T], I32)
        orders = {}
        for o in ("d", "s"):
            orders[o] = {n: sb(f"{o}_{n}", [P, T]) for n in
                         ("prev", "new", "same", "next", "runs", "tail", "fix", "start")}
            orders[o].update({n: sb(f"{o}_{n}", [P, P]) for n in ("from_before", "from_later", "sel_before", "sel_later")})
            orders[o].update({n: sb(f"{o}_{n}", [P, 1]) for n in ("has_new",)})
            orders[o]["extra"] = sb(f"{o}_extra", [P, W])
        s_key = sb("s_key", [P, T])
        s_gather = sb("s_gather", [P, T], I32)
        s_scatter = sb("s_scatter", [P, T], I32)
        s_dstart_i = sb("s_dstart_i", [P, T], I32)
        d_scatter = sb("d_scatter", [P, T], I32)
        ai, aj, top, ex, coef = (sb(n, [P, T]) for n in ("ai", "aj", "top", "ex", "coef"))
        tmp = [sb(f"tmp{n}", [P, T]) for n in range(4)]
        ai2_s = sb("ai2_s", [P, T])
        absent = sb("absent", [P, T])

        x_dst = dram("x_dst", [EP, D])
        record = dram("record", [EP + 1, 4])
        sums = [dram(f"sums{n}", [EP, W]) for n in range(2)]
        hidden = dram("hidden", [ROWS, W])
        hidden_aj = dram("hidden_aj", [ROWS, 1])
        mixed = dram("mixed", [ROWS, D])
        mixed_m = dram("mixed_m", [ROWS, D])

        B = dict(locals())
        setup(nc, B)
        counting(nc, B)
        order_flags(nc, B, "d")
        conv_edges(nc, B, 0)
        by_source(nc, B)
        order_flags(nc, B, "s")
        conv_nodes(nc, B, 0)
        conv_edges(nc, B, 1)
        conv_nodes(nc, B, 1)
        edge_network(nc, B)


def shifted_loads(eng, dest, source, sem, offset=0):
    flat = source
    eng.dma_start(dest[0:1, 1:T], flat[0:T - 1].rearrange("(p t) -> p t", p=1)).then_inc(sem, 16)
    eng.dma_start(dest[1:LAST, :], flat[T - 1:LAST * T - 1].rearrange("(p t) -> p t", t=T)).then_inc(sem, 16)
    eng.dma_start(dest[LAST:P, 0:LEFT + 1], flat[LAST * T - 1:E].rearrange("(p t) -> p t", p=1)).then_inc(sem, 16)


def setup(nc, B):
    with phase(nc) as ctx:
        def sem(name):
            return semaphore(nc, ctx, name)
        key_i = [ctx.enter_context(nc.sbuf_tensor(f"key_i{n}", [P, T], I32)) for n in range(2)]
        prev_i = ctx.enter_context(nc.sbuf_tensor("prev_i", [P, T], I32))
        wt = [ctx.enter_context(nc.sbuf_tensor(f"wt{n}", [P, P], F32)) for n in range(2)]
        att_bc = [ctx.enter_context(nc.sbuf_tensor(f"att_bc{n}", [P, P], F32)) for n in range(4)]
        att_col = ctx.enter_context(nc.sbuf_tensor("att_col", [P, 4], F32))
        hid_row = ctx.enter_context(nc.sbuf_tensor("hid_row", [P, W], F32))
        junk = ctx.enter_context(nc.sbuf_tensor("junk", [P, D], F32))
        more_junk = ctx.enter_context(nc.sbuf_tensor("junk2", [P, D], F32))
        zero_row = ctx.enter_context(nc.sbuf_tensor("zero_row", [P, D], F32))
        place_i = ctx.enter_context(nc.sbuf_tensor("place_i", [P, T], I32))
        filled, loaded, made, own = sem("filled"), sem("loaded"), sem("made"), sem("own")
        weights_up, turned, copied, rows_up, absent_row, stored = (
            sem(n) for n in ("weights_up", "turned", "copied", "rows_up", "absent_row", "stored"))
        pool_own = sem("pool_own")
        block = ctx.enter_context(nc.Block())
        rows_, ps = B["rows_"], B["ps"]

        @block.sync
        def _(sp):
            n = 0
            for dest, source in ((B["w1s"], B["w1"]), (B["w2s"], B["w2"]), (B["m1s"], B["m1"][0:D, :]), (B["m2s"], B["m2"])):
                sp.dma_start(dest[:, :], source).then_inc(weights_up, 16)
            for n, att in enumerate((B["att1"], B["att2"])):
                sp.dma_start(att_col[:, 2 * n:2 * n + 2], att.rearrange("(a p) -> p a", p=P),
                             allow_slow_non_contiguous=True).then_inc(weights_up, 16)
            for name in ("b1", "b2", "mb2", "gamma", "beta"):
                sp.dma_start(rows_[name][:, :], B[name].rearrange("(a n) -> a n", a=1).to_broadcast([P, D]))\
                  .then_inc(weights_up, 16)
            sp.dma_start(B["alpha"][:, :], B["prelu_a"].rearrange("(a n) -> a n", a=1).to_broadcast([P, 1]))\
              .then_inc(weights_up, 16)
            sp.wait_ge(filled, 3)
            for k, source in ((key_i[0], B["src"]), (key_i[1], B["dst"])):
                sp.dma_start(k[0:LAST, :], source[0:LAST * T].rearrange("(p t) -> p t", t=T)).then_inc(loaded, 16)
                sp.dma_start(k[LAST:P, 0:LEFT], source[LAST * T:E].rearrange("(p t) -> p t", p=1)).then_inc(loaded, 16)
            shifted_loads(sp, prev_i, B["dst"], loaded)
            sp.wait_ge(absent_row, 2)
            sp.dma_start(B["hidden"][EP:ROWS, :], hid_row[:, :]).then_inc(stored, 16)
            sp.dma_start(B["hidden_aj"][EP:ROWS, :], B["aj_absent"][:, :]).then_inc(stored, 16)
            sp.dma_start(B["mixed"][EP:ROWS, :], zero_row[:, :]).then_inc(stored, 16)
            sp.dma_start(B["mixed_m"][EP:ROWS, :], zero_row[:, :]).then_inc(stored, 16)
            sp.wait_ge(stored, 64)

        @block.gpsimd
        def _(gp):
            gp.memset(B["ident"][:, :], 0.0).then_inc(pool_own, 1)
            gp.memset(B["before"][:, :], 1.0).then_inc(pool_own, 1)
            gp.memset(B["later"][:, :], 1.0).then_inc(pool_own, 1)
            gp.wait_ge(pool_own, 3)
            gp.affine_select(out=B["ident"][:, :], in_=B["ident"][:, :], compare_op=ALU.not_equal, fill=1.0,
                             base=0, pattern=[[-1, P]], channel_multiplier=1).then_inc(made, 1)
            gp.affine_select(out=B["before"][:, :], in_=B["before"][:, :], compare_op=ALU.is_gt, fill=0.0,
                             base=0, pattern=[[1, P]], channel_multiplier=-1).then_inc(made, 1)
            gp.affine_select(out=B["later"][:, :], in_=B["later"][:, :], compare_op=ALU.is_gt, fill=0.0,
                             base=0, pattern=[[-1, P]], channel_multiplier=1).then_inc(made, 1)
            gp.iota(place_i[:, :], pattern=[[1, T]], base=0, channel_multiplier=T).then_inc(made, 1)

        @block.vector
        def _(dve):
            fin = Finished(dve, own)
            nc.vector.memset(key_i[0][:, :], PAD_KEY).then_inc(filled, 1)
            nc.vector.memset(key_i[1][:, :], PAD_KEY).then_inc(filled, 1)
            nc.vector.memset(prev_i[:, :], PAD_KEY).then_inc(filled, 1)
            nc.vector.memset(B["ones16"][:, :], 1.0)
            nc.vector.memset(B["ones"][:, :], 1.0)
            nc.vector.memset(B["eps"][:, :], EPS)
            nc.vector.memset(B["eps_sq"][:, :], EPS * EPS)
            nc.vector.memset(hid_row[:, :], 0.0)
            nc.vector.memset(zero_row[:, :], 0.0)
            fin.after(nc.vector.memset(B["big"][:, :, :], 0.0))
            dve.wait_ge(made, 4)
            nc.vector.tensor_copy(B["ident16"][:, :], B["ident"][:, :])
            nc.vector.tensor_copy(B["place"][:, :], place_i[:, :])
            dve.wait_ge(loaded, 7 * 16)
            nc.vector.tensor_copy(B["src_key"][:, :], key_i[0][:, :])
            nc.vector.tensor_copy(B["dst_key"][:, :], key_i[1][:, :])
            fin.after(nc.vector.tensor_copy(B["orders"]["d"]["prev"][:, :], prev_i[:, :]))
            fin.after(nc.vector.memset(B["orders"]["d"]["prev"][0:1, 0:1], -1.0))
            nc.vector.tensor_scalar(B["src_gather"][:, :], B["src_key"][:, :], float(N - 1), None, ALU.min)
            nc.vector.tensor_scalar(B["dst_gather"][:, :], B["dst_key"][:, :], float(N - 1), None, ALU.min)
            dve.wait_ge(weights_up, 12 * 16)
            for n in range(4):
                fin.after(nc.vector.tensor_scalar(att_bc[n][:, :], B["ones"][:, :], att_col[:, n:n + 1], None, ALU.mult))
            dve.wait_ge(turned, 2)
            nc.vector.tensor_copy(wt[0][:, :], ps[0][:, 0:P]).then_inc(copied, 1)
            nc.vector.tensor_copy(wt[1][:, :], ps[1][:, 0:P]).then_inc(copied, 1)
            dve.wait_ge(rows_up, 1)
            for n, name in enumerate(("wi1", "wj1", "wi2", "wj2")):
                nc.vector.tensor_copy(rows_[name][:, :], ps[2][:, n * P:n * P + P])
            fin.after(nc.vector.tensor_scalar(B["drop"][:, :], B["alpha"][:, :], -1.0, 1.0, ALU.mult, ALU.add))
            fin.after(nc.vector.tensor_scalar(junk[:, :], rows_["beta"][:, :], 1.0 / D, 0.0, ALU.mult, ALU.add,
                                              accum_out=B["beta_mean"][:, :]))
            fin.after(nc.vector.tensor_scalar(junk[:, :], rows_["b1"][:, :], -1.0, 0.0, ALU.mult, ALU.max))
            fin.after(nc.vector.scalar_tensor_tensor(out=hid_row[:, 0:D], in0=junk[:, :], scalar=B["drop"][:, 0:1],
                                                     in1=rows_["b1"][:, :], op0=ALU.mult, op1=ALU.add))
            fin.after(nc.vector.scalar_tensor_tensor(
                out=junk[:, :], in0=hid_row[:, 0:D], scalar=1.0, in1=rows_["wj2"][:, :],
                op0=ALU.mult, op1=ALU.mult, accum_out=B["aj_absent"][:, :]))
            nc.vector.scalar_tensor_tensor(
                out=more_junk[:, :], in0=hid_row[:, 0:D], scalar=1.0, in1=rows_["wi2"][:, :],
                op0=ALU.mult, op1=ALU.mult, accum_out=hid_row[:, D:D + 1]).then_inc(absent_row, 2)

        @block.tensor
        def _(pe):
            pe.wait_ge(weights_up, 12 * 16)
            pe.wait_ge(made, 1)
            for n, w in enumerate((B["w1s"], B["w2s"])):
                nc.tensor.transpose(ps[n][:, 0:P], w[:, :], B["ident"][:, :]).then_inc(turned, 1)
            pe.wait_ge(copied, 2)
            pe.wait_ge(own, 7)
            for n in range(4):
                last = nc.tensor.matmul(ps[2][:, n * P:n * P + P], att_bc[n][:, :], wt[n // 2][:, :],
                                        start=True, stop=True)
            last.then_inc(rows_up, 1)


def halves(bank0, bank1):
    return (bank0[:, 0:HH], bank1[:, 0:HH])


def counting(nc, B):
    with phase(nc) as ctx:
        def sb(name, shape, dt=F32):
            return ctx.enter_context(nc.sbuf_tensor(name, shape, dt))

        def sem(name):
            return semaphore(nc, ctx, name)
        ps = B["ps"]
        digits_i = sb("digits_i", [P, T], I32)
        lo = {k: sb(f"lo_{k}", [P, T + 4]) for k in "sd"}
        hi = {k: sb(f"hi_{k}", [P, T + 4]) for k in "sd"}
        iota_i = sb("iota_i", [P, HI], I32)
        iota16 = sb("iota16", [P, HI], F16)
        oh_lo = [sb(f"oh_lo{n}", [P, LO], F16) for n in range(2)]
        oh_hi = [sb(f"oh_hi{n}", [P, HI], F16) for n in range(2)]
        count = sb("count", [P, HI])
        upto = sb("upto", [P, HI])
        start = sb("start", [P, HI])
        ones_hi = sb("ones_hi", [P, HI])
        start_i = sb("start_i", [P, HI], I32)
        start_lo_i = sb("start_lo_i", [P, HI], I32)
        start_hi16, start_lo16 = sb("start_hi16", [P, HI], F16), sb("start_lo16", [P, HI], F16)
        offset = sb("offset", [P, 1])
        iota_pi = sb("iota_pi", [P, 1], I32)
        diag = [sb(f"diag{n}", [P, P], F16) for n in range(2)]
        lo_hot16 = [sb(f"lo_hot16_{n}", [P, P], F16) for n in range(2)]
        lo_hot = [sb(f"lo_hot{n}", [P, P]) for n in range(2)]
        twins = [sb(f"twins{n}", [P, P], F16) for n in range(2)]
        so_far = [sb(f"so_far{n}", [P, HI]) for n in range(2)]
        earlier = sb("earlier", [P, T])
        junk = [sb(f"junk_c{n}", [P, HI], F16) for n in range(2)]
        zero16 = sb("zero16", [P, HH], F16)
        ring = [sb(f"x_ring{n}", [P, D]) for n in range(4)]
        place_i = sb("place_si", [P, T], I32)

        with phase(nc) as c2:
            made, own, ready, used, summed, ranked = (semaphore(nc, c2, n) for n in
                                                      ("c_made", "c_own", "c_ready", "c_used", "c_summed", "c_ranked"))
            block = c2.enter_context(nc.Block())

            @block.gpsimd
            def _(gp):
                gp.iota(iota_i[:, :], pattern=[[1, HI]], base=0, channel_multiplier=0).then_inc(made, 1)
                gp.iota(iota_pi[:, :], pattern=[[1, 1]], base=0, channel_multiplier=1).then_inc(made, 1)

            @block.vector
            def _(dve):
                fin = Finished(dve, own)
                dve.wait_ge(made, 2)
                nc.vector.tensor_copy(iota16[:, :], iota_i[:, :])
                nc.vector.tensor_copy(B["iota_p"][:, :], iota_pi[:, :])
                nc.vector.memset(ones_hi[:, :], 1.0)
                nc.vector.memset(zero16[:, :], 0.0)
                for k, key in (("s", B["src_key"]), ("d", B["dst_key"])):
                    nc.vector.memset(lo[k][:, T:T + 4], 0.0)
                    nc.vector.memset(hi[k][:, T:T + 4], 0.0)
                    fin.after(nc.vector.tensor_copy(digits_i[:, :], key[:, :]))
                    fin.after(nc.vector.tensor_single_scalar(place_i[:, :], digits_i[:, :], LO - 1, op=ALU.bitwise_and))
                    fin.after(nc.vector.tensor_copy(lo[k][:, 0:T], place_i[:, :]))
                    fin.after(nc.vector.tensor_single_scalar(place_i[:, :], digits_i[:, :], 7, op=ALU.logical_shift_right))
                    fin.after(nc.vector.tensor_copy(hi[k][:, 0:T], place_i[:, :]))

                def hot(t, slot):
                    dve.wait_ge(used, t + 1)
                    nc.vector.tensor_scalar(oh_lo[slot][:, :], iota16[:, 0:LO], lo["s"][:, bass.ds(t, 1)], None, ALU.is_equal)
                    nc.vector.tensor_scalar(oh_hi[slot][:, :], iota16[:, :], hi["s"][:, bass.ds(t, 1)], None, ALU.is_equal)\
                      .then_inc(ready, 1)
                with dve.Fori(0, T // 4, 1) as i:
                    for j in range(4):
                        hot(i * 4 + j, j % 2)
                dve.wait_ge(summed, 1)
                for h, half in enumerate(halves(ps[0], ps[1])):
                    fin.after(nc.vector.tensor_copy(count[:, h * HH:h * HH + HH], half))
                fin.after(nc.vector.tensor_tensor_scan(upto[:, :], ones_hi[:, :], count[:, :], 0.0, ALU.mult, ALU.add))
                dve.wait_ge(ranked, 1)
                fin.after(nc.vector.tensor_copy(offset[:, :], ps[2][:, 0:1]))
                fin.after(nc.vector.scalar_tensor_tensor(out=start[:, :], in0=upto[:, :], scalar=offset[:, 0:1],
                                                         in1=count[:, :], op0=ALU.add, op1=ALU.subtract))
                fin.after(nc.vector.tensor_scalar(upto[:, :], count[:, :], 0.0, None, ALU.is_gt))
                fin.after(nc.vector.scalar_tensor_tensor(out=start[:, :], in0=start[:, :], scalar=-float(ABSENT),
                                                         in1=upto[:, :], op0=ALU.add, op1=ALU.mult))
                fin.after(nc.vector.tensor_scalar(start[:, :], start[:, :], float(ABSENT), None, ALU.add))
                fin.after(nc.vector.tensor_copy(start_i[:, :], start[:, :]))
                fin.after(nc.vector.tensor_single_scalar(start_lo_i[:, :], start_i[:, :], 255, op=ALU.bitwise_and))
                fin.after(nc.vector.tensor_copy(upto[:, :], start_lo_i[:, :]))
                fin.after(nc.vector.tensor_copy(start_lo16[:, :], upto[:, :]))
                fin.after(nc.vector.tensor_tensor(start_hi16[:, :], start[:, :], upto[:, :], ALU.subtract))

            @block.tensor
            def _(pe):
                pe.sem_inc(used, 2)
                acc = halves(ps[0], ps[1])
                pe.wait_ge(own, 1)
                for h in range(2):
                    nc.tensor.matmul(acc[h], zero16[:, 0:P], zero16[:, :], start=True, stop=False)
                with pe.Fori(0, T // 4, 1) as i:
                    for j in range(4):
                        pe.wait_ge(ready, i * 4 + j + 1)
                        for h in range(2):
                            last = nc.tensor.matmul(acc[h], oh_lo[j % 2][:, :], oh_hi[j % 2][:, h * HH:h * HH + HH],
                                                    start=False, stop=False)
                        last.then_inc(used, 1)
                for h in range(2):
                    last = nc.tensor.matmul(acc[h], zero16[:, 0:P], zero16[:, :], start=False, stop=True)
                last.then_inc(summed, 1)
                pe.wait_ge(own, 13)
                nc.tensor.matmul(ps[2][:, 0:1], B["before"][:, :], upto[:, HI - 1:HI], start=True, stop=True)\
                  .then_inc(ranked, 1)

        with phase(nc) as c2:
            def sem2(name):
                return semaphore(nc, c2, name)
            own, diag_up, lo_up, hot_up, earlier_up, looked, taken, done = (
                sem2(n) for n in ("r_own", "r_diag", "r_lo", "r_hot", "r_snap", "r_looked", "r_taken", "r_done"))
            big_in = [sem2(f"r_big{n}") for n in range(4)]
            ring_in = [sem2(f"r_in{n}") for n in range(4)]
            ring_out = [sem2(f"r_out{n}") for n in range(4)]
            block = c2.enter_context(nc.Block())

            @block.gpsimd
            def _(gp):
                for t in range(T):
                    if t >= 4:
                        gp.wait_ge(big_in[t % 4], 16 * (t // 4))
                    gp.indirect_dma_start(out=B["big"][:, t, 0:D], out_offset=None, in_=B["x"],
                                          in_offset=bass.IndirectOffsetOnAxis(ap=B["src_gather"][:, t:t + 1], axis=0))\
                      .then_inc(big_in[t % 4], 16)
                for t in range(T):
                    if t >= 4:
                        gp.wait_ge(ring_out[t % 4], 16 * (t // 4))
                    gp.indirect_dma_start(out=ring[t % 4][:, :], out_offset=None, in_=B["x"],
                                          in_offset=bass.IndirectOffsetOnAxis(ap=B["dst_gather"][:, t:t + 1], axis=0))\
                      .then_inc(ring_in[t % 4], 16)
                for n in range(4):
                    gp.wait_ge(big_in[n], 16 * (T // 4))

            @block.sync
            def _(sp):
                table = B["x_dst"].rearrange("(p t) d -> p t d", t=T)
                with sp.Fori(0, T // 4, 1) as i:
                    for j in range(4):
                        sp.wait_ge(ring_in[j], i * 16 + 16)
                        sp.dma_start(table[:, bass.ds(i * 4 + j, 1), :], ring[j][:, :].rearrange("p (a d) -> p a d", a=1))\
                          .then_inc(ring_out[j], 16)
                for j in range(4):
                    sp.wait_ge(ring_out[j], 16 * (T // 4))

            @block.scalar
            def _(act):
                def digit(t, slot):
                    act.wait_ge(lo_up, t)
                    act.wait_ge(own, 1)
                    nc.scalar.activation(diag[slot][:, :], B["ident16"][:, :], ACT.Copy,
                                         scale=lo["s"][:, bass.ds(t, 1)]).then_inc(diag_up, 1)

                digit(0, 0)
                with act.Fori(0, T // 4, 1) as i:
                    for j in range(4):
                        t = i * 4 + j
                        digit(t + 1, (j + 1) % 2)
                        act.wait_ge(done, t + 1)
                        for h, half in enumerate(halves(ps[0], ps[1])):
                            last = nc.scalar.activation(so_far[j % 2][:, h * HH:h * HH + HH], half, ACT.Copy)
                        last.then_inc(earlier_up, 1)

            @block.tensor
            def _(pe):
                acc = halves(ps[0], ps[1])
                at_start = halves(ps[2], ps[3])
                at_count = halves(ps[4], ps[5])
                pe.wait_ge(own, 1)
                for h in range(2):
                    last = nc.tensor.matmul(acc[h], zero16[:, 0:P], zero16[:, :], start=True, stop=True)
                last.then_inc(done, 1)

                def low_row(t, slot):
                    pe.wait_ge(diag_up, t + 1)
                    pe.wait_ge(hot_up, t)
                    nc.tensor.matmul(ps[6 + slot][:, 0:P], B["ones16"][:, :], diag[slot][:, :], start=True, stop=True)\
                      .then_inc(lo_up, 1)

                low_row(0, 0)
                with pe.Fori(0, T // 4, 1) as i:
                    for j in range(4):
                        t, s = i * 4 + j, j % 2
                        low_row(t + 1, 1 - s)
                        pe.wait_ge(hot_up, t + 2)
                        pe.wait_ge(taken, t + 1)
                        for h in range(2):
                            nc.tensor.matmul(at_start[h], lo_hot16[s][:, :], start_hi16[:, h * HH:h * HH + HH], start=True, stop=False)
                            nc.tensor.matmul(at_start[h], lo_hot16[s][:, :], start_lo16[:, h * HH:h * HH + HH], start=False, stop=True)
                        pe.wait_ge(earlier_up, t + 1)
                        for h in range(2):
                            nc.tensor.matmul(at_count[h], lo_hot[s][:, :], so_far[s][:, h * HH:h * HH + HH], start=True, stop=False)
                            last = nc.tensor.matmul(at_count[h], twins[s][:, :], oh_hi[s][:, h * HH:h * HH + HH], start=False, stop=True)
                        last.then_inc(looked, 1)
                        for h in range(2):
                            last = nc.tensor.matmul(acc[h], oh_lo[s][:, :], oh_hi[s][:, h * HH:h * HH + HH],
                                                    start=False, stop=True, skip_group_check=True)
                        last.then_inc(done, 1)

            @block.vector
            def _(dve):
                dve.sem_inc(lo_up, 1)
                dve.sem_inc(taken, 1)
                dve.sem_inc(hot_up, 1)
                dve.sem_inc(own, 1)

                def hot(t, slot):
                    dve.wait_ge(lo_up, t + 2)
                    dve.wait_ge(done, t)
                    col = bass.ds(t, 1)
                    nc.vector.tensor_scalar(lo_hot16[slot][:, :], ps[6 + slot][:, 0:P], B["iota_p"][:, 0:1], None, ALU.is_equal)
                    nc.vector.tensor_scalar(lo_hot[slot][:, :], ps[6 + slot][:, 0:P], B["iota_p"][:, 0:1], None, ALU.is_equal)
                    nc.vector.scalar_tensor_tensor(out=twins[slot][:, :], in0=ps[6 + slot][:, 0:P], scalar=lo["s"][:, col],
                                                   in1=B["before"][:, :], op0=ALU.is_equal, op1=ALU.mult)
                    nc.vector.tensor_scalar(oh_lo[slot][:, :], iota16[:, 0:LO], lo["s"][:, col], None, ALU.is_equal)
                    nc.vector.tensor_scalar(oh_hi[slot][:, :], iota16[:, :], hi["s"][:, col], None, ALU.is_equal)\
                      .then_inc(hot_up, 1)

                hot(0, 0)
                with dve.Fori(0, T // 4, 1) as i:
                    for j in range(4):
                        t, s = i * 4 + j, j % 2
                        dve.wait_ge(taken, t + 1)
                        hot(t + 1, 1 - s)
                        dve.wait_ge(looked, t + 1)
                        hot3 = oh_hi[s][:, :].rearrange("p (h k) -> p h k", h=2)
                        dve.wait_ge(hot_up, t + 2)
                        for n, (target, bank) in enumerate(((B["src_start"], 2), (earlier, 4))):
                            pair = B["pairs"][bank]
                            last = nc.vector.scalar_tensor_tensor(
                                out=junk[n][:, :].rearrange("p (h k) -> p h k", h=2), in0=pair, scalar=1.0, in1=hot3,
                                op0=ALU.mult, op1=ALU.mult, accum_out=target[:, bass.ds(t, 1)])
                        last.then_inc(taken, 1)

        with phase(nc) as c2:
            def sem3(name):
                return semaphore(nc, c2, name)
            own, diag_up, lo_up, hot_up, looked, taken = (
                sem3(n) for n in ("q_own", "q_diag", "q_lo", "q_hot", "q_looked", "q_taken"))
            block = c2.enter_context(nc.Block())

            @block.scalar
            def _(act):
                def digit(t, slot):
                    act.wait_ge(lo_up, t)
                    act.wait_ge(own, 1)
                    nc.scalar.activation(diag[slot][:, :], B["ident16"][:, :], ACT.Copy,
                                         scale=lo["d"][:, bass.ds(t, 1)]).then_inc(diag_up, 1)
                digit(0, 0)
                with act.Fori(0, T // 4, 1) as i:
                    for j in range(4):
                        digit(i * 4 + j + 1, (j + 1) % 2)

            @block.tensor
            def _(pe):
                def low_row(t, slot):
                    pe.wait_ge(diag_up, t + 1)
                    pe.wait_ge(hot_up, t)
                    nc.tensor.matmul(ps[6 + slot][:, 0:P], B["ones16"][:, :], diag[slot][:, :], start=True, stop=True)\
                      .then_inc(lo_up, 1)
                low_row(0, 0)
                with pe.Fori(0, T // 4, 1) as i:
                    for j in range(4):
                        t, s = i * 4 + j, j % 2
                        low_row(t + 1, 1 - s)
                        pe.wait_ge(hot_up, t + 2)
                        pe.wait_ge(taken, t)
                        at_start = halves(ps[2 * s], ps[2 * s + 1])
                        for h in range(2):
                            nc.tensor.matmul(at_start[h], lo_hot16[s][:, :], start_hi16[:, h * HH:h * HH + HH], start=True, stop=False)
                            last = nc.tensor.matmul(at_start[h], lo_hot16[s][:, :], start_lo16[:, h * HH:h * HH + HH], start=False, stop=True)
                        last.then_inc(looked, 1)

            @block.vector
            def _(dve):
                dve.sem_inc(lo_up, 1)
                dve.sem_inc(looked, 1)
                dve.sem_inc(hot_up, 1)
                dve.sem_inc(taken, 1)
                dve.sem_inc(own, 1)

                def hot(t, slot, free):
                    dve.wait_ge(lo_up, t + 2)
                    dve.wait_ge(looked, free)
                    nc.vector.tensor_scalar(lo_hot16[slot][:, :], ps[6 + slot][:, 0:P], B["iota_p"][:, 0:1], None, ALU.is_equal)
                    nc.vector.tensor_scalar(oh_hi[slot][:, :], iota16[:, :], hi["d"][:, bass.ds(t, 1)], None, ALU.is_equal)\
                      .then_inc(hot_up, 1)

                hot(0, 0, 1)
                with dve.Fori(0, T // 4, 1) as i:
                    for j in range(4):
                        t, s = i * 4 + j, j % 2
                        dve.wait_ge(taken, t + 1)
                        hot(t + 1, 1 - s, t + 1)
                        dve.wait_ge(looked, t + 2)
                        dve.wait_ge(hot_up, t + 2)
                        nc.vector.scalar_tensor_tensor(
                            out=junk[s][:, :].rearrange("p (h k) -> p h k", h=2), in0=B["pairs"][2 * s], scalar=1.0,
                            in1=oh_hi[s][:, :].rearrange("p (h k) -> p h k", h=2),
                            op0=ALU.mult, op1=ALU.mult, accum_out=B["dst_start"][:, bass.ds(t, 1)]).then_inc(taken, 1)
                fin = Finished(dve, own, 1)
                dve.wait_ge(taken, T + 1)
                fin.after(nc.vector.tensor_tensor(B["src_place"][:, :], B["src_start"][:, :], earlier[:, :], ALU.add))
                nc.vector.tensor_scalar(B["src_place_i"][:, :], B["src_place"][:, :], 1.0, None, ALU.add)
                nc.vector.tensor_copy(B["src_start_i"][:, :], B["src_start"][:, :])
                nc.vector.tensor_copy(B["dst_start_i"][:, :], B["dst_start"][:, :])


def propagate(dve, nc, B, o, fin, values, out, spare, sent, came, turn):
    q = B["orders"][o]
    fin.after(nc.vector.tensor_tensor(spare[:, :], values, q["new"][:, :], ALU.mult))
    fin.after(nc.vector.tensor_tensor_scan(out[:, :], q["same"][:, :], spare[:, :], 0.0, ALU.mult, ALU.add))
    nc.vector.tensor_tensor(spare[:, 0:1], out[:, T - 1:T], q["has_new"][:, :], ALU.mult).then_inc(sent, 1)
    dve.wait_ge(came, turn)
    fin.after(nc.vector.scalar_tensor_tensor(out=out[:, :], in0=q["runs"][:, :], scalar=B["ps"][turn][:, 0:1],
                                             in1=out[:, :], op0=ALU.mult, op1=ALU.add))


def propagate_pe(pe, nc, B, o, spare, sent, came, turn):
    pe.wait_ge(sent, turn)
    nc.tensor.matmul(B["ps"][turn][:, 0:1], B["orders"][o]["from_before"][:, :], spare[:, 0:1],
                     start=True, stop=True).then_inc(came, 1)


def order_flags(nc, B, o):
    q, ps = B["orders"][o], B["ps"]
    key = B["dst_key"] if o == "d" else B["s_key"]
    with phase(nc) as ctx:
        def sem(name):
            return semaphore(nc, ctx, name)
        own, cols_up, rows_up, sent, came = (sem(o + "_f_" + n) for n in ("own", "cols", "rows", "sent", "came"))
        diag_f = ctx.enter_context(nc.sbuf_tensor(o + "_diag_f", [P, P], F32))
        diag_l = ctx.enter_context(nc.sbuf_tensor(o + "_diag_l", [P, P], F32))
        ones_t = ctx.enter_context(nc.sbuf_tensor(o + "_ones_t", [P, T], F32))
        block = ctx.enter_context(nc.Block())
        first, last = key[:, 0:1], key[:, T - 1:T]

        @block.vector
        def _(dve):
            fin = Finished(dve, own)
            nc.vector.tensor_scalar(diag_f[:, :], B["ident"][:, :], first, None, ALU.mult)
            nc.vector.tensor_scalar(diag_l[:, :], B["ident"][:, :], last, None, ALU.mult).then_inc(cols_up, 1)
            nc.vector.memset(ones_t[:, :], 1.0)
            nc.vector.memset(q["next"][:, :], 0.0)
            nc.vector.tensor_tensor(q["same"][:, :], key[:, :], q["prev"][:, :], ALU.is_equal)
            fin.after(nc.vector.tensor_tensor(q["new"][:, :], key[:, :], q["prev"][:, :], ALU.not_equal))
            nc.vector.tensor_scalar(q["tail"][:, :], key[:, :], last, None, ALU.is_equal)
            nc.vector.tensor_copy(q["next"][:, 0:T - 1], q["same"][:, 1:T])
            fin.after(nc.vector.tensor_tensor_scan(q["runs"][:, :], q["same"][:, :], ones_t[:, :], 1.0, ALU.mult, ALU.mult))
            nc.vector.tensor_tensor(q["fix"][:, :], q["new"][:, :], q["tail"][:, :], ALU.mult)
            fin.after(nc.vector.tensor_scalar(q["has_new"][:, :], q["runs"][:, T - 1:T], -1.0, 1.0, ALU.mult, ALU.add))
            dve.wait_ge(rows_up, 1)
            for name, bank, col, side in (("from_before", 0, last, "before"), ("from_later", 1, first, "later"),
                                          ("sel_before", 1, first, "later"), ("sel_later", 0, last, "before")):
                step = nc.vector.scalar_tensor_tensor(out=q[name][:, :], in0=ps[bank][:, 0:P], scalar=col,
                                                      in1=B[side][:, :], op0=ALU.is_equal, op1=ALU.mult)
            fin.after(step)
            propagate(dve, nc, B, o, fin, B["place"][:, :], q["start"], B["tmp"][0], sent, came, 1)
            target = B["d_scatter"] if o == "d" else B["s_scatter"]
            fin.after(nc.vector.scalar_tensor_tensor(out=B["tmp"][1][:, :], in0=key[:, :], scalar=-float(PAD_KEY),
                                                     in1=q["new"][:, :], op0=ALU.add, op1=ALU.mult))
            fin.after(nc.vector.tensor_scalar(target[:, :], B["tmp"][1][:, :], float(PAD_KEY), None, ALU.add))

        @block.tensor
        def _(pe):
            pe.wait_ge(cols_up, 1)
            nc.tensor.matmul(ps[0][:, 0:P], B["ones"][:, :], diag_f[:, :], start=True, stop=True)
            nc.tensor.matmul(ps[1][:, 0:P], B["ones"][:, :], diag_l[:, :], start=True, stop=True).then_inc(rows_up, 1)
            pe.wait_ge(own, 4)
            propagate_pe(pe, nc, B, o, B["tmp"][0], sent, came, 1)


def edge_logits(dve, nc, B, fin, ai, aj, out, spare):
    fin.after(nc.vector.tensor_tensor(spare, ai, aj, ALU.add))
    fin.after(nc.vector.scalar_tensor_tensor(out=out, in0=spare, scalar=0.2, in1=spare, op0=ALU.mult, op1=ALU.max))


def running_sums(nc, B, o, scale, name):
    q, big = B["orders"][o], B["big"]
    with phase(nc) as ctx:
        def sem(n):
            return semaphore(nc, ctx, name + n)
        own, act_scaled, pool_scaled, summed, extra_up = (
            sem(n) for n in ("own", "act_scaled", "pool_scaled", "summed", "extra"))
        mask = ctx.enter_context(nc.sbuf_tensor(name + "mask", [P, PARTS, PT + 1], F32))
        block = ctx.enter_context(nc.Block())

        def scale_rows(v, part, first, last):
            a, b = part * PT + first, part * PT + last
            factor = scale[:, a:b].rearrange("p (t a) -> p t a", a=1).to_broadcast([P, b - a, D])
            return v.tensor_tensor(big[:, a:b, 0:D], big[:, a:b, 0:D], factor, ALU.mult)

        if scale is not None:
            @block.scalar
            def _(act):
                for part in reversed(range(PARTS)):
                    with act.Fori(0, (PT - POOL_END) // 4, 1) as i:
                        for j in range(4):
                            at = bass.ds(i * 4 + part * PT + POOL_END + j, 1)
                            nc.scalar.activation(row(big[:, at, 0:D]), row(big[:, at, 0:D]), ACT.Copy, scale=scale[:, at])\
                                .then_inc(act_scaled, 1)

            @block.gpsimd
            def _(gp):
                for part in reversed(range(PARTS)):
                    scale_rows(nc.gpsimd, part, DVE_END, POOL_END).then_inc(pool_scaled, 1)

        @block.vector
        def _(dve):
            fin = Finished(dve, own)
            nc.vector.memset(mask[:, :, PT], 0.0)
            fin.after(nc.vector.tensor_copy(mask[:, :, 0:PT], q["next"][:, :].rearrange("p (k t) -> p k t", t=PT)))
            for n, part in enumerate(reversed(range(PARTS))):
                if scale is not None:
                    fin.after(scale_rows(nc.vector, part, 0, DVE_END))
                    dve.wait_ge(act_scaled, (n + 1) * (PT - POOL_END))
                    dve.wait_ge(pool_scaled, n + 1)
                a = part * PT
                goes_on = mask[:, part, ::-1]
                for d in range(130):
                        column = big[:, a:a + PT + 1, d][:, ::-1]
                        nc.vector.tensor_tensor_scan(column, goes_on, column, 0.0, ALU.mult, ALU.add).then_inc(summed, 1)
                dve.wait_ge(summed, 130 * (n + 1))
            dve.wait_ge(extra_up, 1)
            nc.vector.tensor_copy(q["extra"][:, :], B["ps"][0][:, 0:W])

        @block.tensor
        def _(pe):
            pe.wait_ge(summed, 130 * PARTS)
            nc.tensor.matmul(B["ps"][0][:, 0:W], q["from_later"][:, :], big[:, 0, :], start=True, stop=True)\
              .then_inc(extra_up, 1)


def conv_edges(nc, B, layer):
    q, big, ps = B["orders"]["d"], B["big"], B["ps"]
    ai, aj, top, ex, tmp = B["ai"], B["aj"], B["top"], B["ex"], B["tmp"]
    with phase(nc) as ctx:
        def sem(n):
            return semaphore(nc, ctx, f"e{layer}_" + n)
        if layer == 0:
            inn, free = [sem(f"in{n}") for n in range(2)], sem("free")
            ring = [ctx.enter_context(nc.sbuf_tensor(f"xd{n}", [P, G, D], F32)) for n in range(2)]
            junk = [ctx.enter_context(nc.sbuf_tensor(f"e_junk{n}", [P, G, D], F32)) for n in range(2)]
            ai_up = sem("ai_up")
            block = ctx.enter_context(nc.Block())

            @block.sync
            def _(sp):
                table = B["x_dst"].rearrange("(p t) d -> p t d", t=T)

                def load(c, slot, last):
                    sp.wait_ge(free, c + 1)
                    sp.dma_start(ring[slot][:, :, :], table[:, bass.ds(c * G, G), :]).then_inc(inn[slot], 16)
                over_chunks(sp, load)

            @block.vector
            def _(dve):
                dve.sem_inc(free, 2)
                dve.sem_inc(ai_up, 1)

                def dots(c, slot, last):
                    dve.wait_ge(ai_up, c + 1)
                    for g in range(G):
                        at = bass.ds(c * G + g, 1)
                        ins = nc.vector.scalar_tensor_tensor(out=junk[0][:, g, :], in0=row(big[:, at, 0:D]), scalar=1.0,
                                                       in1=B["rows_"]["wi1"][:, :], op0=ALU.mult, op1=ALU.mult,
                                                       accum_out=ai[:, at])
                    ins.then_inc(ai_up, 1)
                    dve.wait_ge(free, c + 2)
                    dve.wait_ge(inn[slot], c * 8 + (16 if slot == 0 else 8))
                    for g in range(G):
                        at = bass.ds(c * G + g, 1)
                        ins = nc.vector.scalar_tensor_tensor(out=junk[1][:, g, :], in0=ring[slot][:, g, :], scalar=1.0,
                                                             in1=B["rows_"]["wj1"][:, :], op0=ALU.mult, op1=ALU.mult,
                                                             accum_out=aj[:, at])
                    ins.then_inc(free, 1)
                over_chunks(dve, dots)
        else:
            rows_in = [sem(f"rows{n}") for n in range(4)]
            aj_in = [sem(f"aj{n}") for n in range(4)]
            bare = BareRows(nc, ctx, B, "c1")
            block = ctx.enter_context(nc.Block())

            @block.vector
            def _(dve):
                bare.vector(dve)

            @block.scalar
            def _(act):
                bare.scalar(act)

            @block.sync
            def _(sp):
                bare.sync(sp)

            @block.gpsimd
            def _(gp):
                for t in range(T):
                    if t >= 4:
                        gp.wait_ge(rows_in[t % 4], 16 * (t // 4))
                        gp.wait_ge(aj_in[t % 4], 16 * (t // 4))
                    gp.indirect_dma_start(out=big[:, t, :], out_offset=None, in_=B["hidden"],
                                          in_offset=bass.IndirectOffsetOnAxis(ap=B["src_start_i"][:, t:t + 1], axis=0))\
                      .then_inc(rows_in[t % 4], 16)
                    gp.indirect_dma_start(out=aj[:, t:t + 1], out_offset=None, in_=B["hidden_aj"],
                                          in_offset=bass.IndirectOffsetOnAxis(ap=B["dst_start_i"][:, t:t + 1], axis=0))\
                      .then_inc(aj_in[t % 4], 16)
                for n in range(4):
                    gp.wait_ge(rows_in[n], 16 * (T // 4))
                    gp.wait_ge(aj_in[n], 16 * (T // 4))

    with phase(nc) as ctx:
        def sem(n):
            return semaphore(nc, ctx, f"m{layer}_" + n)
        own, cols_up, rows_up, shifted, exp_up = (sem(n) for n in ("own", "cols", "rows", "shifted", "exp"))
        diag = [ctx.enter_context(nc.sbuf_tensor(f"m{layer}_diag{n}", [P, P], F32)) for n in range(2)]
        masked = [ctx.enter_context(nc.sbuf_tensor(f"m{layer}_masked{n}", [P, P], F32)) for n in range(2)]
        most = ctx.enter_context(nc.sbuf_tensor(f"m{layer}_most", [P, 2], F32))
        block = ctx.enter_context(nc.Block())

        @block.vector
        def _(dve):
            fin = Finished(dve, own)
            if layer == 1:
                fin.after(nc.vector.tensor_copy(ai[:, :], big[:, 0:T, D]))
            edge_logits(dve, nc, B, fin, ai[:, :], aj[:, :], ex[:, :], tmp[0][:, :])
            nc.vector.tensor_scalar(tmp[0][:, :], q["same"][:, :], 1.0, HUGE, ALU.subtract, ALU.mult)
            fin.after(nc.vector.tensor_scalar(tmp[1][:, :], q["next"][:, :], 1.0, HUGE, ALU.subtract, ALU.mult))
            fin.after(nc.vector.tensor_tensor_scan(tmp[2][:, :], tmp[0][:, :], ex[:, :], -HUGE, ALU.add, ALU.max))
            fin.after(nc.vector.tensor_tensor_scan(top[:, ::-1], tmp[1][:, ::-1], tmp[2][:, ::-1], -HUGE, ALU.add, ALU.max))
            nc.vector.tensor_scalar(diag[0][:, :], B["ident"][:, :], tmp[2][:, T - 1:T], None, ALU.mult)
            nc.vector.tensor_scalar(diag[1][:, :], B["ident"][:, :], top[:, 0:1], None, ALU.mult).then_inc(cols_up, 1)
            nc.vector.tensor_scalar(masked[0][:, :], q["sel_before"][:, :], 1.0, HUGE, ALU.subtract, ALU.mult)
            fin.after(nc.vector.tensor_scalar(masked[1][:, :], q["sel_later"][:, :], 1.0, HUGE, ALU.subtract, ALU.mult))
            dve.wait_ge(rows_up, 1)
            nc.vector.tensor_tensor(masked[0][:, :], ps[0][:, 0:P], masked[0][:, :], ALU.add)
            fin.after(nc.vector.tensor_tensor(masked[1][:, :], ps[1][:, 0:P], masked[1][:, :], ALU.add))
            nc.vector.reduce_max(most[:, 0:1], masked[0][:, :], AX.X)
            nc.vector.reduce_max(most[:, 1:2], masked[1][:, :], AX.X)
            nc.vector.tensor_scalar(tmp[0][:, :], B["dst_key"][:, :], B["dst_key"][:, 0:1], None, ALU.is_equal)
            fin.after(nc.vector.tensor_scalar(tmp[1][:, :], q["tail"][:, :], 1.0, HUGE, ALU.subtract, ALU.mult))
            fin.after(nc.vector.tensor_scalar(tmp[0][:, :], tmp[0][:, :], 1.0, HUGE, ALU.subtract, ALU.mult))
            for n in range(2):
                fin.after(nc.vector.scalar_tensor_tensor(out=top[:, :], in0=tmp[n][:, :], scalar=most[:, n:n + 1],
                                                         in1=top[:, :], op0=ALU.add, op1=ALU.max))
            nc.vector.tensor_tensor(tmp[3][:, :], ex[:, :], top[:, :], ALU.subtract).then_inc(shifted, 1)
            nc.vector.tensor_copy(big[:, 0:T, 130], top[:, :])
            nc.vector.tensor_copy(big[:, 0:T, 131], aj[:, :])
            nc.vector.memset(big[:, 0:T, 129], 1.0)
            dve.wait_ge(exp_up, 1)
            fin.after(nc.vector.tensor_copy(big[:, 0:T, D], ex[:, :]))

        @block.tensor
        def _(pe):
            pe.wait_ge(cols_up, 1)
            for n in range(2):
                last = nc.tensor.matmul(ps[n][:, 0:P], B["ones"][:, :], diag[n][:, :], start=True, stop=True)
            last.then_inc(rows_up, 1)

        @block.scalar
        def _(act):
            act.wait_ge(shifted, 1)
            nc.scalar.activation(ex[:, :], tmp[3][:, :], ACT.Exp).then_inc(exp_up, 1)

    running_sums(nc, B, "d", ex, f"se{layer}_")

    with phase(nc) as ctx:
        fixed, stored = (semaphore(nc, ctx, n) for n in (f"w{layer}_fixed", f"w{layer}_stored"))
        block = ctx.enter_context(nc.Block())

        @block.vector
        def _(dve):
            with dve.Fori(0, T // 4, 1) as i:
                for j in range(4):
                    t = i * 4 + j
                    nc.vector.scalar_tensor_tensor(
                        out=row(big[:, bass.ds(t, 1), 0:130]), in0=q["extra"][:, 0:130], scalar=q["fix"][:, bass.ds(t, 1)],
                        in1=row(big[:, bass.ds(t, 1), 0:130]), op0=ALU.mult, op1=ALU.add).then_inc(fixed, 1)

        @block.sync
        def _(sp):
            table = B["sums"][layer].rearrange("(p t) d -> p t d", t=T)
            for c in range(7):
                sp.wait_ge(fixed, 28 * (c + 1))
                sp.dma_start(table[:, 28 * c:28 * c + 28, :], big[:, 28 * c:28 * c + 28, :]).then_inc(stored, 16)
            sp.wait_ge(stored, 16 * 7)


def by_source(nc, B):
    with phase(nc) as ctx:
        def sem(n):
            return semaphore(nc, ctx, "b_" + n)
        own, packed, edged, loaded = (sem(n) for n in ("own", "packed", "edged", "loaded"))
        sent = [sem(f"sent{n}") for n in range(4)]
        rec = ctx.enter_context(nc.sbuf_tensor("rec", [P, T, 4], F32))
        back = ctx.enter_context(nc.sbuf_tensor("back", [P, T, 4], F32))
        prev = rec
        front = ctx.enter_context(nc.sbuf_tensor("front", [1, 4], F32))
        bare = BareRows(nc, ctx, B, "b")
        block = ctx.enter_context(nc.Block())
        table = B["record"]

        @block.vector
        def _(dve):
            fin = Finished(dve, own)
            nc.vector.memset(front[:, :], -1.0)
            fin.after(nc.vector.memset(rec[:, :, :], 0.0))
            nc.vector.tensor_copy(rec[:, :, 0], B["orders"]["d"]["start"][:, :])
            nc.vector.tensor_copy(rec[:, :, 2], B["ai"][:, :])
            nc.vector.tensor_copy(rec[:, :, 1], B["src_key"][:, :]).then_inc(packed, 1)
            bare.vector(dve)
            dve.wait_ge(loaded, 32)
            nc.vector.tensor_copy(B["ai"][:, :], back[:, :, 2])
            nc.vector.tensor_copy(B["s_key"][:, :], back[:, :, 1])
            nc.vector.tensor_copy(B["s_dstart_i"][:, :], back[:, :, 0])
            nc.vector.tensor_copy(B["orders"]["s"]["prev"][:, :], prev[:, :, 1])
            nc.vector.tensor_scalar(B["s_gather"][:, :], back[:, :, 1], float(N - 1), None, ALU.min)

        @block.gpsimd
        def _(gp):
            gp.wait_ge(packed, 1)
            for t in range(T):
                if t >= 4:
                    gp.wait_ge(sent[t % 4], 16 * (t // 4))
                gp.indirect_dma_start(out=table, out_offset=bass.IndirectOffsetOnAxis(ap=B["src_place_i"][:, t:t + 1], axis=0),
                                      in_=rec[:, t, :], in_offset=None).then_inc(sent[t % 4], 16)

        @block.scalar
        def _(act):
            bare.scalar(act)

        @block.sync
        def _(sp):
            sp.wait_ge(own, 1)
            sp.dma_start(table[0:1, :], front[:, :]).then_inc(edged, 16)
            bare.sync(sp)
            sp.wait_ge(edged, 16)
            for n in range(4):
                sp.wait_ge(sent[n], 16 * (T // 4))
            sp.dma_start(back[:, :, :], table[1:EP + 1, :].rearrange("(p t) c -> p t c", t=T)).then_inc(loaded, 16)
            sp.dma_start(prev[:, :, :], table[0:EP, :].rearrange("(p t) c -> p t c", t=T)).then_inc(loaded, 16)


def conv_nodes(nc, B, layer):
    q, big, ps, tmp = B["orders"]["s"], B["big"], B["ps"], B["tmp"]
    ai, coef, top, ex = B["ai"], B["coef"], B["top"], B["ex"]
    with phase(nc) as ctx:
        def sem(n):
            return semaphore(nc, ctx, f"n{layer}_" + n)
        big_in = [sem(f"big{n}") for n in range(4)]
        bare = BareRows(nc, ctx, B, f"n{layer}")
        block = ctx.enter_context(nc.Block())

        @block.gpsimd
        def _(gp):
            for t in range(T):
                if t >= 4:
                    gp.wait_ge(big_in[t % 4], 16 * (t // 4))
                gp.indirect_dma_start(out=big[:, t, :], out_offset=None, in_=B["sums"][layer],
                                      in_offset=bass.IndirectOffsetOnAxis(ap=B["s_dstart_i"][:, t:t + 1], axis=0))\
                  .then_inc(big_in[t % 4], 16)
            for n in range(4):
                gp.wait_ge(big_in[n], 16 * (T // 4))

        @block.vector
        def _(dve):
            bare.vector(dve)

        @block.scalar
        def _(act):
            bare.scalar(act)

        @block.sync
        def _(sp):
            bare.sync(sp)

    with phase(nc) as ctx:
        def sem(n):
            return semaphore(nc, ctx, f"a{layer}_" + n)
        own, shifted, exp_up, sent, came = (sem(n) for n in ("own", "shifted", "exp", "sent", "came"))
        block = ctx.enter_context(nc.Block())

        @block.vector
        def _(dve):
            fin = Finished(dve, own)
            if layer == 1:
                propagate(dve, nc, B, "s", fin, B["ai2_s"][:, :], ai, tmp[2], sent, came, 1)
            edge_logits(dve, nc, B, fin, ai[:, :], big[:, 0:T, 131], ex[:, :], tmp[0][:, :])
            nc.vector.tensor_tensor(tmp[1][:, :], ex[:, :], big[:, 0:T, 130], ALU.subtract).then_inc(shifted, 1)
            fin.after(nc.vector.tensor_scalar(tmp[0][:, :], big[:, 0:T, D], 1e-16, None, ALU.add))
            fin.after(nc.vector.tensor_tensor(tmp[0][:, :], tmp[0][:, :], tmp[0][:, :], ALU.mult))
            fin.after(nc.vector.tensor_tensor(tmp[0][:, :], tmp[0][:, :], big[:, 0:T, 129], ALU.mult))
            fin.after(nc.vector.reciprocal(tmp[3][:, :], tmp[0][:, :]))
            nc.vector.memset(big[:, 0:T, 129], 1.0)
            dve.wait_ge(exp_up, 1)
            fin.after(nc.vector.tensor_tensor(coef[:, :], ex[:, :], tmp[3][:, :], ALU.mult))

        @block.scalar
        def _(act):
            act.wait_ge(shifted, 1)
            nc.scalar.activation(ex[:, :], tmp[1][:, :], ACT.Exp).then_inc(exp_up, 1)

        if layer == 1:
            @block.tensor
            def _(pe):
                propagate_pe(pe, nc, B, "s", tmp[2], sent, came, 1)

    running_sums(nc, B, "s", coef, f"sn{layer}_")
    if layer == 0:
        first_rows(nc, B)
    else:
        second_rows(nc, B)


def bank_rows(ps, first):
    return [ps[first + g // 4][:, (g % 4) * D:(g % 4) * D + D] for g in range(G)]


def fix_step(nc, B, o, dest, t):
    q = B["orders"][o]
    return nc.vector.scalar_tensor_tensor(
        out=dest, in0=q["extra"][:, 0:130], scalar=q["fix"][:, bass.ds(t, 1)],
        in1=row(B["big"][:, bass.ds(t, 1), 0:130]), op0=ALU.mult, op1=ALU.add)


def first_rows(nc, B):
    ps, rows_ = B["ps"], B["rows_"]
    with phase(nc) as ctx:
        def sem(n):
            return semaphore(nc, ctx, "h_" + n)

        def sb(n, shape):
            return ctx.enter_context(nc.sbuf_tensor("h_" + n, shape, F32))
        own, fixed, turned, copied, product, biased, active, dotted = (
            sem(n) for n in ("own", "fixed", "turned", "copied", "product", "biased", "active", "dotted"))
        stored = [sem(f"stored{n}") for n in range(2)]
        aj_stored, kept = sem("aj_stored"), sem("kept")
        full = [sb(f"full{n}", [P, G, W]) for n in range(2)]
        flipped = [sb(f"flipped{n}", [P, G * D]) for n in range(2)]
        inverse = [sb(f"inverse{n}", [P, G]) for n in range(2)]
        pre = [sb(f"pre{n}", [P, G, D]) for n in range(2)]
        below = [sb(f"below{n}", [P, G, D]) for n in range(2)]
        hid = [sb(f"hid{n}", [P, G, W]) for n in range(2)]
        junk = sb("junk", [P, 2 * G, D])
        aj_s = sb("aj_s", [P, T])
        block = ctx.enter_context(nc.Block())

        @block.vector
        def _(dve):
            fin = Finished(dve, own)
            dve.sem_inc(fixed, 1)
            dve.sem_inc(turned, 1)
            dve.sem_inc(kept, 1)
            nc.vector.memset(hid[0][:, :, :], 0.0)
            fin.after(nc.vector.memset(hid[1][:, :, :], 0.0))
            for n in range(2):
                dve.sem_inc(stored[n], 16)

            def fix(c, slot):
                for g in range(G):
                    ins = fix_step(nc, B, "s", full[slot][:, g, 0:130], c * G + g)
                ins.then_inc(fixed, 1)

            fix(0, 0)

            def body(c, slot, last):
                if not last:
                    dve.wait_ge(turned, c + 1)
                    fix(c + 1, 1 - slot)
                dve.wait_ge(fixed, c + 2)
                fin.after(nc.vector.reciprocal(inverse[slot][:, :], full[slot][:, :, 129]))
                dve.wait_ge(product, c + 1)
                for g, o in enumerate(bank_rows(ps, 4 + 2 * slot)):
                    ins = nc.vector.scalar_tensor_tensor(out=pre[slot][:, g, :], in0=o, scalar=inverse[slot][:, g:g + 1],
                                                         in1=rows_["b1"][:, :], op0=ALU.mult, op1=ALU.add)
                ins.then_inc(biased, 1)
                dve.wait_ge(active, c + 1)
                dve.wait_ge(stored[slot], c * 8 + (16 if slot == 0 else 8))
                dve.wait_ge(kept, c + 1)
                fin.after(nc.vector.scalar_tensor_tensor(out=hid[slot][:, :, 0:D], in0=below[slot][:, :, :],
                                                         scalar=B["drop"][:, 0:1], in1=pre[slot][:, :, :],
                                                         op0=ALU.mult, op1=ALU.add))
                for g in range(G):
                    at = bass.ds(c * G + g, 1)
                    nc.vector.scalar_tensor_tensor(out=junk[:, 2 * g, :], in0=hid[slot][:, g, 0:D], scalar=1.0, in1=rows_["wj2"][:, :],
                                                   op0=ALU.mult, op1=ALU.mult, accum_out=aj_s[:, at])
                    ins = nc.vector.scalar_tensor_tensor(out=junk[:, 2 * g + 1, :], in0=hid[slot][:, g, 0:D], scalar=1.0, in1=rows_["wi2"][:, :],
                                                         op0=ALU.mult, op1=ALU.mult, accum_out=hid[slot][:, g, D:D + 1])
                ins.then_inc(dotted, 1)
                dve.wait_ge(dotted, c + 1)
                nc.vector.tensor_copy(B["ai2_s"][:, bass.ds(c * G, G)], hid[slot][:, :, D]).then_inc(kept, 1)
            over_chunks(dve, body, [(fin, 2)])

        @block.tensor
        def _(pe):
            def body(c, slot, last):
                pe.wait_ge(fixed, c + 2)
                for g, o in enumerate(bank_rows(ps, 2 * slot)):
                    ins = nc.tensor.transpose(o, full[slot][:, g, 0:D], B["ident"][:, :])
                ins.then_inc(turned, 1)
                pe.wait_ge(copied, c + 1)
                for g, o in enumerate(bank_rows(ps, 4 + 2 * slot)):
                    ins = nc.tensor.matmul(o, flipped[slot][:, g * D:g * D + D], B["w1s"][:, :], start=True, stop=True)
                ins.then_inc(product, 1)
            over_chunks(pe, body)

        @block.scalar
        def _(act):
            def body(c, slot, last):
                act.wait_ge(turned, c + 2)
                nc.scalar.activation(flipped[slot][:, 0:4 * D], ps[2 * slot][:, 0:4 * D], ACT.Copy)
                nc.scalar.activation(flipped[slot][:, 4 * D:G * D], ps[2 * slot + 1][:, 0:3 * D], ACT.Copy).then_inc(copied, 1)
                act.wait_ge(biased, c + 1)
                nc.scalar.activation(below[slot][:, :, :], pre[slot][:, :, :], ACT.Relu, scale=-1.0).then_inc(active, 1)
            over_chunks(act, body)

        @block.sync
        def _(sp):
            table = B["hidden"][0:EP, :].rearrange("(p t) c -> p t c", t=T)

            def body(c, slot, last):
                sp.wait_ge(dotted, c + 1)
                sp.dma_start(table[:, bass.ds(c * G, G), :], hid[slot][:, :, :]).then_inc(stored[slot], 16)
            over_chunks(sp, body)
            sp.dma_start(B["hidden_aj"][0:EP, :].rearrange("(p t) c -> p (t c)", t=T), aj_s[:, :]).then_inc(aj_stored, 16)
            sp.wait_ge(aj_stored, 16)
            for n in range(2):
                sp.wait_ge(stored[n], 16 * (C // 2 + 1))


def wide(ap, g):
    return ap.rearrange("p (a d) -> p a d", a=1).to_broadcast([ap.shape[0], g, D])


class BareRows:

    def __init__(self, nc, ctx, B, name):
        self.nc, self.B, self.n = nc, B, BARE_CHUNKS[name]
        order = list(BARE_CHUNKS)
        assert sum(BARE_CHUNKS.values()) == DC and self.n % 2 == 0
        self.first = sum(BARE_CHUNKS[k] for k in order[:order.index(name)])

        def sem(n):
            return semaphore(nc, ctx, f"z{name}_" + n)

        def sb(n, shape):
            return ctx.enter_context(nc.sbuf_tensor(f"z{name}_" + n, shape, F32))
        self.own, self.act_own, self.x_free, self.below_up, self.clipped, self.mean_up, self.var_up = (
            sem(n) for n in ("own", "act_own", "x_free", "below_up", "clipped", "mean_up", "var_up"))
        self.roots_up, self.factor_up, self.u_up, self.u_var_up, self.done = (
            sem(n) for n in ("roots_up", "factor_up", "u_up", "u_var_up", "done"))
        self.x_in, self.stored = ([sem(f"{n}{k}") for k in range(2)] for n in ("x_in", "stored"))
        self.x, self.v, self.result = ([sb(f"{n}{k}", [DP, DG, D]) for k in range(2)] for n in ("x", "v", "result"))
        self.below = sb("below", [DP, DG, D])
        self.factor, self.unused = ([B["ps"][first + g // 4][0:DP, (g % 4) * D:(g % 4) * D + D] for g in range(DG)]
                                    for first in (0, 3))
        self.mean = [sb(f"mean{k}", [DP, DG]) for k in range(2)]
        self.sum, self.squares, self.u_sum, self.u_mean, self.u_squares, self.u_dev, self.u_inv = (
            sb(n, [DP, DG]) for n in ("sum", "squares", "u_sum", "u_mean", "u_squares", "u_dev", "u_inv"))
        self.dev, self.inv = sb("dev", [DP, 2, DG]), sb("inv", [DP, 2, DG])

    def vector(self, dve):
        v, B = self.nc.vector, self.B
        fin = Finished(dve, self.own)
        b2, beta = B["rows_"]["b2"][0:DP, :], B["rows_"]["beta"][0:DP, :]

        def body(c, pair, slot, live):
            new, middle, old = live
            this, last = self.v[slot], self.v[1 - slot]
            if middle:
                dve.wait_ge(self.var_up, c)
            if new:
                dve.wait_ge(self.x_in[slot], pair * 16 + 16)
                v.tensor_tensor(self.below[:, :, :], self.x[slot][:, :, :], wide(b2, DG), ALU.add).then_inc(self.below_up, 1)
                v.scalar_tensor_tensor(out=this[:, :, :], in0=self.x[slot][:, :, :], scalar=2.0, in1=wide(b2, DG),
                                       op0=ALU.mult, op1=ALU.add).then_inc(self.x_free, 1)
            if middle:
                v.reciprocal(self.inv[:, :, :], self.dev[:, :, :]).then_inc(self.roots_up, 1)
            if old:
                dve.wait_ge(self.u_var_up, c - 1)
                fin.after(v.reciprocal(self.u_inv[:, :], self.u_dev[:, :]))
                for g in range(DG):
                    ins = v.tensor_scalar(self.result[slot][:, g, :], self.result[slot][:, g, :], self.u_mean[:, g:g + 1],
                                          self.u_inv[:, g:g + 1], ALU.add, ALU.mult)
                ins.then_inc(self.done, 1)
            if new:
                dve.wait_ge(self.clipped, c + 1)
                dve.wait_ge(self.x_free, c + 1)
                for g in range(DG):
                    ins = v.scalar_tensor_tensor(out=this[:, g, :], in0=self.below[:, g, :], scalar=B["drop"][0:DP, 0:1],
                                                 in1=this[:, g, :], op0=ALU.mult, op1=ALU.add,
                                                 accum_out=self.sum[:, g:g + 1])
                fin.after(ins)
                v.tensor_scalar(self.mean[slot][:, :], self.sum[:, :], -1.0 / D, None, ALU.mult).then_inc(self.mean_up, 1)
                dve.wait_ge(self.mean_up, c + 1)
            if middle:
                dve.wait_ge(self.factor_up, c)
                if old:
                    dve.wait_ge(self.done, c - 1)
                wait(dve, self.stored[1 - slot], (pair + slot - 1) * 16)
                u = self.result[1 - slot]
                for g in range(DG):
                    ins = v.scalar_tensor_tensor(out=u[:, g, :], in0=last[:, g, :], scalar=self.mean[1 - slot][:, g:g + 1],
                                                 in1=self.factor[g], op0=ALU.add, op1=ALU.mult,
                                                 accum_out=self.u_sum[:, g:g + 1])
                fin.after(ins)
                v.tensor_tensor(u[:, :, :], u[:, :, :], wide(beta, DG), ALU.add)
                v.tensor_scalar(self.u_mean[:, :], self.u_sum[:, :], -1.0 / D, B["beta_mean"][0:DP, 0:1], ALU.mult,
                                ALU.subtract).then_inc(self.u_up, 1)
        turns(dve, self.n, 2, body, [(fin, 3)])

    def scalar(self, act):
        a, B = self.nc.scalar, self.B
        fin = Finished(act, self.act_own)
        gamma, eps, eps_sq = B["rows_"]["gamma"][0:DP, :], B["eps"][0:DP, 0:1], B["eps_sq"][0:DP, 0:1]

        def body(c, pair, slot, live):
            new, middle, old = live
            if new:
                act.wait_ge(self.below_up, c + 1)
                a.activation(self.below[:, :, :], self.below[:, :, :], ACT.Relu, scale=-1.0).then_inc(self.clipped, 1)
            if middle:
                act.wait_ge(self.roots_up, c)
                for g in range(DG):
                    ins = a.activation(self.factor[g], gamma, ACT.Identity, bias=self.inv[:, 0, g:g + 1],
                                       scale=self.inv[:, 1, g:g + 1])
                ins.then_inc(self.factor_up, 1)
            if new:
                act.wait_ge(self.mean_up, c + 1)
                squares(self.nc, fin, self.v[slot], self.mean[slot], self.unused, self.squares)
                a.activation(self.dev[:, 0, :], self.squares[:, :], ACT.Sqrt, bias=eps, scale=1.0 / D)
                a.activation(self.dev[:, 1, :], self.squares[:, :], ACT.Sqrt, bias=eps_sq, scale=(1.0 + EPS) / D)\
                    .then_inc(self.var_up, 1)
                act.wait_ge(self.var_up, c + 1)
            if middle:
                act.wait_ge(self.u_up, c)
                squares(self.nc, fin, self.result[1 - slot], self.u_mean, self.unused, self.u_squares)
                a.activation(self.u_dev[:, :], self.u_squares[:, :], ACT.Sqrt, bias=eps, scale=1.0 / D)\
                    .then_inc(self.u_var_up, 1)
        turns(act, self.n, 2, body, [(fin, 2)])

    def sync(self, sp):
        rows = DP * DG

        def at(table, c):
            flat = table[self.first * rows:(self.first + self.n) * rows, :].rearrange("(c p g) d -> c p g d", p=DP, g=DG)
            return flat[bass.ds(c, 1), :, :, :].rearrange("c p g d -> (c p) g d")

        def load(c, slot):
            sp.dma_start(self.x[slot][:, :, :], at(self.B["x"], c)).then_inc(self.x_in[slot], 16)

        def store(c, slot):
            sp.wait_ge(self.done, c + 1)
            sp.dma_start(at(self.B["out"], c), self.result[slot][:, :, :]).then_inc(self.stored[slot], 16)
        load(0, 0)
        load(1, 1)
        with sp.Fori(0, self.n // 2 - 1, 1) as i:
            for slot in range(2):
                sp.wait_ge(self.x_free, i * 2 + slot + 1)
                load(i * 2 + slot + 2, slot)
                store(i * 2 + slot, slot)
        for slot in range(2):
            store(self.n - 2 + slot, slot)
        for slot in range(2):
            sp.wait_ge(self.stored[slot], 16 * (self.n // 2))


def second_rows(nc, B):
    ps, rows_ = B["ps"], B["rows_"]
    with phase(nc) as ctx:
        def sem(n):
            return semaphore(nc, ctx, "g_" + n)

        def sb(n, shape):
            return ctx.enter_context(nc.sbuf_tensor("g_" + n, shape, F32))
        own, act_own, fixed, turned, copied, product, biased, added, clipped, mean_up, var_up, roots_up = (
            sem(n) for n in ("own", "act_own", "fixed", "turned", "copied", "product", "biased", "added", "clipped",
                             "mean_up", "var_up", "roots_up"))
        y_up, y_turned, y_copied, y_product, m_up, factor_up, u_up, u_var_up, done, z_free = (
            sem(n) for n in ("y_up", "y_turned", "y_copied", "y_product", "m_up", "factor_up", "u_up", "u_var_up",
                             "done", "z_free"))
        y_stored, m_stored = [sem(f"y_stored{k}") for k in range(2)], sem("m_stored")
        x_in = [sem(f"x_in{n}") for n in range(G)]
        scattered = [sem(f"sc{n}") for n in range(G)]
        full = [sb(f"full{n}", [P, G, 130]) for n in range(2)]
        flipped, y_flipped, ms = (sb(n, [P, G * D]) for n in ("flipped", "y_flipped", "m"))
        xs, v, ys, result = ([sb(f"{k}{n}", [P, G, D]) for n in range(2)] for k in ("x", "v", "y", "result"))
        pre, factor = sb("pre", [P, G, D]), sb("factor", [P, G, D])
        mean = [sb(f"mean{n}", [P, G]) for n in range(2)]
        inverse, total, sq, u_total, u_mean, u_sq, u_dev, u_inv = (
            sb(n, [P, G]) for n in ("inverse", "total", "sq", "u_total", "u_mean", "u_sq", "u_dev", "u_inv"))
        dev, inv = sb("dev", [P, 2, G]), sb("inv", [P, 2, G])
        block = ctx.enter_context(nc.Block())

        @block.vector
        def _(dve):
            fin, vec = Finished(dve, own), nc.vector

            def body(c, pair, slot, live):
                newest, second, third, oldest = live
                other = 1 - slot
                if third:
                    dve.wait_ge(var_up, c - 1)
                if second:
                    dve.wait_ge(fixed, c)
                    fin.after(vec.reciprocal(inverse[:, :], full[other][:, :, 129]))
                    dve.wait_ge(product, c)
                    for g, o in enumerate(bank_rows(ps, 2)):
                        ins = vec.scalar_tensor_tensor(out=pre[:, g, :], in0=o, scalar=inverse[:, g:g + 1],
                                                       in1=rows_["b2"][:, :], op0=ALU.mult, op1=ALU.add)
                    ins.then_inc(biased, 1)
                    dve.wait_ge(biased, c)
                    for n in range(G):
                        dve.wait_ge(x_in[n], c * 16)
                    vec.tensor_tensor(pre[:, :, :], pre[:, :, :], xs[other][:, :, :], ALU.add).then_inc(added, 1)
                    dve.wait_ge(added, c * 2 - 1)
                    vec.tensor_tensor(v[other][:, :, :], pre[:, :, :], xs[other][:, :, :], ALU.add).then_inc(added, 1)
                if third:
                    fin.after(vec.reciprocal(inv[:, :, :], dev[:, :, :]))
                    dve.sem_inc(roots_up, 1)
                    wait(dve, y_stored[slot], (pair - 1) * 16)
                    wait(dve, y_turned, c - 2)
                    for g in range(G):
                        ins = vec.tensor_scalar(ys[slot][:, g, :], v[slot][:, g, :], mean[slot][:, g:g + 1],
                                                inv[:, 0, g:g + 1], ALU.add, ALU.mult)
                    ins.then_inc(y_up, 1)
                if newest:
                    wait(dve, turned, c - 1)
                    for g in range(G):
                        ins = fix_step(nc, B, "s", full[slot][:, g, :], c * G + g)
                    ins.then_inc(fixed, 1)
                if oldest:
                    dve.wait_ge(u_var_up, c - 2)
                    fin.after(vec.reciprocal(u_inv[:, :], u_dev[:, :]))
                    for g in range(G):
                        ins = vec.tensor_scalar(result[other][:, g, :], result[other][:, g, :], u_mean[:, g:g + 1],
                                                u_inv[:, g:g + 1], ALU.add, ALU.mult)
                    ins.then_inc(done, 1)
                if second:
                    dve.wait_ge(clipped, c)
                    dve.wait_ge(added, c * 2)
                    for g in range(G):
                        ins = vec.scalar_tensor_tensor(out=v[other][:, g, :], in0=pre[:, g, :], scalar=B["drop"][:, 0:1],
                                                       in1=v[other][:, g, :], op0=ALU.mult, op1=ALU.add,
                                                       accum_out=total[:, g:g + 1])
                    fin.after(ins)
                    vec.tensor_scalar(mean[other][:, :], total[:, :], -1.0 / D, None, ALU.mult).then_inc(mean_up, 1)
                    dve.wait_ge(mean_up, c)
                if third:
                    dve.wait_ge(factor_up, c - 1)
                    wait(dve, z_free, c - 3)
                    if oldest:
                        dve.wait_ge(done, c - 2)
                    for g in range(G):
                        ins = vec.scalar_tensor_tensor(out=result[slot][:, g, :], in0=v[slot][:, g, :],
                                                       scalar=mean[slot][:, g:g + 1], in1=factor[:, g, :],
                                                       op0=ALU.add, op1=ALU.mult, accum_out=u_total[:, g:g + 1])
                    fin.after(ins)
                    vec.tensor_tensor(result[slot][:, :, :], result[slot][:, :, :], wide(rows_["beta"][:, :], G), ALU.add)
                    vec.tensor_scalar(u_mean[:, :], u_total[:, :], -1.0 / D, B["beta_mean"][:, 0:1], ALU.mult,
                                      ALU.subtract).then_inc(u_up, 1)
            turns(dve, C, 3, body, [(fin, 5)])

        @block.tensor
        def _(pe):
            def body(c, pair, slot, live):
                newest, second, third, oldest = live
                if third:
                    pe.wait_ge(y_up, c - 1)
                    wait(pe, y_copied, c - 2)
                    for g, o in enumerate(bank_rows(ps, 4)):
                        ins = nc.tensor.transpose(o, ys[slot][:, g, :], B["ident"][:, :])
                    ins.then_inc(y_turned, 1)
                if newest:
                    pe.wait_ge(fixed, c + 1)
                    wait(pe, copied, c)
                    for g, o in enumerate(bank_rows(ps, 0)):
                        ins = nc.tensor.transpose(o, full[slot][:, g, 0:D], B["ident"][:, :])
                    ins.then_inc(turned, 1)
                    pe.wait_ge(copied, c + 1)
                    wait(pe, biased, c)
                    for g, o in enumerate(bank_rows(ps, 2)):
                        ins = nc.tensor.matmul(o, flipped[:, g * D:g * D + D], B["w2s"][:, :], start=True, stop=True)
                    ins.then_inc(product, 1)
                if third:
                    pe.wait_ge(y_copied, c - 1)
                    wait(pe, m_up, c - 2)
                    for g, o in enumerate(bank_rows(ps, 6)):
                        ins = nc.tensor.matmul(o, y_flipped[:, g * D:g * D + D], B["m1s"][:, :], start=True, stop=True)
                    ins.then_inc(y_product, 1)
            turns(pe, C, 3, body)

        def copy_flipped(dest, first, sem_up):
            nc.scalar.activation(dest[:, 0:4 * D], ps[first][:, 0:4 * D], ACT.Copy)
            nc.scalar.activation(dest[:, 4 * D:G * D], ps[first + 1][:, 0:3 * D], ACT.Copy).then_inc(sem_up, 1)

        @block.scalar
        def _(act):
            fin = Finished(act, act_own)

            def body(c, pair, slot, live):
                newest, second, third, oldest = live
                if second:
                    act.wait_ge(added, c * 2)
                    nc.scalar.activation(pre[:, :, :], pre[:, :, :], ACT.Relu, scale=-1.0).then_inc(clipped, 1)
                if third:
                    act.wait_ge(roots_up, c - 1)
                    for g in range(G):
                        ins = nc.scalar.activation(factor[:, g, :], rows_["gamma"][:, :], ACT.Identity,
                                                   bias=inv[:, 0, g:g + 1], scale=inv[:, 1, g:g + 1])
                    ins.then_inc(factor_up, 1)
                    act.wait_ge(y_turned, c - 1)
                    wait(act, y_product, c - 2)
                    copy_flipped(y_flipped, 4, y_copied)
                if newest:
                    act.wait_ge(turned, c + 1)
                    wait(act, product, c)
                    copy_flipped(flipped, 0, copied)
                if second:
                    act.wait_ge(mean_up, c)
                    squares(nc, fin, v[1 - slot], mean[1 - slot], [pre[:, g, :] for g in range(G)], sq)
                    nc.scalar.activation(dev[:, 0, :], sq[:, :], ACT.Sqrt, bias=B["eps"][:, 0:1], scale=1.0 / D)
                    nc.scalar.activation(dev[:, 1, :], sq[:, :], ACT.Sqrt, bias=B["eps_sq"][:, 0:1],
                                         scale=(1.0 + EPS) / D).then_inc(var_up, 1)
                if third:
                    act.wait_ge(u_up, c - 1)
                    squares(nc, fin, result[slot], u_mean, [factor[:, g, :] for g in range(G)], u_sq)
                    nc.scalar.activation(u_dev[:, :], u_sq[:, :], ACT.Sqrt, bias=B["eps"][:, 0:1], scale=1.0 / D)\
                        .then_inc(u_var_up, 1)
                    act.wait_ge(y_product, c - 1)
                    wait(act, m_stored, (c - 2) * 16)
                    copy_flipped(ms, 6, m_up)
            turns(act, C, 3, body, [(fin, 2)])

        @block.sync
        def _(sp):
            def at(table, c):
                return table.rearrange("(p t) d -> p t d", t=T)[:, bass.ds(c * G, G), :]

            def body(c, slot, last):
                sp.wait_ge(y_up, c + 1)
                sp.dma_start(at(B["mixed"][0:EP, :], c), ys[slot][:, :, :]).then_inc(y_stored[slot], 16)
                sp.wait_ge(m_up, c + 1)
                sp.dma_start(at(B["mixed_m"][0:EP, :], c), ms[:, :].rearrange("p (g d) -> p g d", d=D)).then_inc(m_stored, 16)
            over_chunks(sp, body)
            for n in range(2):
                sp.wait_ge(y_stored[n], 16 * (C // 2))
            sp.wait_ge(m_stored, 16 * C)

        @block.gpsimd
        def _(gp):
            def gather(c):
                for g in range(G):
                    wait(gp, x_in[g], 16 * c)
                    t = c * G + g
                    gp.indirect_dma_start(out=xs[c % 2][:, g, :], out_offset=None, in_=B["x"],
                                          in_offset=bass.IndirectOffsetOnAxis(ap=B["s_gather"][:, t:t + 1], axis=0))\
                      .then_inc(x_in[g], 16)
            for c in range(C + 3):
                if c < C:
                    wait(gp, added, 2 * c - 2)
                    gather(c)
                if c >= 4:
                    scattered_chunk(gp, scattered, z_free, c - 4)
                if c >= 3:
                    scatter_chunk(gp, B, "s_scatter", result, done, scattered, c - 3)
            scattered_chunk(gp, scattered, z_free, C - 1)


def scatter_chunk(gp, B, name, result, done, scattered, c):
    gp.wait_ge(done, c + 1)
    for g in range(G):
        t = c * G + g
        gp.indirect_dma_start(out=B["out"], out_offset=bass.IndirectOffsetOnAxis(ap=B[name][:, t:t + 1], axis=0),
                              in_=result[c % 2][:, g, :], in_offset=None, bounds_check=N - 1, oob_is_err=False)\
          .then_inc(scattered[g], 16)


def scattered_chunk(gp, scattered, free, c):
    for g in range(G):
        gp.wait_ge(scattered[g], 16 * (c + 1))
    gp.sem_inc(free, 1)


def edge_network(nc, B):
    ps, rows_, big = B["ps"], B["rows_"], B["big"]
    with phase(nc) as ctx:
        def sem(n):
            return semaphore(nc, ctx, "u_" + n)

        def sb(n, shape):
            return ctx.enter_context(nc.sbuf_tensor("u_" + n, shape, F32))
        own, act_own, attr_in, cleared, sliced, turned, copied, product, summed = (
            sem(n) for n in ("own", "act_own", "attr_in", "cleared", "sliced", "turned", "copied", "product", "summed"))
        big_in = [sem(f"big{n}") for n in range(G)]
        attr = sb("attr", [P, T, 4])
        piece = [sb(f"piece{n}", [P, 4 * G]) for n in range(2)]
        below_up, clipped, mean_up, var_up, y_up, x_free = (
            sem(n) for n in ("below_up", "clipped", "mean_up", "var_up", "y_up", "x_free"))
        x_in, y_stored = ([sem(f"{k}{n}") for n in range(2)] for k in ("x_in", "y_stored"))
        xs, ys = ([sb(f"{k}{n}", [P, G, D]) for n in range(2)] for k in ("x", "y"))
        below = sb("below", [P, G, D])
        mean, total, sq, dev, inv = (sb(n, [P, G]) for n in ("mean", "total", "sq", "dev", "inv"))
        flipped = [sb(f"flipped{n}", [4 * G, P]) for n in range(2)]
        block = ctx.enter_context(nc.Block())

        @block.gpsimd
        def _(gp):
            gp.wait_ge(cleared, 1)
            for t in range(T):
                if t >= G:
                    gp.wait_ge(big_in[t % G], 16 * (t // G))
                gp.indirect_dma_start(out=big[:, t, 0:D], out_offset=None, in_=B["mixed_m"],
                                      in_offset=bass.IndirectOffsetOnAxis(ap=B["src_start_i"][:, t:t + 1], axis=0))\
                  .then_inc(big_in[t % G], 16)

        @block.sync
        def _(sp):
            sp.wait_ge(cleared, 1)
            sp.dma_start(attr[0:LAST, :, 0:3], B["edge_attr"][0:LAST * T, :].rearrange("(p t) k -> p t k", t=T))\
              .then_inc(attr_in, 16)
            sp.dma_start(attr[LAST:P, 0:LEFT, 0:3], B["edge_attr"][LAST * T:E, :].rearrange("(p t) k -> p t k", p=1))\
              .then_inc(attr_in, 16)
            for g in range(G):
                sp.dma_start(B["edge_w"][4 * g:4 * g + 3, g * D:g * D + D], B["m1"][D:D + 3, :]).then_inc(attr_in, 16)
                sp.dma_start(B["edge_w"][4 * g + 3:4 * g + 4, g * D:g * D + D], B["mb1"].rearrange("(a n) -> a n", a=1))\
                  .then_inc(attr_in, 16)
            table = B["x_dst"].rearrange("(p t) d -> p t d", t=T)

            def rows_of(c, pair, slot, live):
                new, _, old = live
                if new:
                    wait(sp, x_free, c - 1)
                    sp.dma_start(xs[slot][:, :, :], table[:, bass.ds(c * G, G), :]).then_inc(x_in[slot], 16)
                if old:
                    sp.wait_ge(y_up, c - 1)
                    sp.dma_start(table[:, bass.ds(c * G - 2 * G, G), :], ys[slot][:, :, :]).then_inc(y_stored[slot], 16)
            turns(sp, C, 2, rows_of)
            for n in range(2):
                sp.wait_ge(y_stored[n], 16 * (C // 2))

        @block.vector
        def _(dve):
            fin = Finished(dve, own)
            dve.sem_inc(turned, 1)
            fin.after(nc.vector.memset(attr[:, :, :], 0.0))
            nc.vector.memset(attr[:, :, 3], 1.0)
            nc.vector.memset(big[:, 0:T, 129], 1.0)
            nc.vector.memset(B["edge_w"][:, :], 0.0).then_inc(cleared, 1)
            dve.wait_ge(attr_in, 16 * (2 + 2 * G))
            nc.vector.tensor_copy(piece[0][:, :], attr[:, 0:G, :].rearrange("p g k -> p (g k)")).then_inc(sliced, 1)
            dve.wait_ge(sliced, 1)

            def result_row(c, slot):
                dve.wait_ge(var_up, c + 1)
                fin.after(nc.vector.reciprocal(inv[:, :], dev[:, :]))
                for g in range(G):
                    ins = nc.vector.tensor_scalar(ys[slot][:, g, :], ys[slot][:, g, :], mean[:, g:g + 1], inv[:, g:g + 1],
                                                  ALU.add, ALU.mult)
                ins.then_inc(y_up, 1)
                dve.wait_ge(y_up, c + 1)

            def body(c, pair, slot, live):
                new, old = live
                if new:
                    wait(dve, y_stored[slot], pair * 16)
                    dve.wait_ge(x_in[slot], pair * 16 + 16)
                    if old:
                        dve.wait_ge(var_up, c)
                    nc.vector.tensor_tensor(below[:, :, :], xs[slot][:, :, :], wide(rows_["b2"][:, :], G), ALU.add)\
                      .then_inc(below_up, 1)
                    nc.vector.scalar_tensor_tensor(out=ys[slot][:, :, :], in0=xs[slot][:, :, :], scalar=2.0,
                                                   in1=wide(rows_["b2"][:, :], G), op0=ALU.mult, op1=ALU.add).then_inc(x_free, 1)
                if old:
                    result_row(c - 1, 1 - slot)
                if new:
                    if not (isinstance(c, int) and c == 0):
                        dve.wait_ge(turned, c)
                        nc.vector.tensor_copy(piece[slot][:, :].rearrange("p (g k) -> p g k", k=4),
                                              attr[:, bass.ds(c * G, G), :]).then_inc(sliced, 1)
                    dve.wait_ge(clipped, c + 1)
                    dve.wait_ge(x_free, c + 1)
                    for g in range(G):
                        ins = nc.vector.scalar_tensor_tensor(out=ys[slot][:, g, :], in0=below[:, g, :],
                                                             scalar=B["drop"][:, 0:1], in1=ys[slot][:, g, :],
                                                             op0=ALU.mult, op1=ALU.add, accum_out=total[:, g:g + 1])
                    fin.after(ins)
                    nc.vector.tensor_scalar(mean[:, :], total[:, :], -1.0 / D, None, ALU.mult).then_inc(mean_up, 1)
                    dve.wait_ge(mean_up, c + 1)
                    dve.wait_ge(product, c + 1)
                    for n in range(G):
                        dve.wait_ge(big_in[n], c * 16 + 16)
                    for first, n in ((0, 4), (4, 3)):
                        rows = big[:, bass.ds(c * G + first, n), 0:D]
                        ins = nc.vector.tensor_tensor(
                            rows, ps[2 + 2 * slot + first // 4][:, 0:n * D].rearrange("p (g d) -> p g d", d=D), rows, ALU.add)
                    ins.then_inc(summed, 1)
            turns(dve, C, 1, body, [(fin, 2)])

        @block.tensor
        def _(pe):
            def body(c, slot, last):
                pe.wait_ge(sliced, c + 1)
                nc.tensor.transpose(ps[slot][0:4 * G, 0:P], piece[slot][:, :], B["ident"][:, :]).then_inc(turned, 1)
                pe.wait_ge(copied, c + 1)
                for n, wd in ((0, 4 * D), (1, 3 * D)):
                    ins = nc.tensor.matmul(ps[2 + 2 * slot + n][:, 0:wd], flipped[slot][:, :],
                                           B["edge_w"][:, n * 4 * D:n * 4 * D + wd], start=True, stop=True)
                ins.then_inc(product, 1)
            over_chunks(pe, body)

        @block.scalar
        def _(act):
            fin = Finished(act, act_own)

            def body(c, slot, last):
                act.wait_ge(turned, c + 2)
                nc.scalar.activation(flipped[slot][:, :], ps[slot][0:4 * G, 0:P], ACT.Copy).then_inc(copied, 1)
                act.wait_ge(below_up, c + 1)
                nc.scalar.activation(below[:, :, :], below[:, :, :], ACT.Relu, scale=-1.0).then_inc(clipped, 1)
                act.wait_ge(mean_up, c + 1)
                act.wait_ge(cleared, 1)
                squares(nc, fin, ys[slot], mean, bank_rows(ps, 6), sq)
                nc.scalar.activation(dev[:, :], sq[:, :], ACT.Sqrt, bias=B["eps"][:, 0:1], scale=1.0 / D).then_inc(var_up, 1)
                act.wait_ge(summed, c + 1)
                rows = big[:, bass.ds(c * G, G), 0:D]
                nc.scalar.activation(rows, rows, ACT.Gelu)
            over_chunks(act, body, [(fin, 1)])

    running_sums(nc, B, "d", None, "su_")
    with phase(nc) as ctx:
        def sem(n):
            return semaphore(nc, ctx, "v_" + n)

        def sb(n, shape):
            return ctx.enter_context(nc.sbuf_tensor("v_" + n, shape, F32))
        own, act_own, fixed, turned, copied, product, counted, mean_up, var_up, roots_up, factor_up, u_up, u_var_up = (
            sem(n) for n in ("own", "act_own", "fixed", "turned", "copied", "product", "counted", "mean_up", "var_up",
                             "roots_up", "factor_up", "u_up", "u_var_up"))
        done, y_free, z_free, alone_in, alone_free = (
            sem(n) for n in ("done", "y_free", "z_free", "alone_in", "alone_free"))
        y_in = [sem(f"y_in{n}") for n in range(G)]
        scattered = [sem(f"sc{n}") for n in range(G)]
        full = [sb(f"full{n}", [P, G, 130]) for n in range(2)]
        flipped, alone = sb("flipped", [P, G * D]), sb("alone", [P, G, D])
        ys, y_beta, z, result = ([sb(f"{k}{n}", [P, G, D]) for n in range(2)] for k in ("y", "y_beta", "z", "result"))
        mean = [sb(f"mean{n}", [P, G]) for n in range(2)]
        total, sq, dev, inv, u_total, u_mean, u_sq, u_dev, u_inv = (
            sb(n, [P, G]) for n in ("total", "sq", "dev", "inv", "u_total", "u_mean", "u_sq", "u_dev", "u_inv"))
        factor, unused = bank_rows(ps, 4), bank_rows(ps, 6)
        block = ctx.enter_context(nc.Block())

        @block.vector
        def _(dve):
            fin, vec = Finished(dve, own), nc.vector
            fin.after(vec.tensor_scalar(B["absent"][:, :], B["dst_start"][:, :], float(ABSENT), None, ALU.is_equal))

            def body(c, pair, slot, live):
                newest, second, third, oldest = live
                other = 1 - slot
                if third:
                    dve.wait_ge(var_up, c - 1)
                    vec.reciprocal(inv[:, :], dev[:, :]).then_inc(roots_up, 1)
                if second:
                    dve.wait_ge(fixed, c)
                    dve.wait_ge(product, c)
                    for g, o in enumerate(bank_rows(ps, 2)):
                        ins = vec.scalar_tensor_tensor(out=z[other][:, g, :], in0=rows_["mb2"][:, :],
                                                       scalar=full[other][:, g, 129:130], in1=o, op0=ALU.mult, op1=ALU.add)
                    ins.then_inc(counted, 1)
                    dve.wait_ge(alone_in, c * 16)
                    for n in range(G):
                        dve.wait_ge(y_in[n], c * 16)
                    for g in range(G):
                        ins = vec.scalar_tensor_tensor(out=ys[other][:, g, :], in0=alone[:, g, :],
                                                       scalar=B["absent"][:, bass.ds(c * G + (g - G), 1)],
                                                       in1=ys[other][:, g, :], op0=ALU.mult, op1=ALU.add)
                    fin.after(ins)
                    dve.sem_inc(alone_free, 1)
                    vec.tensor_tensor(y_beta[other][:, :, :], ys[other][:, :, :], wide(rows_["beta"][:, :], G), ALU.add)
                    for g in range(G):
                        ins = vec.scalar_tensor_tensor(out=z[other][:, g, :], in0=z[other][:, g, :], scalar=1.0,
                                                       in1=ys[other][:, g, :], op0=ALU.mult, op1=ALU.add,
                                                       accum_out=total[:, g:g + 1])
                    fin.after(ins)
                    dve.sem_inc(y_free, 1)
                    vec.tensor_scalar(mean[other][:, :], total[:, :], -1.0 / D, None, ALU.mult).then_inc(mean_up, 1)
                    dve.wait_ge(mean_up, c)
                if newest:
                    wait(dve, turned, c - 1)
                    for g in range(G):
                        ins = fix_step(nc, B, "d", full[slot][:, g, :], c * G + g)
                    ins.then_inc(fixed, 1)
                if oldest:
                    dve.wait_ge(u_var_up, c - 2)
                    fin.after(vec.reciprocal(u_inv[:, :], u_dev[:, :]))
                    for g in range(G):
                        ins = vec.tensor_scalar(result[other][:, g, :], result[other][:, g, :], u_mean[:, g:g + 1],
                                                u_inv[:, g:g + 1], ALU.add, ALU.mult)
                    ins.then_inc(done, 1)
                if third:
                    dve.wait_ge(factor_up, c - 1)
                    wait(dve, z_free, c - 3)
                    for g in range(G):
                        ins = vec.scalar_tensor_tensor(out=result[slot][:, g, :], in0=z[slot][:, g, :],
                                                       scalar=mean[slot][:, g:g + 1], in1=factor[g],
                                                       op0=ALU.add, op1=ALU.mult)
                    fin.after(ins)
                    for g in range(G):
                        ins = vec.scalar_tensor_tensor(out=result[slot][:, g, :], in0=result[slot][:, g, :], scalar=1.0,
                                                       in1=y_beta[slot][:, g, :], op0=ALU.mult, op1=ALU.add,
                                                       accum_out=u_total[:, g:g + 1])
                    fin.after(ins)
                    if oldest:
                        dve.wait_ge(done, c - 2)
                    vec.tensor_scalar(u_mean[:, :], u_total[:, :], -1.0 / D, None, ALU.mult).then_inc(u_up, 1)
            turns(dve, C, 3, body, [(fin, 5)])

        @block.tensor
        def _(pe):
            def body(c, slot, last):
                pe.wait_ge(fixed, c + 1)
                for g, o in enumerate(bank_rows(ps, 0)):
                    ins = nc.tensor.transpose(o, full[slot][:, g, 0:D], B["ident"][:, :])
                ins.then_inc(turned, 1)
                pe.wait_ge(copied, c + 1)
                pe.wait_ge(counted, c)
                for g, o in enumerate(bank_rows(ps, 2)):
                    ins = nc.tensor.matmul(o, flipped[:, g * D:g * D + D], B["m2s"][:, :], start=True, stop=True)
                ins.then_inc(product, 1)
            over_chunks(pe, body)

        @block.scalar
        def _(act):
            fin = Finished(act, act_own)

            def body(c, pair, slot, live):
                newest, second, third, oldest = live
                if third:
                    act.wait_ge(roots_up, c - 1)
                    for g in range(G):
                        ins = nc.scalar.activation(factor[g], rows_["gamma"][:, :], ACT.Copy, scale=inv[:, g:g + 1])
                    ins.then_inc(factor_up, 1)
                if second:
                    act.wait_ge(mean_up, c)
                    squares(nc, fin, z[1 - slot], mean[1 - slot], unused, sq)
                    nc.scalar.activation(dev[:, :], sq[:, :], ACT.Sqrt, bias=B["eps"][:, 0:1], scale=1.0 / D)\
                        .then_inc(var_up, 1)
                if newest:
                    act.wait_ge(turned, c + 1)
                    wait(act, product, c)
                    nc.scalar.activation(flipped[:, 0:4 * D], ps[0][:, 0:4 * D], ACT.Copy)
                    nc.scalar.activation(flipped[:, 4 * D:G * D], ps[1][:, 0:3 * D], ACT.Copy).then_inc(copied, 1)
                if third:
                    act.wait_ge(u_up, c - 1)
                    squares(nc, fin, result[slot], u_mean, unused, u_sq)
                    nc.scalar.activation(u_dev[:, :], u_sq[:, :], ACT.Sqrt, bias=B["eps"][:, 0:1], scale=1.0 / D)\
                        .then_inc(u_var_up, 1)
            turns(act, C, 3, body, [(fin, 2)])

        @block.sync
        def _(sp):
            table = B["x_dst"].rearrange("(p t) d -> p t d", t=T)

            def load(c):
                sp.dma_start(alone[:, :, :], table[:, bass.ds(c * G, G), :]).then_inc(alone_in, 16)
            load(0)
            with sp.Fori(0, C - 1, 1) as i:
                sp.wait_ge(alone_free, i + 1)
                load(i + 1)

        @block.gpsimd
        def _(gp):
            def gather(c):
                for g in range(G):
                    wait(gp, y_in[g], 16 * c)
                    t = c * G + g
                    gp.indirect_dma_start(out=ys[c % 2][:, g, :], out_offset=None, in_=B["mixed"],
                                          in_offset=bass.IndirectOffsetOnAxis(ap=B["dst_start_i"][:, t:t + 1], axis=0))\
                      .then_inc(y_in[g], 16)
            for c in range(C + 3):
                if c < C:
                    wait(gp, y_free, c - 1)
                    gather(c)
                if c >= 4:
                    scattered_chunk(gp, scattered, z_free, c - 4)
                if c >= 3:
                    scatter_chunk(gp, B, "d_scatter", result, done, scattered, c - 3)
            scattered_chunk(gp, scattered, z_free, C - 1)


_INS = ['x', 'src', 'dst', 'edge_attr_3', 'L0_gnn_W1', 'L0_gnn_att1', 'L0_gnn_b1', 'L0_gnn_W2', 'L0_gnn_att2',
        'L0_gnn_b2', 'L0_gnn_prelu_a', 'L1_gnn_W1', 'L1_gnn_b1', 'L1_gnn_W2', 'L1_gnn_b2', 'L1_gnn_gamma', 'L1_gnn_beta']


def kernel(**inputs):
    import numpy as _np
    import concourse.bacc as _bacc
    from concourse import mybir as _mybir
    from concourse.bass_utils import run_bass_kernel_spmd as _run

    nc = _bacc.Bacc("TRN2", target_bir_lowering=False, num_devices=1)
    arrays, args = {}, []
    for name in _INS:
        a = _np.ascontiguousarray(inputs[name])
        if a.ndim == 0:
            a = a.reshape(1)
        arrays[f"in_{name}"] = a
        args.append(nc.dram_tensor(f"in_{name}", a.shape, _mybir.dt.from_np(a.dtype), kind="ExternalInput").ap())
    out = nc.dram_tensor("out_rows", (N, D), _mybir.dt.float32, kind="ExternalOutput").ap()
    program(nc, *args, out)
    r = _run(nc, [arrays], core_ids=[0])
    return r.results[0]["out_rows"]
```

```python
import concourse.bass as bass
import concourse.mybir as mybir
from contextlib import ExitStack

F32 = mybir.dt.float32
F16 = mybir.dt.float16
I32 = mybir.dt.int32
ALU = mybir.AluOpType
ACT = mybir.ActivationFunctionType
AX = mybir.AxisListType

P = 128
N = 100000
D = 128
E = 25000
T = 196
EP = P * T
LO = 128
HI = 782
BANK = 512
PAD_KEY = HI * LO - 1
ABSENT = EP
ROWS = EP + P
W = 132
EPS = 1e-5
LAST = P - 1
LEFT = E - LAST * T
HUGE = 1.0e38
PARTS = 2
PT = T // PARTS
DVE_END, POOL_END = 20, 50
G = 7
C = T // G
DP = 125
DG = 10
DC = N // (DP * DG)
BARE_CHUNKS = {"b": 16, "n0": 16, "c1": 32, "n1": 16}


class Tally:

    def __init__(self, n=0):
        self.n, self.base, self.start = n, 0, 0

    def next(self, by=1):
        self.n += by
        return self.base + self.n

    def loop(self, turn, each):
        self.start = self.base + self.n
        self.base, self.n = turn * each + self.start, 0

    def end(self, turns, each):
        assert self.n == each, (self.n, each)
        self.base, self.n = self.start + turns * each, 0


class Finished(Tally):

    def __init__(self, eng, sem, n=0):
        Tally.__init__(self, n)
        self.eng, self.sem = eng, sem

    def after(self, ins):
        ins.then_inc(self.sem, 1)
        self.eng.wait_ge(self.sem, self.next())


def over_chunks(eng, body, tallies=()):
    turns = C // 2 - 1
    with eng.Fori(0, turns, 1) as i:
        for tally, each in tallies:
            tally.loop(i, 2 * each)
        body(i * 2, 0, False)
        body(i * 2 + 1, 1, False)
    for tally, each in tallies:
        tally.end(turns, 2 * each)
    body(C - 2, 0, False)
    body(C - 1, 1, True)


def turns(eng, n, depth, body, tallies=()):
    warm = depth + depth % 2

    def live(c):
        return [0 <= c - k < n for k in range(depth + 1)]
    for c in range(warm):
        body(c, c // 2, c % 2, live(c))
    pairs = (n - warm) // 2
    with eng.Fori(0, pairs, 1) as i:
        for tally, each in tallies:
            tally.loop(i, 2 * each)
        for slot in range(2):
            body(i * 2 + (warm + slot), i + warm // 2, slot, [True] * (depth + 1))
    for tally, each in tallies:
        tally.end(pairs, 2 * each)
    for c in range(n, n + depth):
        body(c, c // 2, c % 2, live(c))


def wait(eng, sem, value):
    if not isinstance(value, int) or value > 0:
        eng.wait_ge(sem, value)


def squares(nc, fin, rows, less_mean, unused, total):
    for g, place in enumerate(unused):
        ins = nc.scalar.activation(place, rows[:, g, :], ACT.Square, bias=less_mean[:, g:g + 1],
                                   accum_out=total[:, g:g + 1])
    fin.after(ins)


def semaphore(nc, ctx, name):
    handle = nc.alloc_semaphore(name)
    ctx.callback(nc.clear_and_free_semaphores, [handle])
    return handle


def phase(nc):
    ctx = ExitStack()
    ctx.callback(nc.all_engine_barrier, sem_only=True)
    return ctx


def row(ap):
    return ap.rearrange("p a n -> p (a n)")


def program(nc, x, src, dst, edge_attr, w1, att1, b1, w2, att2, b2, prelu_a,
            m1, mb1, m2, mb2, gamma, beta, out):
    ctx = ExitStack()
    with ctx:
        def sb(name, shape, dt=F32):
            return ctx.enter_context(nc.sbuf_tensor(name, shape, dt))

        def dram(name, shape, dt=F32):
            return nc.dram_tensor(name, shape, dt, kind="Internal").ap()

        big = sb("big", [P, T + 1, W])
        psum = ctx.enter_context(nc.psum_tensor("psum", [P, 8, 512], F32))
        ps = [psum[:, n, :] for n in range(8)]
        flat_psum = psum[:, :, :].rearrange("p b n -> p (b n)")
        ident = sb("ident", [P, P])
        ident16 = sb("ident16", [P, P], F16)
        ones16 = sb("ones16", [P, P], F16)
        ones = sb("ones", [P, P])
        before = sb("before", [P, P])
        later = sb("later", [P, P])
        iota_p = sb("iota_p", [P, 1])
        place = sb("place", [P, T])
        eps = sb("eps", [P, 1])
        eps_sq = sb("eps_sq", [P, 1])
        beta_mean = sb("beta_mean", [P, 1])
        alpha = sb("alpha", [P, 1])
        drop = sb("drop", [P, 1])
        w1s, w2s, m1s, m2s = (sb(n, [P, D]) for n in ("w1s", "w2s", "m1s", "m2s"))
        edge_w = sb("edge_w", [4 * G, G * D])
        rows_ = {n: sb("row_" + n, [P, D]) for n in ("b1", "b2", "mb2", "gamma", "beta", "wi1", "wj1", "wi2", "wj2")}
        aj_absent = sb("aj_absent", [P, 1])
        src_key, dst_key = sb("src_key", [P, T]), sb("dst_key", [P, T])
        src_gather, dst_gather = sb("src_gather", [P, T], I32), sb("dst_gather", [P, T], I32)
        src_start, dst_start = sb("src_start", [P, T]), sb("dst_start", [P, T])
        src_start_i, dst_start_i = sb("src_start_i", [P, T], I32), sb("dst_start_i", [P, T], I32)
        src_place, src_place_i = sb("src_place", [P, T]), sb("src_place_i", [P, T], I32)
        orders = {}
        for o in ("d", "s"):
            orders[o] = {n: sb(f"{o}_{n}", [P, T]) for n in
                         ("prev", "new", "same", "next", "runs", "tail", "fix", "start")}
            orders[o].update({n: sb(f"{o}_{n}", [P, P]) for n in ("from_before", "from_later", "sel_before", "sel_later")})
            orders[o].update({n: sb(f"{o}_{n}", [P, 1]) for n in ("has_new",)})
            orders[o]["extra"] = sb(f"{o}_extra", [P, W])
        s_key = sb("s_key", [P, T])
        s_gather = sb("s_gather", [P, T], I32)
        s_scatter = sb("s_scatter", [P, T], I32)
        s_dstart_i = sb("s_dstart_i", [P, T], I32)
        d_scatter = sb("d_scatter", [P, T], I32)
        ai, aj, top, ex, coef = (sb(n, [P, T]) for n in ("ai", "aj", "top", "ex", "coef"))
        tmp_all = sb("tmp_all", [P, 4 * T])
        tmp = [tmp_all[:, n * T:n * T + T] for n in range(4)]
        attr = tmp_all[:, :].rearrange("p (t k) -> p t k", k=4)
        ai2_s = sb("ai2_s", [P, T])
        absent = sb("absent", [P, T])

        x_dst = dram("x_dst", [EP, D])
        record = dram("record", [EP + 1, 4])
        start_of = dram("start_of", [LO * HI, 1])
        sums = [dram(f"sums{n}", [EP, W]) for n in range(2)]
        hidden = dram("hidden", [ROWS, W])
        hidden_aj = dram("hidden_aj", [ROWS, 1])
        mixed = dram("mixed", [ROWS, D])
        mixed_m = dram("mixed_m", [ROWS, D])

        B = dict(locals())
        setup(nc, B)
        counting(nc, B)
        order_flags(nc, B, "d")
        conv_edges(nc, B, 0)
        by_source(nc, B)
        order_flags(nc, B, "s")
        conv_nodes(nc, B, 0)
        conv_edges(nc, B, 1)
        conv_nodes(nc, B, 1)
        edge_network(nc, B)


def shifted_loads(eng, dest, source, sem):
    eng.dma_start(dest[0:1, 1:T], source[0:T - 1].rearrange("(p t) -> p t", p=1)).then_inc(sem, 16)
    eng.dma_start(dest[1:LAST, :], source[T - 1:LAST * T - 1].rearrange("(p t) -> p t", t=T)).then_inc(sem, 16)
    eng.dma_start(dest[LAST:P, 0:LEFT + 1], source[LAST * T - 1:E].rearrange("(p t) -> p t", p=1)).then_inc(sem, 16)


def setup(nc, B):
    with phase(nc) as ctx:
        def sem(name):
            return semaphore(nc, ctx, name)
        key_i = [ctx.enter_context(nc.sbuf_tensor(f"key_i{n}", [P, T], I32)) for n in range(2)]
        prev_i = ctx.enter_context(nc.sbuf_tensor("prev_i", [P, T], I32))
        wt = [ctx.enter_context(nc.sbuf_tensor(f"wt{n}", [P, P], F32)) for n in range(2)]
        att_bc = [ctx.enter_context(nc.sbuf_tensor(f"att_bc{n}", [P, P], F32)) for n in range(4)]
        att_col = ctx.enter_context(nc.sbuf_tensor("att_col", [P, 4], F32))
        hid_row = ctx.enter_context(nc.sbuf_tensor("hid_row", [P, W], F32))
        junk = ctx.enter_context(nc.sbuf_tensor("junk", [P, D], F32))
        unused_i = ctx.enter_context(nc.sbuf_tensor("unused_i", [P, D], F32))
        zero_row = ctx.enter_context(nc.sbuf_tensor("zero_row", [P, D], F32))
        place_i = ctx.enter_context(nc.sbuf_tensor("place_i", [P, T], I32))
        filled, loaded, made, own = sem("filled"), sem("loaded"), sem("made"), sem("own")
        weights_up, turned, copied, rows_up, absent_row, stored = (
            sem(n) for n in ("weights_up", "turned", "copied", "rows_up", "absent_row", "stored"))
        pool_own = sem("pool_own")
        block = ctx.enter_context(nc.Block())
        rows_, ps = B["rows_"], B["ps"]

        @block.sync
        def _(sp):
            n = 0
            for dest, source in ((B["w1s"], B["w1"]), (B["w2s"], B["w2"]), (B["m1s"], B["m1"][0:D, :]), (B["m2s"], B["m2"])):
                sp.dma_start(dest[:, :], source).then_inc(weights_up, 16)
            for n, att in enumerate((B["att1"], B["att2"])):
                sp.dma_start(att_col[:, 2 * n:2 * n + 2], att.rearrange("(a p) -> p a", p=P),
                             allow_slow_non_contiguous=True).then_inc(weights_up, 16)
            for name in ("b1", "b2", "mb2", "gamma", "beta"):
                sp.dma_start(rows_[name][:, :], B[name].rearrange("(a n) -> a n", a=1).to_broadcast([P, D]))\
                  .then_inc(weights_up, 16)
            sp.dma_start(B["alpha"][:, :], B["prelu_a"].rearrange("(a n) -> a n", a=1).to_broadcast([P, 1]))\
              .then_inc(weights_up, 16)
            sp.wait_ge(filled, 3)
            for k, source in ((key_i[0], B["src"]), (key_i[1], B["dst"])):
                sp.dma_start(k[0:LAST, :], source[0:LAST * T].rearrange("(p t) -> p t", t=T)).then_inc(loaded, 16)
                sp.dma_start(k[LAST:P, 0:LEFT], source[LAST * T:E].rearrange("(p t) -> p t", p=1)).then_inc(loaded, 16)
            shifted_loads(sp, prev_i, B["dst"], loaded)
            sp.wait_ge(absent_row, 2)
            sp.dma_start(B["hidden"][EP:ROWS, :], hid_row[:, :]).then_inc(stored, 16)
            sp.dma_start(B["hidden_aj"][EP:ROWS, :], B["aj_absent"][:, :]).then_inc(stored, 16)
            sp.dma_start(B["mixed"][EP:ROWS, :], zero_row[:, :]).then_inc(stored, 16)
            sp.dma_start(B["mixed_m"][EP:ROWS, :], zero_row[:, :]).then_inc(stored, 16)
            sp.wait_ge(stored, 64)

        @block.gpsimd
        def _(gp):
            gp.memset(B["ident"][:, :], 0.0).then_inc(pool_own, 1)
            gp.memset(B["before"][:, :], 1.0).then_inc(pool_own, 1)
            gp.memset(B["later"][:, :], 1.0).then_inc(pool_own, 1)
            gp.wait_ge(pool_own, 3)
            gp.affine_select(out=B["ident"][:, :], in_=B["ident"][:, :], compare_op=ALU.not_equal, fill=1.0,
                             base=0, pattern=[[-1, P]], channel_multiplier=1).then_inc(made, 1)
            gp.affine_select(out=B["before"][:, :], in_=B["before"][:, :], compare_op=ALU.is_gt, fill=0.0,
                             base=0, pattern=[[1, P]], channel_multiplier=-1).then_inc(made, 1)
            gp.affine_select(out=B["later"][:, :], in_=B["later"][:, :], compare_op=ALU.is_gt, fill=0.0,
                             base=0, pattern=[[-1, P]], channel_multiplier=1).then_inc(made, 1)
            gp.iota(place_i[:, :], pattern=[[1, T]], base=0, channel_multiplier=T).then_inc(made, 1)

        @block.vector
        def _(dve):
            fin = Finished(dve, own)
            nc.vector.memset(key_i[0][:, :], PAD_KEY).then_inc(filled, 1)
            nc.vector.memset(key_i[1][:, :], PAD_KEY).then_inc(filled, 1)
            nc.vector.memset(prev_i[:, :], PAD_KEY).then_inc(filled, 1)
            nc.vector.memset(B["ones16"][:, :], 1.0)
            nc.vector.memset(B["ones"][:, :], 1.0)
            nc.vector.memset(B["eps"][:, :], EPS)
            nc.vector.memset(B["eps_sq"][:, :], EPS * EPS)
            nc.vector.memset(hid_row[:, :], 0.0)
            nc.vector.memset(zero_row[:, :], 0.0)
            fin.after(nc.vector.memset(B["big"][:, :, :], 0.0))
            dve.wait_ge(made, 4)
            nc.vector.tensor_copy(B["ident16"][:, :], B["ident"][:, :])
            nc.vector.tensor_copy(B["place"][:, :], place_i[:, :])
            dve.wait_ge(loaded, 7 * 16)
            nc.vector.tensor_copy(B["src_key"][:, :], key_i[0][:, :])
            nc.vector.tensor_copy(B["dst_key"][:, :], key_i[1][:, :])
            fin.after(nc.vector.tensor_copy(B["orders"]["d"]["prev"][:, :], prev_i[:, :]))
            fin.after(nc.vector.memset(B["orders"]["d"]["prev"][0:1, 0:1], -1.0))
            nc.vector.tensor_scalar(B["src_gather"][:, :], B["src_key"][:, :], float(N - 1), None, ALU.min)
            nc.vector.tensor_scalar(B["dst_gather"][:, :], B["dst_key"][:, :], float(N - 1), None, ALU.min)
            dve.wait_ge(weights_up, 12 * 16)
            for n in range(4):
                fin.after(nc.vector.tensor_scalar(att_bc[n][:, :], B["ones"][:, :], att_col[:, n:n + 1], None, ALU.mult))
            dve.wait_ge(turned, 2)
            nc.vector.tensor_copy(wt[0][:, :], ps[0][:, 0:P]).then_inc(copied, 1)
            nc.vector.tensor_copy(wt[1][:, :], ps[1][:, 0:P]).then_inc(copied, 1)
            dve.wait_ge(rows_up, 1)
            for n, name in enumerate(("wi1", "wj1", "wi2", "wj2")):
                nc.vector.tensor_copy(rows_[name][:, :], ps[2][:, n * P:n * P + P])
            fin.after(nc.vector.tensor_scalar(B["drop"][:, :], B["alpha"][:, :], -1.0, 1.0, ALU.mult, ALU.add))
            fin.after(nc.vector.tensor_scalar(junk[:, :], rows_["beta"][:, :], 1.0 / D, 0.0, ALU.mult, ALU.add,
                                              accum_out=B["beta_mean"][:, :]))
            fin.after(nc.vector.tensor_scalar(junk[:, :], rows_["b1"][:, :], -1.0, 0.0, ALU.mult, ALU.max))
            fin.after(nc.vector.scalar_tensor_tensor(out=hid_row[:, 0:D], in0=junk[:, :], scalar=B["drop"][:, 0:1],
                                                     in1=rows_["b1"][:, :], op0=ALU.mult, op1=ALU.add))
            fin.after(nc.vector.scalar_tensor_tensor(
                out=junk[:, :], in0=hid_row[:, 0:D], scalar=1.0, in1=rows_["wj2"][:, :],
                op0=ALU.mult, op1=ALU.mult, accum_out=B["aj_absent"][:, :]))
            nc.vector.scalar_tensor_tensor(
                out=unused_i[:, :], in0=hid_row[:, 0:D], scalar=1.0, in1=rows_["wi2"][:, :],
                op0=ALU.mult, op1=ALU.mult, accum_out=hid_row[:, D:D + 1]).then_inc(absent_row, 2)

        @block.tensor
        def _(pe):
            pe.wait_ge(weights_up, 12 * 16)
            pe.wait_ge(made, 1)
            for n, w in enumerate((B["w1s"], B["w2s"])):
                nc.tensor.transpose(ps[n][:, 0:P], w[:, :], B["ident"][:, :]).then_inc(turned, 1)
            pe.wait_ge(copied, 2)
            pe.wait_ge(own, 7)
            for n in range(4):
                last = nc.tensor.matmul(ps[2][:, n * P:n * P + P], att_bc[n][:, :], wt[n // 2][:, :],
                                        start=True, stop=True)
            last.then_inc(rows_up, 1)


def pieces(B, bank):
    first = bank * BANK
    return [(B["flat_psum"][:, first + a:first + b], slice(a, b)) for a, b in ((0, BANK), (BANK, HI))]


def counting(nc, B):
    with phase(nc) as ctx:
        def sb(name, shape, dt=F32):
            return ctx.enter_context(nc.sbuf_tensor(name, shape, dt))

        def sem(name):
            return semaphore(nc, ctx, name)
        ps = B["ps"]
        digits_i = sb("digits_i", [P, T], I32)
        lo = {k: sb(f"lo_{k}", [P, T + 4]) for k in "sd"}
        hi = {k: sb(f"hi_{k}", [P, T + 4]) for k in "sd"}
        iota_i = sb("iota_i", [P, HI], I32)
        iota16 = sb("iota16", [P, HI], F16)
        oh_lo = [sb(f"oh_lo{n}", [P, LO], F16) for n in range(4)]
        oh_hi = [sb(f"oh_hi{n}", [P, HI], F16) for n in range(4)]
        count = sb("count", [P, HI])
        upto = sb("upto", [P, HI])
        start = sb("start", [P, HI])
        ones_hi = sb("ones_hi", [P, HI])
        start_i = iota_i
        start_lo_i = sb("start_lo_i", [P, HI], I32)
        start_hi16, start_lo16 = sb("start_hi16", [P, HI], F16), sb("start_lo16", [P, HI], F16)
        offset = sb("offset", [P, 1])
        iota_pi = sb("iota_pi", [P, 1], I32)
        diag = [sb(f"diag{n}", [P, P], F16) for n in range(2)]
        lo_hot16 = [sb(f"lo_hot16_{n}", [P, P], F16) for n in range(4)]
        lo_hot = [sb(f"lo_hot{n}", [P, P]) for n in range(4)]
        twins = [sb(f"twins{n}", [P, P], F16) for n in range(4)]
        so_far = [sb(f"so_far{n}", [P, HI]) for n in range(2)]
        earlier = sb("earlier", [P, T])
        junk = [sb(f"junk_c{n}", [P, HI], F16) for n in range(2)]
        zero16 = sb("zero16", [P, BANK], F16)
        ring = [sb(f"x_ring{n}", [P, D]) for n in range(4)]
        place_i = sb("place_si", [P, T], I32)

        with phase(nc) as c2:
            made, own, ready, used, summed, ranked, start_up, stored = (
                semaphore(nc, c2, "c_" + n)
                for n in ("made", "own", "ready", "used", "summed", "ranked", "start_up", "stored"))
            block = c2.enter_context(nc.Block())

            @block.gpsimd
            def _(gp):
                gp.iota(iota_i[:, :], pattern=[[1, HI]], base=0, channel_multiplier=0).then_inc(made, 1)
                gp.iota(iota_pi[:, :], pattern=[[1, 1]], base=0, channel_multiplier=1).then_inc(made, 1)

            @block.vector
            def _(dve):
                fin = Finished(dve, own)
                dve.wait_ge(made, 2)
                nc.vector.tensor_copy(iota16[:, :], iota_i[:, :])
                nc.vector.tensor_copy(B["iota_p"][:, :], iota_pi[:, :])
                nc.vector.memset(ones_hi[:, :], 1.0)
                nc.vector.memset(zero16[:, :], 0.0)
                for k, key in (("s", B["src_key"]), ("d", B["dst_key"])):
                    nc.vector.memset(lo[k][:, T:T + 4], 0.0)
                    nc.vector.memset(hi[k][:, T:T + 4], 0.0)
                    fin.after(nc.vector.tensor_copy(digits_i[:, :], key[:, :]))
                    fin.after(nc.vector.tensor_single_scalar(place_i[:, :], digits_i[:, :], LO - 1, op=ALU.bitwise_and))
                    fin.after(nc.vector.tensor_copy(lo[k][:, 0:T], place_i[:, :]))
                    fin.after(nc.vector.tensor_single_scalar(place_i[:, :], digits_i[:, :], 7, op=ALU.logical_shift_right))
                    fin.after(nc.vector.tensor_copy(hi[k][:, 0:T], place_i[:, :]))

                def hot(t, slot):
                    dve.wait_ge(used, t + 1)
                    nc.vector.tensor_scalar(oh_lo[slot][:, :], iota16[:, 0:LO], lo["s"][:, bass.ds(t, 1)], None, ALU.is_equal)
                    nc.vector.tensor_scalar(oh_hi[slot][:, :], iota16[:, :], hi["s"][:, bass.ds(t, 1)], None, ALU.is_equal)\
                      .then_inc(ready, 1)
                with dve.Fori(0, T // 4, 1) as i:
                    for j in range(4):
                        hot(i * 4 + j, j)
                dve.wait_ge(summed, 1)
                for sums, his in pieces(B, 0):
                    fin.after(nc.vector.tensor_copy(count[:, his], sums))
                fin.after(nc.vector.tensor_tensor_scan(upto[:, :], ones_hi[:, :], count[:, :], 0.0, ALU.mult, ALU.add))
                dve.wait_ge(ranked, 1)
                fin.after(nc.vector.tensor_copy(offset[:, :], ps[2][:, 0:1]))
                fin.after(nc.vector.scalar_tensor_tensor(out=start[:, :], in0=upto[:, :], scalar=offset[:, 0:1],
                                                         in1=count[:, :], op0=ALU.add, op1=ALU.subtract))
                fin.after(nc.vector.tensor_scalar(upto[:, :], count[:, :], 0.0, None, ALU.is_gt))
                fin.after(nc.vector.scalar_tensor_tensor(out=start[:, :], in0=start[:, :], scalar=-float(ABSENT),
                                                         in1=upto[:, :], op0=ALU.add, op1=ALU.mult))
                fin.after(nc.vector.tensor_scalar(start[:, :], start[:, :], float(ABSENT), None, ALU.add))
                dve.sem_inc(start_up, 1)
                fin.after(nc.vector.tensor_copy(start_i[:, :], start[:, :]))
                fin.after(nc.vector.tensor_single_scalar(start_lo_i[:, :], start_i[:, :], 255, op=ALU.bitwise_and))
                fin.after(nc.vector.tensor_copy(upto[:, :], start_lo_i[:, :]))
                fin.after(nc.vector.tensor_copy(start_lo16[:, :], upto[:, :]))
                fin.after(nc.vector.tensor_tensor(start_hi16[:, :], start[:, :], upto[:, :], ALU.subtract))
                fin.after(nc.vector.scalar_tensor_tensor(out=earlier[:, :], in0=lo["d"][:, 0:T], scalar=float(HI),
                                                         in1=hi["d"][:, 0:T], op0=ALU.mult, op1=ALU.add))
                nc.vector.tensor_copy(place_i[:, :], earlier[:, :])

            @block.sync
            def _(sp):
                sp.wait_ge(start_up, 1)
                sp.dma_start(B["start_of"].rearrange("(p t) a -> p (t a)", p=P), start[:, :]).then_inc(stored, 16)
                sp.wait_ge(stored, 16)

            @block.tensor
            def _(pe):
                pe.sem_inc(used, 4)
                acc = pieces(B, 0)
                pe.wait_ge(own, 1)
                for sums, his in acc:
                    nc.tensor.matmul(sums, zero16[:, 0:P], zero16[:, 0:his.stop - his.start], start=True, stop=False)
                with pe.Fori(0, T // 4, 1) as i:
                    for j in range(4):
                        pe.wait_ge(ready, i * 4 + j + 1)
                        for sums, his in acc:
                            last = nc.tensor.matmul(sums, oh_lo[j][:, :], oh_hi[j][:, his], start=False, stop=False)
                        last.then_inc(used, 1)
                for sums, his in acc:
                    last = nc.tensor.matmul(sums, zero16[:, 0:P], zero16[:, 0:his.stop - his.start], start=False, stop=True)
                last.then_inc(summed, 1)
                pe.wait_ge(own, 13)
                nc.tensor.matmul(ps[2][:, 0:1], B["before"][:, :], upto[:, HI - 1:HI], start=True, stop=True)\
                  .then_inc(ranked, 1)

        with phase(nc) as c2:
            def sem2(name):
                return semaphore(nc, c2, name)
            own, diag_up, lo_up, hot_up, lo_hot_up, earlier_up, done = (
                sem2("r_" + n) for n in ("own", "diag", "lo", "hot", "lo_hot", "earlier", "done"))
            start_up, start_taken, count_up, count_taken = (
                sem2("r_" + n) for n in ("start_up", "start_taken", "count_up", "count_taken"))
            low_digits = ps[3][:, BANK - P:BANK]
            big_in = [sem2(f"r_big{n}") for n in range(4)]
            start_in = [sem2(f"r_start{n}") for n in range(4)]
            ring_in = [sem2(f"r_in{n}") for n in range(4)]
            ring_out = [sem2(f"r_out{n}") for n in range(4)]
            block = c2.enter_context(nc.Block())

            @block.gpsimd
            def _(gp):
                for t in range(T):
                    if t >= 4:
                        gp.wait_ge(big_in[t % 4], 16 * (t // 4))
                    gp.indirect_dma_start(out=B["big"][:, t, 0:D], out_offset=None, in_=B["x"],
                                          in_offset=bass.IndirectOffsetOnAxis(ap=B["src_gather"][:, t:t + 1], axis=0))\
                      .then_inc(big_in[t % 4], 16)
                for t in range(T):
                    if t >= 4:
                        gp.wait_ge(ring_out[t % 4], 16 * (t // 4))
                    gp.indirect_dma_start(out=ring[t % 4][:, :], out_offset=None, in_=B["x"],
                                          in_offset=bass.IndirectOffsetOnAxis(ap=B["dst_gather"][:, t:t + 1], axis=0))\
                      .then_inc(ring_in[t % 4], 16)
                for t in range(T):
                    if t >= 4:
                        gp.wait_ge(start_in[t % 4], 16 * (t // 4))
                    gp.indirect_dma_start(out=B["dst_start"][:, t:t + 1], out_offset=None, in_=B["start_of"],
                                          in_offset=bass.IndirectOffsetOnAxis(ap=place_i[:, t:t + 1], axis=0))\
                      .then_inc(start_in[t % 4], 16)
                for n in range(4):
                    gp.wait_ge(big_in[n], 16 * (T // 4))

            @block.sync
            def _(sp):
                table = B["x_dst"].rearrange("(p t) d -> p t d", t=T)
                with sp.Fori(0, T // 4, 1) as i:
                    for j in range(4):
                        sp.wait_ge(ring_in[j], i * 16 + 16)
                        sp.dma_start(table[:, bass.ds(i * 4 + j, 1), :], ring[j][:, :].rearrange("p (a d) -> p a d", a=1))\
                          .then_inc(ring_out[j], 16)
                for j in range(4):
                    sp.wait_ge(ring_out[j], 16 * (T // 4))

            @block.scalar
            def _(act):
                def digit(t, slot):
                    act.wait_ge(lo_up, t)
                    act.wait_ge(own, 1)
                    nc.scalar.activation(diag[slot][:, :], B["ident16"][:, :], ACT.Copy,
                                         scale=lo["s"][:, bass.ds(t, 1)]).then_inc(diag_up, 1)

                digit(0, 0)
                with act.Fori(0, T // 4, 1) as i:
                    for j in range(4):
                        t = i * 4 + j
                        digit(t + 1, (j + 1) % 2)
                        act.wait_ge(done, t + 1)
                        for sums, his in pieces(B, 0):
                            last = nc.scalar.activation(so_far[j % 2][:, his], sums, ACT.Copy)
                        last.then_inc(earlier_up, 1)
                digit(T + 1, 1)

            @block.tensor
            def _(pe):
                acc, at_start, at_count = pieces(B, 0), pieces(B, 2), [pieces(B, bank) for bank in (4, 6)]
                pe.wait_ge(own, 1)
                for sums, his in acc:
                    last = nc.tensor.matmul(sums, zero16[:, 0:P], zero16[:, 0:his.stop - his.start], start=True, stop=True)
                last.then_inc(done, 1)

                def low_row(t, slot):
                    pe.wait_ge(diag_up, t + 1)
                    nc.tensor.matmul(low_digits, B["ones16"][:, :], diag[slot][:, :], start=True, stop=True)\
                      .then_inc(lo_up, 1)

                low_row(0, 0)
                with pe.Fori(0, T // 4, 1) as i:
                    for j in range(4):
                        t, s = i * 4 + j, j % 2
                        pe.wait_ge(lo_hot_up, t + 1)
                        pe.wait_ge(start_taken, t + 1)
                        low_row(t + 1, 1 - s)
                        pe.wait_ge(hot_up, t + 1)
                        pe.wait_ge(earlier_up, t + 1)
                        for sums, his in acc:
                            last = nc.tensor.matmul(sums, oh_lo[j][:, :], oh_hi[j][:, his],
                                                    start=False, stop=True, skip_group_check=True)
                        last.then_inc(done, 1)
                        pe.wait_ge(lo_hot_up, t + 2)
                        for place, his in at_start:
                            nc.tensor.matmul(place, lo_hot16[j][:, :], start_hi16[:, his], start=True, stop=False)
                            last = nc.tensor.matmul(place, lo_hot16[j][:, :], start_lo16[:, his], start=False, stop=True)
                        last.then_inc(start_up, 1)
                        pe.wait_ge(count_taken, t + 1)
                        for place, his in at_count[s]:
                            nc.tensor.matmul(place, lo_hot[j][:, :], so_far[s][:, his], start=True, stop=False)
                            last = nc.tensor.matmul(place, twins[j][:, :], oh_hi[j][:, his], start=False, stop=True)
                        last.then_inc(count_up, 1)
                pe.wait_ge(lo_hot_up, T + 1)
                pe.wait_ge(start_taken, T + 1)
                low_row(T + 1, 1)

            @block.vector
            def _(dve):
                dve.sem_inc(lo_up, 1)
                dve.sem_inc(start_taken, 1)
                dve.sem_inc(count_taken, 2)
                dve.sem_inc(own, 1)

                def hot(t, slot):
                    col = bass.ds(t, 1)
                    nc.vector.tensor_scalar(oh_lo[slot][:, :], iota16[:, 0:LO], lo["s"][:, col], None, ALU.is_equal)
                    nc.vector.tensor_scalar(oh_hi[slot][:, :], iota16[:, :], hi["s"][:, col], None, ALU.is_equal)\
                      .then_inc(hot_up, 1)

                def low_hot(t, slot):
                    dve.wait_ge(lo_up, t + 2)
                    nc.vector.tensor_scalar(lo_hot16[slot][:, :], low_digits, B["iota_p"][:, 0:1], None, ALU.is_equal)
                    nc.vector.tensor_scalar(lo_hot[slot][:, :], low_digits, B["iota_p"][:, 0:1], None, ALU.is_equal)
                    nc.vector.scalar_tensor_tensor(out=twins[slot][:, :], in0=low_digits, scalar=lo["s"][:, bass.ds(t, 1)],
                                                   in1=B["before"][:, :], op0=ALU.is_equal, op1=ALU.mult)\
                      .then_inc(lo_hot_up, 1)

                def lookup(t, slot, target, bank, up, unused):
                    dve.wait_ge(up, t + 1)
                    return nc.vector.scalar_tensor_tensor(
                        out=unused[:, :], in0=B["flat_psum"][:, bank * BANK:bank * BANK + HI], scalar=1.0,
                        in1=oh_hi[slot][:, :], op0=ALU.mult, op1=ALU.mult, accum_out=target[:, bass.ds(t, 1)])

                for t in range(2):
                    hot(t, t)
                    low_hot(t, t)
                with dve.Fori(0, T // 4, 1) as i:
                    for j in range(4):
                        t = i * 4 + j
                        dve.wait_ge(start_taken, t + 1)
                        dve.wait_ge(hot_up, t + 1)
                        lookup(t, j, B["src_start"], 2, start_up, junk[0]).then_inc(start_taken, 1)
                        dve.wait_ge(count_taken, t + 2)
                        hot(t + 2, (j + 2) % 4)
                        low_hot(t + 2, (j + 2) % 4)
                        lookup(t, j, earlier, 4 + 2 * (j % 2), count_up, junk[1]).then_inc(count_taken, 1)
                fin = Finished(dve, own, 1)
                dve.wait_ge(start_taken, T + 1)
                dve.wait_ge(count_taken, T + 2)
                fin.after(nc.vector.tensor_tensor(B["src_place"][:, :], B["src_start"][:, :], earlier[:, :], ALU.add))
                nc.vector.tensor_scalar(B["src_place_i"][:, :], B["src_place"][:, :], 1.0, None, ALU.add)
                nc.vector.tensor_copy(B["src_start_i"][:, :], B["src_start"][:, :])
                for n in range(4):
                    dve.wait_ge(start_in[n], 16 * (T // 4))
                nc.vector.tensor_copy(B["dst_start_i"][:, :], B["dst_start"][:, :])


def propagate(dve, nc, B, o, fin, values, out, spare, sent, came, turn):
    q = B["orders"][o]
    fin.after(nc.vector.tensor_tensor(spare[:, :], values, q["new"][:, :], ALU.mult))
    fin.after(nc.vector.tensor_tensor_scan(out[:, :], q["same"][:, :], spare[:, :], 0.0, ALU.mult, ALU.add))
    nc.vector.tensor_tensor(spare[:, 0:1], out[:, T - 1:T], q["has_new"][:, :], ALU.mult).then_inc(sent, 1)
    dve.wait_ge(came, turn)
    fin.after(nc.vector.scalar_tensor_tensor(out=out[:, :], in0=q["runs"][:, :], scalar=B["ps"][turn][:, 0:1],
                                             in1=out[:, :], op0=ALU.mult, op1=ALU.add))


def propagate_pe(pe, nc, B, o, spare, sent, came, turn):
    pe.wait_ge(sent, turn)
    nc.tensor.matmul(B["ps"][turn][:, 0:1], B["orders"][o]["from_before"][:, :], spare[:, 0:1],
                     start=True, stop=True).then_inc(came, 1)


def order_flags(nc, B, o):
    q, ps = B["orders"][o], B["ps"]
    key = B["dst_key"] if o == "d" else B["s_key"]
    with phase(nc) as ctx:
        def sem(name):
            return semaphore(nc, ctx, name)
        own, cols_up, rows_up, sent, came = (sem(o + "_f_" + n) for n in ("own", "cols", "rows", "sent", "came"))
        diag_f = ctx.enter_context(nc.sbuf_tensor(o + "_diag_f", [P, P], F32))
        diag_l = ctx.enter_context(nc.sbuf_tensor(o + "_diag_l", [P, P], F32))
        ones_t = ctx.enter_context(nc.sbuf_tensor(o + "_ones_t", [P, T], F32))
        block = ctx.enter_context(nc.Block())
        first, last = key[:, 0:1], key[:, T - 1:T]

        @block.vector
        def _(dve):
            fin = Finished(dve, own)
            nc.vector.tensor_scalar(diag_f[:, :], B["ident"][:, :], first, None, ALU.mult)
            nc.vector.tensor_scalar(diag_l[:, :], B["ident"][:, :], last, None, ALU.mult).then_inc(cols_up, 1)
            nc.vector.memset(ones_t[:, :], 1.0)
            nc.vector.memset(q["next"][:, :], 0.0)
            nc.vector.tensor_tensor(q["same"][:, :], key[:, :], q["prev"][:, :], ALU.is_equal)
            fin.after(nc.vector.tensor_tensor(q["new"][:, :], key[:, :], q["prev"][:, :], ALU.not_equal))
            nc.vector.tensor_scalar(q["tail"][:, :], key[:, :], last, None, ALU.is_equal)
            nc.vector.tensor_copy(q["next"][:, 0:T - 1], q["same"][:, 1:T])
            fin.after(nc.vector.tensor_tensor_scan(q["runs"][:, :], q["same"][:, :], ones_t[:, :], 1.0, ALU.mult, ALU.mult))
            nc.vector.tensor_tensor(q["fix"][:, :], q["new"][:, :], q["tail"][:, :], ALU.mult)
            fin.after(nc.vector.tensor_scalar(q["has_new"][:, :], q["runs"][:, T - 1:T], -1.0, 1.0, ALU.mult, ALU.add))
            dve.wait_ge(rows_up, 1)
            for name, bank, col, side in (("from_before", 0, last, "before"), ("from_later", 1, first, "later"),
                                          ("sel_before", 1, first, "later"), ("sel_later", 0, last, "before")):
                step = nc.vector.scalar_tensor_tensor(out=q[name][:, :], in0=ps[bank][:, 0:P], scalar=col,
                                                      in1=B[side][:, :], op0=ALU.is_equal, op1=ALU.mult)
            fin.after(step)
            propagate(dve, nc, B, o, fin, B["place"][:, :], q["start"], B["tmp"][0], sent, came, 1)
            target = B["d_scatter"] if o == "d" else B["s_scatter"]
            fin.after(nc.vector.scalar_tensor_tensor(out=B["tmp"][1][:, :], in0=key[:, :], scalar=-float(PAD_KEY),
                                                     in1=q["new"][:, :], op0=ALU.add, op1=ALU.mult))
            fin.after(nc.vector.tensor_scalar(target[:, :], B["tmp"][1][:, :], float(PAD_KEY), None, ALU.add))

        @block.tensor
        def _(pe):
            pe.wait_ge(cols_up, 1)
            nc.tensor.matmul(ps[0][:, 0:P], B["ones"][:, :], diag_f[:, :], start=True, stop=True)
            nc.tensor.matmul(ps[1][:, 0:P], B["ones"][:, :], diag_l[:, :], start=True, stop=True).then_inc(rows_up, 1)
            pe.wait_ge(own, 4)
            propagate_pe(pe, nc, B, o, B["tmp"][0], sent, came, 1)


def edge_logits(dve, nc, B, fin, ai, aj, out, spare):
    fin.after(nc.vector.tensor_tensor(spare, ai, aj, ALU.add))
    fin.after(nc.vector.scalar_tensor_tensor(out=out, in0=spare, scalar=0.2, in1=spare, op0=ALU.mult, op1=ALU.max))


def running_sums(nc, B, o, scale, name):
    q, big = B["orders"][o], B["big"]
    with phase(nc) as ctx:
        def sem(n):
            return semaphore(nc, ctx, name + n)
        own, act_scaled, pool_scaled, summed, extra_up = (
            sem(n) for n in ("own", "act_scaled", "pool_scaled", "summed", "extra"))
        mask = ctx.enter_context(nc.sbuf_tensor(name + "mask", [P, PARTS, PT + 1], F32))
        block = ctx.enter_context(nc.Block())

        def scale_rows(v, part, first, last):
            a, b = part * PT + first, part * PT + last
            factor = scale[:, a:b].rearrange("p (t a) -> p t a", a=1).to_broadcast([P, b - a, D])
            return v.tensor_tensor(big[:, a:b, 0:D], big[:, a:b, 0:D], factor, ALU.mult)

        if scale is not None:
            @block.scalar
            def _(act):
                for part in reversed(range(PARTS)):
                    with act.Fori(0, (PT - POOL_END) // 4, 1) as i:
                        for j in range(4):
                            at = bass.ds(i * 4 + part * PT + POOL_END + j, 1)
                            nc.scalar.activation(row(big[:, at, 0:D]), row(big[:, at, 0:D]), ACT.Copy, scale=scale[:, at])\
                                .then_inc(act_scaled, 1)

            @block.gpsimd
            def _(gp):
                for part in reversed(range(PARTS)):
                    scale_rows(nc.gpsimd, part, DVE_END, POOL_END).then_inc(pool_scaled, 1)

        @block.vector
        def _(dve):
            fin = Finished(dve, own)
            nc.vector.memset(mask[:, :, PT], 0.0)
            fin.after(nc.vector.tensor_copy(mask[:, :, 0:PT], q["next"][:, :].rearrange("p (k t) -> p k t", t=PT)))
            for n, part in enumerate(reversed(range(PARTS))):
                if scale is not None:
                    fin.after(scale_rows(nc.vector, part, 0, DVE_END))
                    dve.wait_ge(act_scaled, (n + 1) * (PT - POOL_END))
                    dve.wait_ge(pool_scaled, n + 1)
                a = part * PT
                goes_on = mask[:, part, ::-1]
                for d in range(130):
                        column = big[:, a:a + PT + 1, d][:, ::-1]
                        nc.vector.tensor_tensor_scan(column, goes_on, column, 0.0, ALU.mult, ALU.add).then_inc(summed, 1)
                dve.wait_ge(summed, 130 * (n + 1))
            dve.wait_ge(extra_up, 1)
            nc.vector.tensor_copy(q["extra"][:, :], B["ps"][0][:, 0:W])

        @block.tensor
        def _(pe):
            pe.wait_ge(summed, 130 * PARTS)
            nc.tensor.matmul(B["ps"][0][:, 0:W], q["from_later"][:, :], big[:, 0, :], start=True, stop=True)\
              .then_inc(extra_up, 1)


def conv_edges(nc, B, layer):
    q, big, ps = B["orders"]["d"], B["big"], B["ps"]
    ai, aj, top, ex, tmp = B["ai"], B["aj"], B["top"], B["ex"], B["tmp"]
    with phase(nc) as ctx:
        def sem(n):
            return semaphore(nc, ctx, f"e{layer}_" + n)
        if layer == 0:
            inn, free = [sem(f"in{n}") for n in range(2)], sem("free")
            ring = [ctx.enter_context(nc.sbuf_tensor(f"xd{n}", [P, G, D], F32)) for n in range(2)]
            junk = [ctx.enter_context(nc.sbuf_tensor(f"e_junk{n}", [P, G, D], F32)) for n in range(2)]
            ai_up = sem("ai_up")
            block = ctx.enter_context(nc.Block())

            @block.sync
            def _(sp):
                table = B["x_dst"].rearrange("(p t) d -> p t d", t=T)

                def load(c, slot, last):
                    sp.wait_ge(free, c + 1)
                    sp.dma_start(ring[slot][:, :, :], table[:, bass.ds(c * G, G), :]).then_inc(inn[slot], 16)
                over_chunks(sp, load)

            @block.vector
            def _(dve):
                dve.sem_inc(free, 2)
                dve.sem_inc(ai_up, 1)

                def dots(c, slot, last):
                    dve.wait_ge(ai_up, c + 1)
                    for g in range(G):
                        at = bass.ds(c * G + g, 1)
                        ins = nc.vector.scalar_tensor_tensor(out=junk[0][:, g, :], in0=row(big[:, at, 0:D]), scalar=1.0,
                                                       in1=B["rows_"]["wi1"][:, :], op0=ALU.mult, op1=ALU.mult,
                                                       accum_out=ai[:, at])
                    ins.then_inc(ai_up, 1)
                    dve.wait_ge(free, c + 2)
                    dve.wait_ge(inn[slot], c * 8 + (16 if slot == 0 else 8))
                    for g in range(G):
                        at = bass.ds(c * G + g, 1)
                        ins = nc.vector.scalar_tensor_tensor(out=junk[1][:, g, :], in0=ring[slot][:, g, :], scalar=1.0,
                                                             in1=B["rows_"]["wj1"][:, :], op0=ALU.mult, op1=ALU.mult,
                                                             accum_out=aj[:, at])
                    ins.then_inc(free, 1)
                over_chunks(dve, dots)
        else:
            rows_in = [sem(f"rows{n}") for n in range(4)]
            aj_in = [sem(f"aj{n}") for n in range(4)]
            bare = BareRows(nc, ctx, B, "c1")
            block = ctx.enter_context(nc.Block())

            @block.vector
            def _(dve):
                bare.vector(dve)

            @block.scalar
            def _(act):
                bare.scalar(act)

            @block.tensor
            def _(pe):
                bare.tensor(pe)

            @block.sync
            def _(sp):
                bare.sync(sp)

            @block.gpsimd
            def _(gp):
                for t in range(T):
                    if t >= 4:
                        gp.wait_ge(rows_in[t % 4], 16 * (t // 4))
                        gp.wait_ge(aj_in[t % 4], 16 * (t // 4))
                    gp.indirect_dma_start(out=big[:, t, :], out_offset=None, in_=B["hidden"],
                                          in_offset=bass.IndirectOffsetOnAxis(ap=B["src_start_i"][:, t:t + 1], axis=0))\
                      .then_inc(rows_in[t % 4], 16)
                    gp.indirect_dma_start(out=aj[:, t:t + 1], out_offset=None, in_=B["hidden_aj"],
                                          in_offset=bass.IndirectOffsetOnAxis(ap=B["dst_start_i"][:, t:t + 1], axis=0))\
                      .then_inc(aj_in[t % 4], 16)
                for n in range(4):
                    gp.wait_ge(rows_in[n], 16 * (T // 4))
                    gp.wait_ge(aj_in[n], 16 * (T // 4))

    with phase(nc) as ctx:
        def sem(n):
            return semaphore(nc, ctx, f"m{layer}_" + n)
        own, cols_up, rows_up, shifted, exp_up = (sem(n) for n in ("own", "cols", "rows", "shifted", "exp"))
        diag = [ctx.enter_context(nc.sbuf_tensor(f"m{layer}_diag{n}", [P, P], F32)) for n in range(2)]
        masked = [ctx.enter_context(nc.sbuf_tensor(f"m{layer}_masked{n}", [P, P], F32)) for n in range(2)]
        most = ctx.enter_context(nc.sbuf_tensor(f"m{layer}_most", [P, 2], F32))
        block = ctx.enter_context(nc.Block())

        @block.vector
        def _(dve):
            fin = Finished(dve, own)
            if layer == 1:
                fin.after(nc.vector.tensor_copy(ai[:, :], big[:, 0:T, D]))
            edge_logits(dve, nc, B, fin, ai[:, :], aj[:, :], ex[:, :], tmp[0][:, :])
            nc.vector.tensor_scalar(tmp[0][:, :], q["same"][:, :], 1.0, HUGE, ALU.subtract, ALU.mult)
            fin.after(nc.vector.tensor_scalar(tmp[1][:, :], q["next"][:, :], 1.0, HUGE, ALU.subtract, ALU.mult))
            fin.after(nc.vector.tensor_tensor_scan(tmp[2][:, :], tmp[0][:, :], ex[:, :], -HUGE, ALU.add, ALU.max))
            fin.after(nc.vector.tensor_tensor_scan(top[:, ::-1], tmp[1][:, ::-1], tmp[2][:, ::-1], -HUGE, ALU.add, ALU.max))
            nc.vector.tensor_scalar(diag[0][:, :], B["ident"][:, :], tmp[2][:, T - 1:T], None, ALU.mult)
            nc.vector.tensor_scalar(diag[1][:, :], B["ident"][:, :], top[:, 0:1], None, ALU.mult).then_inc(cols_up, 1)
            nc.vector.tensor_scalar(masked[0][:, :], q["sel_before"][:, :], 1.0, HUGE, ALU.subtract, ALU.mult)
            fin.after(nc.vector.tensor_scalar(masked[1][:, :], q["sel_later"][:, :], 1.0, HUGE, ALU.subtract, ALU.mult))
            dve.wait_ge(rows_up, 1)
            nc.vector.tensor_tensor(masked[0][:, :], ps[0][:, 0:P], masked[0][:, :], ALU.add)
            fin.after(nc.vector.tensor_tensor(masked[1][:, :], ps[1][:, 0:P], masked[1][:, :], ALU.add))
            nc.vector.reduce_max(most[:, 0:1], masked[0][:, :], AX.X)
            nc.vector.reduce_max(most[:, 1:2], masked[1][:, :], AX.X)
            nc.vector.tensor_scalar(tmp[0][:, :], B["dst_key"][:, :], B["dst_key"][:, 0:1], None, ALU.is_equal)
            fin.after(nc.vector.tensor_scalar(tmp[1][:, :], q["tail"][:, :], 1.0, HUGE, ALU.subtract, ALU.mult))
            fin.after(nc.vector.tensor_scalar(tmp[0][:, :], tmp[0][:, :], 1.0, HUGE, ALU.subtract, ALU.mult))
            for n in range(2):
                fin.after(nc.vector.scalar_tensor_tensor(out=top[:, :], in0=tmp[n][:, :], scalar=most[:, n:n + 1],
                                                         in1=top[:, :], op0=ALU.add, op1=ALU.max))
            nc.vector.tensor_tensor(tmp[3][:, :], ex[:, :], top[:, :], ALU.subtract).then_inc(shifted, 1)
            nc.vector.tensor_copy(big[:, 0:T, 130], top[:, :])
            nc.vector.tensor_copy(big[:, 0:T, 131], aj[:, :])
            nc.vector.memset(big[:, 0:T, 129], 1.0)
            dve.wait_ge(exp_up, 1)
            fin.after(nc.vector.tensor_copy(big[:, 0:T, D], ex[:, :]))

        @block.tensor
        def _(pe):
            pe.wait_ge(cols_up, 1)
            for n in range(2):
                last = nc.tensor.matmul(ps[n][:, 0:P], B["ones"][:, :], diag[n][:, :], start=True, stop=True)
            last.then_inc(rows_up, 1)

        @block.scalar
        def _(act):
            act.wait_ge(shifted, 1)
            nc.scalar.activation(ex[:, :], tmp[3][:, :], ACT.Exp).then_inc(exp_up, 1)

    running_sums(nc, B, "d", ex, f"se{layer}_")

    with phase(nc) as ctx:
        fixed, stored = (semaphore(nc, ctx, n) for n in (f"w{layer}_fixed", f"w{layer}_stored"))
        block = ctx.enter_context(nc.Block())

        @block.vector
        def _(dve):
            with dve.Fori(0, T // 14, 1) as i:
                for j in range(14):
                    t = i * 14 + j
                    nc.vector.scalar_tensor_tensor(
                        out=row(big[:, bass.ds(t, 1), 0:130]), in0=q["extra"][:, 0:130], scalar=q["fix"][:, bass.ds(t, 1)],
                        in1=row(big[:, bass.ds(t, 1), 0:130]), op0=ALU.mult, op1=ALU.add).then_inc(fixed, 1)

        if layer == 1:
            @block.sync
            def _(sp):
                store_sums(sp, B, layer, stored, fixed)
                sp.wait_ge(stored, 16 * 7)


def store_sums(sp, B, layer, stored, fixed=None):
    table = B["sums"][layer].rearrange("(p t) d -> p t d", t=T)
    part = T // 7
    for c in range(7):
        if fixed is not None:
            sp.wait_ge(fixed, part * (c + 1))
        sp.dma_start(table[:, part * c:part * c + part, :], B["big"][:, part * c:part * c + part, :]).then_inc(stored, 16)


def by_source(nc, B):
    with phase(nc) as ctx:
        def sem(n):
            return semaphore(nc, ctx, "b_" + n)
        own, packed, edged, loaded, stored = (sem(n) for n in ("own", "packed", "edged", "loaded", "stored"))
        sent = [sem(f"sent{n}") for n in range(4)]
        rec = ctx.enter_context(nc.sbuf_tensor("rec", [P, T, 4], F32))
        back = ctx.enter_context(nc.sbuf_tensor("back", [P, T, 4], F32))
        prev = rec
        front = ctx.enter_context(nc.sbuf_tensor("front", [1, 4], F32))
        bare = BareRows(nc, ctx, B, "b")
        block = ctx.enter_context(nc.Block())
        table = B["record"]

        @block.vector
        def _(dve):
            fin = Finished(dve, own)
            nc.vector.memset(front[:, :], -1.0)
            fin.after(nc.vector.memset(rec[:, :, :], 0.0))
            nc.vector.tensor_copy(rec[:, :, 0], B["orders"]["d"]["start"][:, :])
            nc.vector.tensor_copy(rec[:, :, 2], B["ai"][:, :])
            nc.vector.tensor_copy(rec[:, :, 1], B["src_key"][:, :]).then_inc(packed, 1)
            bare.vector(dve)
            dve.wait_ge(loaded, 32)
            nc.vector.tensor_copy(B["ai"][:, :], back[:, :, 2])
            nc.vector.tensor_copy(B["s_key"][:, :], back[:, :, 1])
            nc.vector.tensor_copy(B["s_dstart_i"][:, :], back[:, :, 0])
            nc.vector.tensor_copy(B["orders"]["s"]["prev"][:, :], prev[:, :, 1])
            nc.vector.tensor_scalar(B["s_gather"][:, :], back[:, :, 1], float(N - 1), None, ALU.min)

        @block.gpsimd
        def _(gp):
            gp.wait_ge(packed, 1)
            for t in range(T):
                if t >= 4:
                    gp.wait_ge(sent[t % 4], 16 * (t // 4))
                gp.indirect_dma_start(out=table, out_offset=bass.IndirectOffsetOnAxis(ap=B["src_place_i"][:, t:t + 1], axis=0),
                                      in_=rec[:, t, :], in_offset=None).then_inc(sent[t % 4], 16)

        @block.scalar
        def _(act):
            bare.scalar(act)

        @block.tensor
        def _(pe):
            bare.tensor(pe)

        @block.sync
        def _(sp):
            sp.wait_ge(own, 1)
            sp.dma_start(table[0:1, :], front[:, :]).then_inc(edged, 16)
            store_sums(sp, B, 0, stored)
            bare.sync(sp)
            sp.wait_ge(stored, 16 * 7)
            sp.wait_ge(edged, 16)
            for n in range(4):
                sp.wait_ge(sent[n], 16 * (T // 4))
            sp.dma_start(back[:, :, :], table[1:EP + 1, :].rearrange("(p t) c -> p t c", t=T)).then_inc(loaded, 16)
            sp.dma_start(prev[:, :, :], table[0:EP, :].rearrange("(p t) c -> p t c", t=T)).then_inc(loaded, 16)


def conv_nodes(nc, B, layer):
    q, big, ps, tmp = B["orders"]["s"], B["big"], B["ps"], B["tmp"]
    ai, coef, top, ex = B["ai"], B["coef"], B["top"], B["ex"]
    with phase(nc) as ctx:
        def sem(n):
            return semaphore(nc, ctx, f"n{layer}_" + n)
        big_in = [sem(f"big{n}") for n in range(4)]
        bare = BareRows(nc, ctx, B, f"n{layer}")
        block = ctx.enter_context(nc.Block())

        @block.gpsimd
        def _(gp):
            for t in range(T):
                if t >= 4:
                    gp.wait_ge(big_in[t % 4], 16 * (t // 4))
                gp.indirect_dma_start(out=big[:, t, :], out_offset=None, in_=B["sums"][layer],
                                      in_offset=bass.IndirectOffsetOnAxis(ap=B["s_dstart_i"][:, t:t + 1], axis=0))\
                  .then_inc(big_in[t % 4], 16)
            for n in range(4):
                gp.wait_ge(big_in[n], 16 * (T // 4))

        @block.vector
        def _(dve):
            bare.vector(dve)

        @block.scalar
        def _(act):
            bare.scalar(act)

        @block.tensor
        def _(pe):
            bare.tensor(pe)

        @block.sync
        def _(sp):
            bare.sync(sp)

    with phase(nc) as ctx:
        def sem(n):
            return semaphore(nc, ctx, f"a{layer}_" + n)
        own, shifted, exp_up, sent, came = (sem(n) for n in ("own", "shifted", "exp", "sent", "came"))
        block = ctx.enter_context(nc.Block())

        @block.vector
        def _(dve):
            fin = Finished(dve, own)
            if layer == 1:
                propagate(dve, nc, B, "s", fin, B["ai2_s"][:, :], ai, tmp[2], sent, came, 1)
            edge_logits(dve, nc, B, fin, ai[:, :], big[:, 0:T, 131], ex[:, :], tmp[0][:, :])
            nc.vector.tensor_tensor(tmp[1][:, :], ex[:, :], big[:, 0:T, 130], ALU.subtract).then_inc(shifted, 1)
            fin.after(nc.vector.tensor_scalar(tmp[0][:, :], big[:, 0:T, D], 1e-16, None, ALU.add))
            fin.after(nc.vector.tensor_tensor(tmp[0][:, :], tmp[0][:, :], tmp[0][:, :], ALU.mult))
            fin.after(nc.vector.tensor_tensor(tmp[0][:, :], tmp[0][:, :], big[:, 0:T, 129], ALU.mult))
            fin.after(nc.vector.reciprocal(tmp[3][:, :], tmp[0][:, :]))
            nc.vector.memset(big[:, 0:T, 129], 1.0)
            dve.wait_ge(exp_up, 1)
            fin.after(nc.vector.tensor_tensor(coef[:, :], ex[:, :], tmp[3][:, :], ALU.mult))

        @block.scalar
        def _(act):
            act.wait_ge(shifted, 1)
            nc.scalar.activation(ex[:, :], tmp[1][:, :], ACT.Exp).then_inc(exp_up, 1)

        if layer == 1:
            @block.tensor
            def _(pe):
                propagate_pe(pe, nc, B, "s", tmp[2], sent, came, 1)

    running_sums(nc, B, "s", coef, f"sn{layer}_")
    if layer == 0:
        first_rows(nc, B)
    else:
        second_rows(nc, B)


def bank_rows(ps, first):
    return [ps[first + g // 4][:, (g % 4) * D:(g % 4) * D + D] for g in range(G)]


def fix_step(nc, B, o, dest, t):
    q = B["orders"][o]
    return nc.vector.scalar_tensor_tensor(
        out=dest, in0=q["extra"][:, 0:130], scalar=q["fix"][:, bass.ds(t, 1)],
        in1=row(B["big"][:, bass.ds(t, 1), 0:130]), op0=ALU.mult, op1=ALU.add)


def first_rows(nc, B):
    ps, rows_ = B["ps"], B["rows_"]
    with phase(nc) as ctx:
        def sem(n):
            return semaphore(nc, ctx, "h_" + n)

        def sb(n, shape):
            return ctx.enter_context(nc.sbuf_tensor("h_" + n, shape, F32))
        own, fixed, turned, copied, product, biased, active, dotted = (
            sem(n) for n in ("own", "fixed", "turned", "copied", "product", "biased", "active", "dotted"))
        stored = [sem(f"stored{n}") for n in range(2)]
        aj_stored, kept = sem("aj_stored"), sem("kept")
        full = [sb(f"full{n}", [P, G, W]) for n in range(2)]
        flipped = [sb(f"flipped{n}", [P, G * D]) for n in range(2)]
        inverse = [sb(f"inverse{n}", [P, G]) for n in range(2)]
        pre = [sb(f"pre{n}", [P, G, D]) for n in range(2)]
        below = [sb(f"below{n}", [P, G, D]) for n in range(2)]
        hid = [sb(f"hid{n}", [P, G, W]) for n in range(2)]
        junk = sb("junk", [P, 2 * G, D])
        aj_s = sb("aj_s", [P, T])
        block = ctx.enter_context(nc.Block())

        @block.vector
        def _(dve):
            fin = Finished(dve, own)
            nc.vector.memset(hid[0][:, :, :], 0.0)
            fin.after(nc.vector.memset(hid[1][:, :, :], 0.0))

            def body(c, pair, slot, live):
                newest, second, third = live
                other = 1 - slot
                if newest:
                    wait(dve, turned, c - 1)
                    for g in range(G):
                        ins = fix_step(nc, B, "s", full[slot][:, g, 0:130], c * G + g)
                    ins.then_inc(fixed, 1)
                if third:
                    dve.wait_ge(active, c - 1)
                    dve.wait_ge(biased, c - 1)
                    wait(dve, stored[slot], (pair - 1) * 16)
                    wait(dve, kept, c - 2)
                    fin.after(nc.vector.scalar_tensor_tensor(out=hid[slot][:, :, 0:D], in0=below[slot][:, :, :],
                                                             scalar=B["drop"][:, 0:1], in1=pre[slot][:, :, :],
                                                             op0=ALU.mult, op1=ALU.add))
                    for g in range(G):
                        at = bass.ds(c * G + (g - 2 * G), 1)
                        nc.vector.scalar_tensor_tensor(
                            out=junk[:, 2 * g, :], in0=hid[slot][:, g, 0:D], scalar=1.0, in1=rows_["wj2"][:, :],
                            op0=ALU.mult, op1=ALU.mult, accum_out=aj_s[:, at])
                        ins = nc.vector.scalar_tensor_tensor(
                            out=junk[:, 2 * g + 1, :], in0=hid[slot][:, g, 0:D], scalar=1.0, in1=rows_["wi2"][:, :],
                            op0=ALU.mult, op1=ALU.mult, accum_out=hid[slot][:, g, D:D + 1])
                    ins.then_inc(dotted, 1)
                    dve.wait_ge(dotted, c - 1)
                    nc.vector.tensor_copy(B["ai2_s"][:, bass.ds(c * G - 2 * G, G)], hid[slot][:, :, D]).then_inc(kept, 1)
                if second:
                    dve.wait_ge(fixed, c)
                    fin.after(nc.vector.reciprocal(inverse[other][:, :], full[other][:, :, 129]))
                    dve.wait_ge(product, c)
                    for g, o in enumerate(bank_rows(ps, 4 + 2 * other)):
                        ins = nc.vector.scalar_tensor_tensor(
                            out=pre[other][:, g, :], in0=o, scalar=inverse[other][:, g:g + 1],
                            in1=rows_["b1"][:, :], op0=ALU.mult, op1=ALU.add)
                    ins.then_inc(biased, 1)
            turns(dve, C, 2, body, [(fin, 2)])

        @block.tensor
        def _(pe):
            def body(c, pair, slot, live):
                if not live[0]:
                    return
                pe.wait_ge(fixed, c + 1)
                for g, o in enumerate(bank_rows(ps, 2 * slot)):
                    ins = nc.tensor.transpose(o, full[slot][:, g, 0:D], B["ident"][:, :])
                ins.then_inc(turned, 1)
                pe.wait_ge(copied, c + 1)
                wait(pe, biased, c - 1)
                for g, o in enumerate(bank_rows(ps, 4 + 2 * slot)):
                    ins = nc.tensor.matmul(o, flipped[slot][:, g * D:g * D + D], B["w1s"][:, :], start=True, stop=True)
                ins.then_inc(product, 1)
            turns(pe, C, 2, body)

        @block.scalar
        def _(act):
            def body(c, pair, slot, live):
                other = 1 - slot
                if live[0]:
                    act.wait_ge(turned, c + 1)
                    wait(act, product, c - 1)
                    nc.scalar.activation(flipped[slot][:, 0:4 * D], ps[2 * slot][:, 0:4 * D], ACT.Copy)
                    nc.scalar.activation(flipped[slot][:, 4 * D:G * D], ps[2 * slot + 1][:, 0:3 * D], ACT.Copy)\
                        .then_inc(copied, 1)
                if live[1]:
                    act.wait_ge(biased, c)
                    nc.scalar.activation(below[other][:, :, :], pre[other][:, :, :], ACT.Relu, scale=-1.0)\
                        .then_inc(active, 1)
            turns(act, C, 2, body)

        @block.sync
        def _(sp):
            table = B["hidden"][0:EP, :].rearrange("(p t) c -> p t c", t=T)

            def body(c, slot, last):
                sp.wait_ge(dotted, c + 1)
                sp.dma_start(table[:, bass.ds(c * G, G), :], hid[slot][:, :, :]).then_inc(stored[slot], 16)
            over_chunks(sp, body)
            sp.dma_start(B["hidden_aj"][0:EP, :].rearrange("(p t) c -> p (t c)", t=T), aj_s[:, :]).then_inc(aj_stored, 16)
            sp.wait_ge(aj_stored, 16)
            for n in range(2):
                sp.wait_ge(stored[n], 16 * (C // 2))


def wide(ap, g):
    return ap.rearrange("p (a d) -> p a d", a=1).to_broadcast([ap.shape[0], g, D])


class BareRows:

    def __init__(self, nc, ctx, B, name):
        self.nc, self.B, self.n = nc, B, BARE_CHUNKS[name]
        order = list(BARE_CHUNKS)
        assert sum(BARE_CHUNKS.values()) == DC and self.n % 2 == 0
        self.first = sum(BARE_CHUNKS[k] for k in order[:order.index(name)])

        def sem(n):
            return semaphore(nc, ctx, f"z{name}_" + n)

        def sb(n, shape):
            return ctx.enter_context(nc.sbuf_tensor(f"z{name}_" + n, shape, F32))
        self.own, self.act_own, self.x_free, self.below_up, self.clipped, self.mean_up, self.var_up = (
            sem(n) for n in ("own", "act_own", "x_free", "below_up", "clipped", "mean_up", "var_up"))
        self.roots_up, self.roots_turned, self.roots_row, self.factor_up, self.u_up, self.u_var_up, self.done, self.spread_up = (
            sem(n) for n in ("roots_up", "roots_turned", "roots_row", "factor_up", "u_up", "u_var_up", "done", "spread_up"))
        self.x_in, self.stored = ([sem(f"{n}{k}") for k in range(2)] for n in ("x_in", "stored"))
        self.x, self.v, self.result = ([sb(f"{n}{k}", [DP, DG, D]) for k in range(2)] for n in ("x", "v", "result"))
        self.below = sb("below", [DP, DG, D])
        self.factor, self.unused = ([B["ps"][first + g // 4][0:DP, (g % 4) * D:(g % 4) * D + D] for g in range(DG)]
                                    for first in (0, 3))
        self.mean = [sb(f"mean{k}", [DP, DG]) for k in range(2)]
        self.sum, self.squares, self.u_sum, self.u_mean, self.u_squares, self.u_dev, self.u_inv = (
            sb(n, [DP, DG]) for n in ("sum", "squares", "u_sum", "u_mean", "u_squares", "u_dev", "u_inv"))
        self.dev, self.inv = sb("dev", [DP, 2, DG]), sb("inv", [DP, 4, 32])
        self.spread, self.inv_row = sb("spread", [P, DG, D]), sb("inv_row", [P, DP])

    def vector(self, dve):
        v, B = self.nc.vector, self.B
        fin = Finished(dve, self.own)
        b2, beta = B["rows_"]["b2"][0:DP, :], B["rows_"]["beta"][0:DP, :]
        v.memset(self.inv[:, :, :], 0.0)
        v.memset(self.spread[64:P, :, :], 0.0)
        for g in range(DG):
            v.tensor_scalar(self.spread[0:32, g, :], B["ones"][0:32, :], B["ident"][0:32, g:g + 1], None, ALU.mult)
            ins = v.tensor_scalar(self.spread[32:64, g, :], B["rows_"]["gamma"][32:64, :], B["ident"][32:64, 32 + g:33 + g],
                                  None, ALU.mult)
        ins.then_inc(self.spread_up, 1)
        dve.wait_ge(self.spread_up, 1)

        def body(c, pair, slot, live):
            ahead, new, middle, old = live
            other = 1 - slot
            if new:
                v.scalar_tensor_tensor(out=self.v[other][:, :, :], in0=self.x[other][:, :, :], scalar=2.0, in1=wide(b2, DG),
                                       op0=ALU.mult, op1=ALU.add).then_inc(self.x_free, 1)
            if middle:
                dve.wait_ge(self.var_up, c - 1)
                v.reciprocal(self.inv[:, 0:2, 0:DG], self.dev[:, :, :]).then_inc(self.roots_up, 1)
            if new:
                dve.wait_ge(self.clipped, c)
                dve.wait_ge(self.x_free, c)
                for g in range(DG):
                    ins = v.scalar_tensor_tensor(out=self.v[other][:, g, :], in0=self.below[:, g, :],
                                                 scalar=B["drop"][0:DP, 0:1], in1=self.v[other][:, g, :],
                                                 op0=ALU.mult, op1=ALU.add, accum_out=self.sum[:, g:g + 1])
                fin.after(ins)
                v.tensor_scalar(self.mean[other][:, :], self.sum[:, :], -1.0 / D, None, ALU.mult).then_inc(self.mean_up, 1)
                dve.wait_ge(self.mean_up, c)
            if ahead:
                dve.wait_ge(self.x_in[slot], pair * 16 + 16)
                v.tensor_tensor(self.below[:, :, :], self.x[slot][:, :, :], wide(b2, DG), ALU.add).then_inc(self.below_up, 1)
            if old:
                dve.wait_ge(self.u_var_up, c - 2)
                fin.after(v.reciprocal(self.u_inv[:, :], self.u_dev[:, :]))
                result = self.result[other]
                for g in range(DG):
                    ins = v.tensor_scalar(result[:, g, :], result[:, g, :], self.u_mean[:, g:g + 1],
                                          self.u_inv[:, g:g + 1], ALU.add, ALU.mult)
                ins.then_inc(self.done, 1)
            if middle:
                dve.wait_ge(self.factor_up, c - 1)
                if old:
                    dve.wait_ge(self.done, c - 2)
                wait(dve, self.stored[slot], (pair - 1) * 16)
                u = self.result[slot]
                for g in range(DG):
                    ins = v.scalar_tensor_tensor(out=u[:, g, :], in0=self.v[slot][:, g, :], scalar=self.mean[slot][:, g:g + 1],
                                                 in1=self.factor[g], op0=ALU.add, op1=ALU.mult,
                                                 accum_out=self.u_sum[:, g:g + 1])
                fin.after(ins)
                v.tensor_tensor(u[:, :, :], u[:, :, :], wide(beta, DG), ALU.add)
                v.tensor_scalar(self.u_mean[:, :], self.u_sum[:, :], -1.0 / D, B["beta_mean"][0:DP, 0:1], ALU.mult,
                                ALU.subtract).then_inc(self.u_up, 1)
        turns(dve, self.n, 3, body, [(fin, 3)])

    def scalar(self, act):
        a, B = self.nc.scalar, self.B
        fin = Finished(act, self.act_own)
        eps, eps_sq = B["eps"][0:DP, 0:1], B["eps_sq"][0:DP, 0:1]

        def body(c, pair, slot, live):
            ahead, new, middle, old = live
            other = 1 - slot
            if middle:
                act.wait_ge(self.roots_turned, c - 1)
                a.activation(self.inv_row[:, :], B["ps"][6][:, 0:DP], ACT.Copy).then_inc(self.roots_row, 1)
            if new:
                act.wait_ge(self.mean_up, c)
                squares(self.nc, fin, self.v[other], self.mean[other], self.unused, self.squares)
                a.activation(self.dev[:, 0, :], self.squares[:, :], ACT.Sqrt, bias=eps, scale=1.0 / D)
                a.activation(self.dev[:, 1, :], self.squares[:, :], ACT.Sqrt, bias=eps_sq, scale=(1.0 + EPS) / D)\
                    .then_inc(self.var_up, 1)
                act.wait_ge(self.var_up, c)
            if ahead:
                act.wait_ge(self.below_up, c + 1)
                a.activation(self.below[:, :, :], self.below[:, :, :], ACT.Relu, scale=-1.0).then_inc(self.clipped, 1)
            if middle:
                act.wait_ge(self.u_up, c - 1)
                squares(self.nc, fin, self.result[slot], self.u_mean, self.unused, self.u_squares)
                a.activation(self.u_dev[:, :], self.u_squares[:, :], ACT.Sqrt, bias=eps, scale=1.0 / D)\
                    .then_inc(self.u_var_up, 1)
        turns(act, self.n, 3, body, [(fin, 2)])

    def tensor(self, pe):
        t, ps = self.nc.tensor, self.B["ps"]
        pe.wait_ge(self.spread_up, 1)

        def body(c, pair, slot, live):
            if not live[2]:
                return
            pe.wait_ge(self.roots_up, c - 1)
            t.transpose(ps[6][:, 0:DP], self.inv[:, :, :].rearrange("p k g -> p (k g)"), self.B["ident"][0:DP, 0:DP])\
             .then_inc(self.roots_turned, 1)
            pe.wait_ge(self.roots_row, c - 1)
            for bank in range(3):
                first, last = bank * 4, min(bank * 4 + 4, DG)
                ins = t.matmul(ps[bank][0:DP, 0:(last - first) * D], self.inv_row[:, :],
                               self.spread[:, first:last, :].rearrange("p g d -> p (g d)"), start=True, stop=True)
            ins.then_inc(self.factor_up, 1)
        turns(pe, self.n, 3, body)

    def sync(self, sp):
        rows = DP * DG

        def at(table, c):
            flat = table[self.first * rows:(self.first + self.n) * rows, :].rearrange("(c p g) d -> c p g d", p=DP, g=DG)
            return flat[bass.ds(c, 1), :, :, :].rearrange("c p g d -> (c p) g d")

        def load(c, slot):
            sp.dma_start(self.x[slot][:, :, :], at(self.B["x"], c)).then_inc(self.x_in[slot], 16)

        def store(c, slot):
            sp.wait_ge(self.done, c + 1)
            sp.dma_start(at(self.B["out"], c), self.result[slot][:, :, :]).then_inc(self.stored[slot], 16)
        def load_and_store(c, slot):
            sp.wait_ge(self.x_free, c + 2)
            load(c + 3, 1 - slot)
            store(c, slot)
        load(0, 0)
        load(1, 1)
        sp.wait_ge(self.x_free, 1)
        load(2, 0)
        with sp.Fori(0, self.n // 2 - 2, 1) as i:
            for slot in range(2):
                load_and_store(i * 2 + slot, slot)
        load_and_store(self.n - 4, 0)
        for c in range(self.n - 3, self.n):
            store(c, c % 2)
        for slot in range(2):
            sp.wait_ge(self.stored[slot], 16 * (self.n // 2))


def second_rows(nc, B):
    ps, rows_ = B["ps"], B["rows_"]
    with phase(nc) as ctx:
        def sem(n):
            return semaphore(nc, ctx, "g_" + n)

        def sb(n, shape):
            return ctx.enter_context(nc.sbuf_tensor("g_" + n, shape, F32))
        own, act_own, fixed, turned, copied, product, biased, added, clipped, mean_up, var_up, roots_up = (
            sem(n) for n in ("own", "act_own", "fixed", "turned", "copied", "product", "biased", "added", "clipped",
                             "mean_up", "var_up", "roots_up"))
        y_up, y_turned, y_copied, y_product, m_up, factor_up, u_up, u_var_up, done, z_free = (
            sem(n) for n in ("y_up", "y_turned", "y_copied", "y_product", "m_up", "factor_up", "u_up", "u_var_up",
                             "done", "z_free"))
        y_stored, m_stored = [sem(f"y_stored{k}") for k in range(2)], sem("m_stored")
        x_in = [sem(f"x_in{n}") for n in range(G)]
        attr_zero, attr_cleared, attr_in = sem("attr_zero"), sem("attr_cleared"), sem("attr_in")
        scattered = [sem(f"sc{n}") for n in range(G)]
        full = [sb(f"full{n}", [P, G, 130]) for n in range(2)]
        flipped, y_flipped, ms = (sb(n, [P, G * D]) for n in ("flipped", "y_flipped", "m"))
        xs, v, ys, result = ([sb(f"{k}{n}", [P, G, D]) for n in range(2)] for k in ("x", "v", "y", "result"))
        pre, factor = sb("pre", [P, G, D]), sb("factor", [P, G, D])
        mean = [sb(f"mean{n}", [P, G]) for n in range(2)]
        inverse, total, sq, u_total, u_mean, u_sq, u_dev, u_inv = (
            sb(n, [P, G]) for n in ("inverse", "total", "sq", "u_total", "u_mean", "u_sq", "u_dev", "u_inv"))
        dev, inv = sb("dev", [P, 2, G]), sb("inv", [P, 2, G])
        block = ctx.enter_context(nc.Block())

        @block.vector
        def _(dve):
            fin, vec = Finished(dve, own), nc.vector
            vec.memset(B["edge_w"][:, :], 0.0)
            vec.memset(B["attr"][:, :, :], 0.0).then_inc(attr_zero, 1)
            dve.wait_ge(attr_zero, 1)
            vec.memset(B["attr"][:, :, 3], 1.0).then_inc(attr_cleared, 1)

            def body(c, pair, slot, live):
                newest, second, third, oldest = live
                other = 1 - slot
                if third:
                    dve.wait_ge(var_up, c - 1)
                if second:
                    dve.wait_ge(fixed, c)
                    fin.after(vec.reciprocal(inverse[:, :], full[other][:, :, 129]))
                    dve.wait_ge(product, c)
                    for g, o in enumerate(bank_rows(ps, 2)):
                        ins = vec.scalar_tensor_tensor(out=pre[:, g, :], in0=o, scalar=inverse[:, g:g + 1],
                                                       in1=rows_["b2"][:, :], op0=ALU.mult, op1=ALU.add)
                    ins.then_inc(biased, 1)
                    dve.wait_ge(biased, c)
                    for n in range(G):
                        dve.wait_ge(x_in[n], c * 16)
                    vec.tensor_tensor(pre[:, :, :], pre[:, :, :], xs[other][:, :, :], ALU.add).then_inc(added, 1)
                    dve.wait_ge(added, c * 2 - 1)
                    vec.tensor_tensor(v[other][:, :, :], pre[:, :, :], xs[other][:, :, :], ALU.add).then_inc(added, 1)
                if third:
                    fin.after(vec.reciprocal(inv[:, :, :], dev[:, :, :]))
                    dve.sem_inc(roots_up, 1)
                    wait(dve, y_stored[slot], (pair - 1) * 16)
                    wait(dve, y_turned, c - 2)
                    for g in range(G):
                        ins = vec.tensor_scalar(ys[slot][:, g, :], v[slot][:, g, :], mean[slot][:, g:g + 1],
                                                inv[:, 0, g:g + 1], ALU.add, ALU.mult)
                    ins.then_inc(y_up, 1)
                if newest:
                    wait(dve, turned, c - 1)
                    for g in range(G):
                        ins = fix_step(nc, B, "s", full[slot][:, g, :], c * G + g)
                    ins.then_inc(fixed, 1)
                if oldest:
                    dve.wait_ge(u_var_up, c - 2)
                    fin.after(vec.reciprocal(u_inv[:, :], u_dev[:, :]))
                    for g in range(G):
                        ins = vec.tensor_scalar(result[other][:, g, :], result[other][:, g, :], u_mean[:, g:g + 1],
                                                u_inv[:, g:g + 1], ALU.add, ALU.mult)
                    ins.then_inc(done, 1)
                if second:
                    dve.wait_ge(clipped, c)
                    dve.wait_ge(added, c * 2)
                    for g in range(G):
                        ins = vec.scalar_tensor_tensor(out=v[other][:, g, :], in0=pre[:, g, :], scalar=B["drop"][:, 0:1],
                                                       in1=v[other][:, g, :], op0=ALU.mult, op1=ALU.add,
                                                       accum_out=total[:, g:g + 1])
                    fin.after(ins)
                    vec.tensor_scalar(mean[other][:, :], total[:, :], -1.0 / D, None, ALU.mult).then_inc(mean_up, 1)
                    dve.wait_ge(mean_up, c)
                if third:
                    dve.wait_ge(factor_up, c - 1)
                    wait(dve, z_free, c - 3)
                    if oldest:
                        dve.wait_ge(done, c - 2)
                    for g in range(G):
                        ins = vec.scalar_tensor_tensor(out=result[slot][:, g, :], in0=v[slot][:, g, :],
                                                       scalar=mean[slot][:, g:g + 1], in1=factor[:, g, :],
                                                       op0=ALU.add, op1=ALU.mult, accum_out=u_total[:, g:g + 1])
                    fin.after(ins)
                    vec.tensor_tensor(result[slot][:, :, :], result[slot][:, :, :], wide(rows_["beta"][:, :], G), ALU.add)
                    vec.tensor_scalar(u_mean[:, :], u_total[:, :], -1.0 / D, B["beta_mean"][:, 0:1], ALU.mult,
                                      ALU.subtract).then_inc(u_up, 1)
            turns(dve, C, 3, body, [(fin, 5)])

        @block.tensor
        def _(pe):
            def body(c, pair, slot, live):
                newest, second, third, oldest = live
                if third:
                    pe.wait_ge(y_up, c - 1)
                    wait(pe, y_copied, c - 2)
                    for g, o in enumerate(bank_rows(ps, 4)):
                        ins = nc.tensor.transpose(o, ys[slot][:, g, :], B["ident"][:, :])
                    ins.then_inc(y_turned, 1)
                if newest:
                    pe.wait_ge(fixed, c + 1)
                    wait(pe, copied, c)
                    for g, o in enumerate(bank_rows(ps, 0)):
                        ins = nc.tensor.transpose(o, full[slot][:, g, 0:D], B["ident"][:, :])
                    ins.then_inc(turned, 1)
                    pe.wait_ge(copied, c + 1)
                    wait(pe, biased, c)
                    for g, o in enumerate(bank_rows(ps, 2)):
                        ins = nc.tensor.matmul(o, flipped[:, g * D:g * D + D], B["w2s"][:, :], start=True, stop=True)
                    ins.then_inc(product, 1)
                if third:
                    pe.wait_ge(y_copied, c - 1)
                    wait(pe, m_up, c - 2)
                    for g, o in enumerate(bank_rows(ps, 6)):
                        ins = nc.tensor.matmul(o, y_flipped[:, g * D:g * D + D], B["m1s"][:, :], start=True, stop=True)
                    ins.then_inc(y_product, 1)
            turns(pe, C, 3, body)

        def copy_flipped(dest, first, sem_up):
            nc.scalar.activation(dest[:, 0:4 * D], ps[first][:, 0:4 * D], ACT.Copy)
            nc.scalar.activation(dest[:, 4 * D:G * D], ps[first + 1][:, 0:3 * D], ACT.Copy).then_inc(sem_up, 1)

        @block.scalar
        def _(act):
            fin = Finished(act, act_own)

            def body(c, pair, slot, live):
                newest, second, third, oldest = live
                if second:
                    act.wait_ge(added, c * 2)
                    nc.scalar.activation(pre[:, :, :], pre[:, :, :], ACT.Relu, scale=-1.0).then_inc(clipped, 1)
                if third:
                    act.wait_ge(roots_up, c - 1)
                    for g in range(G):
                        ins = nc.scalar.activation(factor[:, g, :], rows_["gamma"][:, :], ACT.Identity,
                                                   bias=inv[:, 0, g:g + 1], scale=inv[:, 1, g:g + 1])
                    ins.then_inc(factor_up, 1)
                    act.wait_ge(y_turned, c - 1)
                    wait(act, y_product, c - 2)
                    copy_flipped(y_flipped, 4, y_copied)
                if newest:
                    act.wait_ge(turned, c + 1)
                    wait(act, product, c)
                    copy_flipped(flipped, 0, copied)
                if second:
                    act.wait_ge(mean_up, c)
                    squares(nc, fin, v[1 - slot], mean[1 - slot], [pre[:, g, :] for g in range(G)], sq)
                    nc.scalar.activation(dev[:, 0, :], sq[:, :], ACT.Sqrt, bias=B["eps"][:, 0:1], scale=1.0 / D)
                    nc.scalar.activation(dev[:, 1, :], sq[:, :], ACT.Sqrt, bias=B["eps_sq"][:, 0:1],
                                         scale=(1.0 + EPS) / D).then_inc(var_up, 1)
                if third:
                    act.wait_ge(u_up, c - 1)
                    squares(nc, fin, result[slot], u_mean, [factor[:, g, :] for g in range(G)], u_sq)
                    nc.scalar.activation(u_dev[:, :], u_sq[:, :], ACT.Sqrt, bias=B["eps"][:, 0:1], scale=1.0 / D)\
                        .then_inc(u_var_up, 1)
                    act.wait_ge(y_product, c - 1)
                    wait(act, m_stored, (c - 2) * 16)
                    copy_flipped(ms, 6, m_up)
            turns(act, C, 3, body, [(fin, 2)])

        @block.sync
        def _(sp):
            sp.wait_ge(attr_cleared, 1)
            sp.dma_start(B["attr"][0:LAST, :, 0:3], B["edge_attr"][0:LAST * T, :].rearrange("(p t) k -> p t k", t=T))\
              .then_inc(attr_in, 16)
            sp.dma_start(B["attr"][LAST:P, 0:LEFT, 0:3], B["edge_attr"][LAST * T:E, :].rearrange("(p t) k -> p t k", p=1))\
              .then_inc(attr_in, 16)
            for g in range(G):
                sp.dma_start(B["edge_w"][4 * g:4 * g + 3, g * D:g * D + D], B["m1"][D:D + 3, :]).then_inc(attr_in, 16)
                sp.dma_start(B["edge_w"][4 * g + 3:4 * g + 4, g * D:g * D + D], B["mb1"].rearrange("(a n) -> a n", a=1))\
                  .then_inc(attr_in, 16)
            def at(table, c):
                return table.rearrange("(p t) d -> p t d", t=T)[:, bass.ds(c * G, G), :]

            def body(c, slot, last):
                sp.wait_ge(y_up, c + 1)
                sp.dma_start(at(B["mixed"][0:EP, :], c), ys[slot][:, :, :]).then_inc(y_stored[slot], 16)
                sp.wait_ge(m_up, c + 1)
                sp.dma_start(at(B["mixed_m"][0:EP, :], c), ms[:, :].rearrange("p (g d) -> p g d", d=D)).then_inc(m_stored, 16)
            over_chunks(sp, body)
            sp.wait_ge(attr_in, 16 * (2 + 2 * G))
            for n in range(2):
                sp.wait_ge(y_stored[n], 16 * (C // 2))
            sp.wait_ge(m_stored, 16 * C)

        @block.gpsimd
        def _(gp):
            def gather(c):
                for g in range(G):
                    wait(gp, x_in[g], 16 * c)
                    t = c * G + g
                    gp.indirect_dma_start(out=xs[c % 2][:, g, :], out_offset=None, in_=B["x"],
                                          in_offset=bass.IndirectOffsetOnAxis(ap=B["s_gather"][:, t:t + 1], axis=0))\
                      .then_inc(x_in[g], 16)
            for c in range(C + 3):
                if c < C:
                    wait(gp, added, 2 * c - 2)
                    gather(c)
                if c >= 4:
                    scattered_chunk(gp, scattered, z_free, c - 4)
                if c >= 3:
                    scatter_chunk(gp, B, "s_scatter", result, done, scattered, c - 3)
            scattered_chunk(gp, scattered, z_free, C - 1)


def scatter_chunk(gp, B, name, result, done, scattered, c):
    gp.wait_ge(done, c + 1)
    for g in range(G):
        t = c * G + g
        gp.indirect_dma_start(out=B["out"], out_offset=bass.IndirectOffsetOnAxis(ap=B[name][:, t:t + 1], axis=0),
                              in_=result[c % 2][:, g, :], in_offset=None, bounds_check=N - 1, oob_is_err=False)\
          .then_inc(scattered[g], 16)


def scattered_chunk(gp, scattered, free, c):
    for g in range(G):
        gp.wait_ge(scattered[g], 16 * (c + 1))
    gp.sem_inc(free, 1)


def edge_network(nc, B):
    ps, rows_, big = B["ps"], B["rows_"], B["big"]
    with phase(nc) as ctx:
        def sem(n):
            return semaphore(nc, ctx, "u_" + n)

        def sb(n, shape):
            return ctx.enter_context(nc.sbuf_tensor("u_" + n, shape, F32))
        own, act_own, cleared, sliced, turned, copied, product, summed = (
            sem(n) for n in ("own", "act_own", "cleared", "sliced", "turned", "copied", "product", "summed"))
        big_in = [sem(f"big{n}") for n in range(G)]
        attr = B["attr"]
        piece = [sb(f"piece{n}", [P, 4 * G]) for n in range(2)]
        below_up, clipped, mean_up, var_up, y_up, x_free = (
            sem(n) for n in ("below_up", "clipped", "mean_up", "var_up", "y_up", "x_free"))
        x_in, y_stored = ([sem(f"{k}{n}") for n in range(2)] for k in ("x_in", "y_stored"))
        xs, ys = ([sb(f"{k}{n}", [P, G, D]) for n in range(2)] for k in ("x", "y"))
        below = sb("below", [P, G, D])
        mean, total, sq, dev, inv = (sb(n, [P, G]) for n in ("mean", "total", "sq", "dev", "inv"))
        flipped = [sb(f"flipped{n}", [4 * G, P]) for n in range(2)]
        block = ctx.enter_context(nc.Block())

        @block.gpsimd
        def _(gp):
            gp.wait_ge(cleared, 1)
            for t in range(T):
                if t >= G:
                    gp.wait_ge(big_in[t % G], 16 * (t // G))
                gp.indirect_dma_start(out=big[:, t, 0:D], out_offset=None, in_=B["mixed_m"],
                                      in_offset=bass.IndirectOffsetOnAxis(ap=B["src_start_i"][:, t:t + 1], axis=0))\
                  .then_inc(big_in[t % G], 16)

        @block.sync
        def _(sp):
            table = B["x_dst"].rearrange("(p t) d -> p t d", t=T)

            def rows_of(c, pair, slot, live):
                new, _, old = live
                if new:
                    wait(sp, x_free, c - 1)
                    sp.dma_start(xs[slot][:, :, :], table[:, bass.ds(c * G, G), :]).then_inc(x_in[slot], 16)
                if old:
                    sp.wait_ge(y_up, c - 1)
                    sp.dma_start(table[:, bass.ds(c * G - 2 * G, G), :], ys[slot][:, :, :]).then_inc(y_stored[slot], 16)
            turns(sp, C, 2, rows_of)
            for n in range(2):
                sp.wait_ge(y_stored[n], 16 * (C // 2))

        @block.vector
        def _(dve):
            fin = Finished(dve, own)
            dve.sem_inc(turned, 1)
            nc.vector.memset(big[:, 0:T, 129], 1.0).then_inc(cleared, 1)
            nc.vector.tensor_copy(piece[0][:, :], attr[:, 0:G, :].rearrange("p g k -> p (g k)")).then_inc(sliced, 1)
            dve.wait_ge(sliced, 1)

            def result_row(c, slot):
                dve.wait_ge(var_up, c + 1)
                fin.after(nc.vector.reciprocal(inv[:, :], dev[:, :]))
                for g in range(G):
                    ins = nc.vector.tensor_scalar(ys[slot][:, g, :], ys[slot][:, g, :], mean[:, g:g + 1], inv[:, g:g + 1],
                                                  ALU.add, ALU.mult)
                ins.then_inc(y_up, 1)
                dve.wait_ge(y_up, c + 1)

            def body(c, pair, slot, live):
                new, old = live
                if new:
                    if not (isinstance(c, int) and c == 0):
                        dve.wait_ge(turned, c)
                        nc.vector.tensor_copy(piece[slot][:, :].rearrange("p (g k) -> p g k", k=4),
                                              attr[:, bass.ds(c * G, G), :]).then_inc(sliced, 1)
                    wait(dve, y_stored[slot], pair * 16)
                    dve.wait_ge(x_in[slot], pair * 16 + 16)
                    nc.vector.tensor_tensor(below[:, :, :], xs[slot][:, :, :], wide(rows_["b2"][:, :], G), ALU.add)\
                      .then_inc(below_up, 1)
                    nc.vector.scalar_tensor_tensor(out=ys[slot][:, :, :], in0=xs[slot][:, :, :], scalar=2.0,
                                                   in1=wide(rows_["b2"][:, :], G), op0=ALU.mult, op1=ALU.add).then_inc(x_free, 1)
                if old:
                    result_row(c - 1, 1 - slot)
                if new:
                    dve.wait_ge(clipped, c + 1)
                    dve.wait_ge(x_free, c + 1)
                    for g in range(G):
                        ins = nc.vector.scalar_tensor_tensor(out=ys[slot][:, g, :], in0=below[:, g, :],
                                                             scalar=B["drop"][:, 0:1], in1=ys[slot][:, g, :],
                                                             op0=ALU.mult, op1=ALU.add, accum_out=total[:, g:g + 1])
                    fin.after(ins)
                    nc.vector.tensor_scalar(mean[:, :], total[:, :], -1.0 / D, None, ALU.mult).then_inc(mean_up, 1)
                    dve.wait_ge(mean_up, c + 1)
                    dve.wait_ge(product, c + 1)
                    for n in range(G):
                        dve.wait_ge(big_in[n], c * 16 + 16)
                    for first, n in ((0, 4), (4, 3)):
                        rows = big[:, bass.ds(c * G + first, n), 0:D]
                        ins = nc.vector.tensor_tensor(
                            rows, ps[2 + 2 * slot + first // 4][:, 0:n * D].rearrange("p (g d) -> p g d", d=D), rows, ALU.add)
                    ins.then_inc(summed, 1)
            turns(dve, C, 1, body, [(fin, 2)])

        @block.tensor
        def _(pe):
            def body(c, slot, last):
                pe.wait_ge(sliced, c + 1)
                nc.tensor.transpose(ps[slot][0:4 * G, 0:P], piece[slot][:, :], B["ident"][:, :]).then_inc(turned, 1)
                pe.wait_ge(copied, c + 1)
                for n, wd in ((0, 4 * D), (1, 3 * D)):
                    ins = nc.tensor.matmul(ps[2 + 2 * slot + n][:, 0:wd], flipped[slot][:, :],
                                           B["edge_w"][:, n * 4 * D:n * 4 * D + wd], start=True, stop=True)
                ins.then_inc(product, 1)
            over_chunks(pe, body)

        @block.scalar
        def _(act):
            fin = Finished(act, act_own)

            def body(c, pair, slot, live):
                new, last = live
                if new:
                    act.wait_ge(turned, c + 2)
                    nc.scalar.activation(flipped[slot][:, :], ps[slot][0:4 * G, 0:P], ACT.Copy).then_inc(copied, 1)
                    act.wait_ge(below_up, c + 1)
                    nc.scalar.activation(below[:, :, :], below[:, :, :], ACT.Relu, scale=-1.0).then_inc(clipped, 1)
                if last:
                    act.wait_ge(summed, c)
                    act.wait_ge(cleared, 1)
                    rows = big[:, bass.ds(c * G - G, G), 0:D]
                    nc.scalar.activation(rows, rows, ACT.Gelu)
                if new:
                    act.wait_ge(mean_up, c + 1)
                    act.wait_ge(cleared, 1)
                    squares(nc, fin, ys[slot], mean, bank_rows(ps, 6), sq)
                    nc.scalar.activation(dev[:, :], sq[:, :], ACT.Sqrt, bias=B["eps"][:, 0:1], scale=1.0 / D).then_inc(var_up, 1)
            turns(act, C, 1, body, [(fin, 1)])

    running_sums(nc, B, "d", None, "su_")
    with phase(nc) as ctx:
        def sem(n):
            return semaphore(nc, ctx, "v_" + n)

        def sb(n, shape):
            return ctx.enter_context(nc.sbuf_tensor("v_" + n, shape, F32))
        own, act_own, fixed, turned, copied, product, counted, mean_up, var_up, roots_up, factor_up, u_up, u_var_up = (
            sem(n) for n in ("own", "act_own", "fixed", "turned", "copied", "product", "counted", "mean_up", "var_up",
                             "roots_up", "factor_up", "u_up", "u_var_up"))
        done, y_free, z_free, alone_in, alone_free = (
            sem(n) for n in ("done", "y_free", "z_free", "alone_in", "alone_free"))
        y_in = [sem(f"y_in{n}") for n in range(G)]
        scattered = [sem(f"sc{n}") for n in range(G)]
        full = [sb(f"full{n}", [P, G, 130]) for n in range(2)]
        flipped, alone = sb("flipped", [P, G * D]), sb("alone", [P, G, D])
        ys, y_beta, z, result = ([sb(f"{k}{n}", [P, G, D]) for n in range(2)] for k in ("y", "y_beta", "z", "result"))
        mean = [sb(f"mean{n}", [P, G]) for n in range(2)]
        total, sq, dev, inv, u_total, u_mean, u_sq, u_dev, u_inv = (
            sb(n, [P, G]) for n in ("total", "sq", "dev", "inv", "u_total", "u_mean", "u_sq", "u_dev", "u_inv"))
        factor, unused = bank_rows(ps, 4), bank_rows(ps, 6)
        block = ctx.enter_context(nc.Block())

        @block.vector
        def _(dve):
            fin, vec = Finished(dve, own), nc.vector
            fin.after(vec.tensor_scalar(B["absent"][:, :], B["dst_start"][:, :], float(ABSENT), None, ALU.is_equal))

            def body(c, pair, slot, live):
                newest, second, third, oldest = live
                other = 1 - slot
                if third:
                    dve.wait_ge(var_up, c - 1)
                    vec.reciprocal(inv[:, :], dev[:, :]).then_inc(roots_up, 1)
                if second:
                    dve.wait_ge(fixed, c)
                    dve.wait_ge(product, c)
                    for g, o in enumerate(bank_rows(ps, 2)):
                        ins = vec.scalar_tensor_tensor(out=z[other][:, g, :], in0=rows_["mb2"][:, :],
                                                       scalar=full[other][:, g, 129:130], in1=o, op0=ALU.mult, op1=ALU.add)
                    ins.then_inc(counted, 1)
                    dve.wait_ge(alone_in, c * 16)
                    for n in range(G):
                        dve.wait_ge(y_in[n], c * 16)
                    for g in range(G):
                        ins = vec.scalar_tensor_tensor(out=ys[other][:, g, :], in0=alone[:, g, :],
                                                       scalar=B["absent"][:, bass.ds(c * G + (g - G), 1)],
                                                       in1=ys[other][:, g, :], op0=ALU.mult, op1=ALU.add)
                    fin.after(ins)
                    dve.sem_inc(alone_free, 1)
                    vec.tensor_tensor(y_beta[other][:, :, :], ys[other][:, :, :], wide(rows_["beta"][:, :], G), ALU.add)
                    for g in range(G):
                        ins = vec.scalar_tensor_tensor(out=z[other][:, g, :], in0=z[other][:, g, :], scalar=1.0,
                                                       in1=ys[other][:, g, :], op0=ALU.mult, op1=ALU.add,
                                                       accum_out=total[:, g:g + 1])
                    fin.after(ins)
                    dve.sem_inc(y_free, 1)
                    vec.tensor_scalar(mean[other][:, :], total[:, :], -1.0 / D, None, ALU.mult).then_inc(mean_up, 1)
                    dve.wait_ge(mean_up, c)
                if newest:
                    wait(dve, turned, c - 1)
                    for g in range(G):
                        ins = fix_step(nc, B, "d", full[slot][:, g, :], c * G + g)
                    ins.then_inc(fixed, 1)
                if oldest:
                    dve.wait_ge(u_var_up, c - 2)
                    fin.after(vec.reciprocal(u_inv[:, :], u_dev[:, :]))
                    for g in range(G):
                        ins = vec.tensor_scalar(result[other][:, g, :], result[other][:, g, :], u_mean[:, g:g + 1],
                                                u_inv[:, g:g + 1], ALU.add, ALU.mult)
                    ins.then_inc(done, 1)
                if third:
                    dve.wait_ge(factor_up, c - 1)
                    wait(dve, z_free, c - 3)
                    for g in range(G):
                        ins = vec.scalar_tensor_tensor(out=result[slot][:, g, :], in0=z[slot][:, g, :],
                                                       scalar=mean[slot][:, g:g + 1], in1=factor[g],
                                                       op0=ALU.add, op1=ALU.mult)
                    fin.after(ins)
                    for g in range(G):
                        ins = vec.scalar_tensor_tensor(out=result[slot][:, g, :], in0=result[slot][:, g, :], scalar=1.0,
                                                       in1=y_beta[slot][:, g, :], op0=ALU.mult, op1=ALU.add,
                                                       accum_out=u_total[:, g:g + 1])
                    fin.after(ins)
                    if oldest:
                        dve.wait_ge(done, c - 2)
                    vec.tensor_scalar(u_mean[:, :], u_total[:, :], -1.0 / D, None, ALU.mult).then_inc(u_up, 1)
            turns(dve, C, 3, body, [(fin, 5)])

        @block.tensor
        def _(pe):
            def body(c, slot, last):
                pe.wait_ge(fixed, c + 1)
                for g, o in enumerate(bank_rows(ps, 0)):
                    ins = nc.tensor.transpose(o, full[slot][:, g, 0:D], B["ident"][:, :])
                ins.then_inc(turned, 1)
                pe.wait_ge(copied, c + 1)
                pe.wait_ge(counted, c)
                for g, o in enumerate(bank_rows(ps, 2)):
                    ins = nc.tensor.matmul(o, flipped[:, g * D:g * D + D], B["m2s"][:, :], start=True, stop=True)
                ins.then_inc(product, 1)
            over_chunks(pe, body)

        @block.scalar
        def _(act):
            fin = Finished(act, act_own)

            def body(c, pair, slot, live):
                newest, second, third, oldest = live
                if third:
                    act.wait_ge(roots_up, c - 1)
                    for g in range(G):
                        ins = nc.scalar.activation(factor[g], rows_["gamma"][:, :], ACT.Copy, scale=inv[:, g:g + 1])
                    ins.then_inc(factor_up, 1)
                if second:
                    act.wait_ge(mean_up, c)
                    squares(nc, fin, z[1 - slot], mean[1 - slot], unused, sq)
                    nc.scalar.activation(dev[:, :], sq[:, :], ACT.Sqrt, bias=B["eps"][:, 0:1], scale=1.0 / D)\
                        .then_inc(var_up, 1)
                if newest:
                    act.wait_ge(turned, c + 1)
                    wait(act, product, c)
                    nc.scalar.activation(flipped[:, 0:4 * D], ps[0][:, 0:4 * D], ACT.Copy)
                    nc.scalar.activation(flipped[:, 4 * D:G * D], ps[1][:, 0:3 * D], ACT.Copy).then_inc(copied, 1)
                if third:
                    act.wait_ge(u_up, c - 1)
                    squares(nc, fin, result[slot], u_mean, unused, u_sq)
                    nc.scalar.activation(u_dev[:, :], u_sq[:, :], ACT.Sqrt, bias=B["eps"][:, 0:1], scale=1.0 / D)\
                        .then_inc(u_var_up, 1)
            turns(act, C, 3, body, [(fin, 2)])

        @block.sync
        def _(sp):
            table = B["x_dst"].rearrange("(p t) d -> p t d", t=T)

            def load(c):
                sp.dma_start(alone[:, :, :], table[:, bass.ds(c * G, G), :]).then_inc(alone_in, 16)
            load(0)
            with sp.Fori(0, C - 1, 1) as i:
                sp.wait_ge(alone_free, i + 1)
                load(i + 1)

        @block.gpsimd
        def _(gp):
            def gather(c):
                for g in range(G):
                    wait(gp, y_in[g], 16 * c)
                    t = c * G + g
                    gp.indirect_dma_start(out=ys[c % 2][:, g, :], out_offset=None, in_=B["mixed"],
                                          in_offset=bass.IndirectOffsetOnAxis(ap=B["dst_start_i"][:, t:t + 1], axis=0))\
                      .then_inc(y_in[g], 16)
            for c in range(C + 3):
                if c < C:
                    wait(gp, y_free, c - 1)
                    gather(c)
                if c >= 4:
                    scattered_chunk(gp, scattered, z_free, c - 4)
                if c >= 3:
                    scatter_chunk(gp, B, "d_scatter", result, done, scattered, c - 3)
            scattered_chunk(gp, scattered, z_free, C - 1)


_INS = ['x', 'src', 'dst', 'edge_attr_3', 'L0_gnn_W1', 'L0_gnn_att1', 'L0_gnn_b1', 'L0_gnn_W2', 'L0_gnn_att2',
        'L0_gnn_b2', 'L0_gnn_prelu_a', 'L1_gnn_W1', 'L1_gnn_b1', 'L1_gnn_W2', 'L1_gnn_b2', 'L1_gnn_gamma', 'L1_gnn_beta']


def kernel(**inputs):
    import numpy as _np
    import concourse.bacc as _bacc
    from concourse import mybir as _mybir
    from concourse.bass_utils import run_bass_kernel_spmd as _run

    nc = _bacc.Bacc("TRN2", target_bir_lowering=False, num_devices=1)
    arrays, args = {}, []
    for name in _INS:
        a = _np.ascontiguousarray(inputs[name])
        if a.ndim == 0:
            a = a.reshape(1)
        arrays[f"in_{name}"] = a
        args.append(nc.dram_tensor(f"in_{name}", a.shape, _mybir.dt.from_np(a.dtype), kind="ExternalInput").ap())
    out = nc.dram_tensor("out_rows", (N, D), _mybir.dt.float32, kind="ExternalOutput").ap()
    program(nc, *args, out)
    r = _run(nc, [arrays], core_ids=[0])
    return r.results[0]["out_rows"]
```
